# Optimizing a Trainium2 kernel written in Bass

```python
import numpy as np
import jax
import jax.numpy as jnp

def _softmax(x, axis=-1):
    return jax.nn.softmax(x, axis=axis)

def _gelu(x):
    return jax.nn.gelu(x, approximate=True)

def _silu(x):
    return jax.nn.silu(x)

def _sigmoid(x):
    return jax.nn.sigmoid(x)

def _layernorm(x, axis=-1, eps=1e-05):
    m = jnp.mean(x, axis=axis, keepdims=True)
    v = jnp.var(x, axis=axis, keepdims=True)
    return (x - m) / jnp.sqrt(v + eps)

def _scatter_add(tgt, idx, src, axis=0):
    return tgt.at[idx].add(src)

def _segment_sum(src, seg, n):
    return jax.ops.segment_sum(src, seg, n)
kernel_name = 'mk_gnn_resnorm_d4_gnn_r32_0c920b'

def setup_inputs(seed: int=0):
    np.random.seed(seed)
    _w = jnp.asarray

    def _rec_inputs():
        import jax
        import jax.numpy as jnp
        _gk = jax.random.key(seed)
        x = -0.0003713 + 1 * jax.random.normal(jax.random.fold_in(_gk, 1), (50000, 128), jnp.float32)
        src = jax.random.randint(jax.random.fold_in(_gk, 2), (25000,), 0, 50000, jnp.int32)
        dst = jnp.minimum((50000 * jax.random.uniform(jax.random.fold_in(_gk, 3), (25000,)) ** 2.0).astype(jnp.int32), 49999)
        _o = jnp.argsort(dst, stable=True)
        src = src[_o]
        dst = dst[_o]
        edge_type_8 = jax.random.randint(jax.random.fold_in(_gk, 13), (25000,), 0, 8, jnp.int32)
        edge_weight = jax.random.uniform(jax.random.fold_in(_gk, 14), (25000,), jnp.float32, 0.0, 0.999999)
        return (x, src, dst, edge_type_8, edge_weight)
    x, src, dst, edge_type_8, edge_weight = _rec_inputs()

    def _L0_gnn_setup():
        import jax, jax.numpy as jnp
        import numpy as np
        N = 3125
        C = 128
        E = 50000

        def _gru_step(x, h, w_ih, w_hh, b_ih, b_hh):
            gi = x @ w_ih.T + b_ih
            gh = h @ w_hh.T + b_hh
            i_r, i_z, i_n = jnp.split(gi, 3, axis=-1)
            h_r, h_z, h_n = jnp.split(gh, 3, axis=-1)
            r = jax.nn.sigmoid(i_r + h_r)
            z = jax.nn.sigmoid(i_z + h_z)
            n = jnp.tanh(i_n + r * h_n)
            return (1.0 - z) * n + z * h
        key = jax.random.key(seed)
        ks = jax.random.split(key, 9)
        s = 1.0 / np.sqrt(C)
        return {'X': jax.random.normal(ks[0], (N, C), jnp.float32), 'edge_index': jax.random.randint(ks[1], (2, E), 0, N, jnp.int64), 'edge_weight': jax.random.uniform(ks[2], (E,), jnp.float32), 'p': jax.random.normal(ks[3], (C,), jnp.float32), 'w_ih': jax.random.uniform(ks[4], (3 * C, C), jnp.float32, -s, s), 'w_hh': jax.random.uniform(ks[5], (3 * C, C), jnp.float32, -s, s), 'b_ih': jax.random.uniform(ks[6], (3 * C,), jnp.float32, -s, s), 'b_hh': jax.random.uniform(ks[7], (3 * C,), jnp.float32, -s, s), 'W0': jax.random.normal(ks[8], (C, C), jnp.float32) * s}
    _L0_gnn_all = _L0_gnn_setup()
    _L0_gnn_in = {k: v for k, v in _L0_gnn_all.items() if k in ('p', 'w_ih', 'w_hh', 'b_ih', 'b_hh', 'W0')}
    del _L0_gnn_all

    def _L1_gnn_setup():
        import jax, jax.numpy as jnp
        import numpy as np
        N, E, F = (50000, 25000, 128)
        DELTA = 1.0
        EPS = 1e-05

        def _pna_forward(x, edge_index, W_pre, b_pre, W_post, b_post, W_lin, b_lin):
            src, dst = (edge_index[0], edge_index[1])
            n = x.shape[0]
            h = jnp.concatenate([x[dst], x[src]], axis=-1)
            m = h @ W_pre.T + b_pre
            deg = jax.ops.segment_sum(jnp.ones((m.shape[0],), m.dtype), dst, num_segments=n)
            deg_c = jnp.maximum(deg, 1.0)[:, None]
            has_edge = (deg > 0)[:, None]
            mx = jax.ops.segment_max(m, dst, num_segments=n)
            mx = jnp.where(has_edge, mx, 0.0)
            mn = jax.ops.segment_min(m, dst, num_segments=n)
            mn = jnp.where(has_edge, mn, 0.0)
            s1 = jax.ops.segment_sum(m, dst, num_segments=n)
            s2 = jax.ops.segment_sum(m * m, dst, num_segments=n)
            mean = s1 / deg_c
            var = s2 / deg_c - mean * mean
            std = jnp.sqrt(jax.nn.relu(var) + EPS)
            agg = jnp.concatenate([mx, mn, mean, std], axis=-1)
            log_deg = jnp.log(deg_c + 1.0)
            amp = log_deg / DELTA
            att = DELTA / log_deg
            scaled = jnp.concatenate([agg, agg * amp, agg * att], axis=-1)
            out = jnp.concatenate([x, scaled], axis=-1) @ W_post.T + b_post
            return out @ W_lin.T + b_lin
        key = jax.random.key(seed)
        ks = jax.random.split(key, 6)
        x = jax.random.normal(ks[0], (N, F), dtype=jnp.float32)
        edge_index = jax.random.randint(ks[1], (2, E), 0, N, dtype=jnp.int32)
        W_pre = jax.random.normal(ks[2], (F, 2 * F), dtype=jnp.float32) * (2 * F) ** (-0.5)
        b_pre = jnp.zeros((F,), jnp.float32)
        W_post = jax.random.normal(ks[3], (F, 13 * F), dtype=jnp.float32) * (13 * F) ** (-0.5)
        b_post = jnp.zeros((F,), jnp.float32)
        W_lin = jax.random.normal(ks[4], (F, F), dtype=jnp.float32) * F ** (-0.5)
        b_lin = jnp.zeros((F,), jnp.float32)
        return {'x': x, 'edge_index': edge_index, 'W_pre': W_pre, 'b_pre': b_pre, 'W_post': W_post, 'b_post': b_post, 'W_lin': W_lin, 'b_lin': b_lin}
    _L1_gnn_all = _L1_gnn_setup()
    _L1_gnn_in = {k: v for k, v in _L1_gnn_all.items() if k in ('W_pre', 'b_pre', 'W_post', 'b_post', 'W_lin', 'b_lin')}
    del _L1_gnn_all

    def _L2_gnn_setup():
        import jax, jax.numpy as jnp
        import numpy as np
        N = 3125
        E = 50000
        D = 128
        H = 8
        HD = D // H
        T = 8

        def _layernorm(x, g, b, eps=1e-05):
            m = jnp.mean(x, axis=-1, keepdims=True)
            v = jnp.mean((x - m) ** 2, axis=-1, keepdims=True)
            return (x - m) * jax.lax.rsqrt(v + eps) * g + b
        key = jax.random.key(seed)
        ks = jax.random.split(key, 16)
        s = 0.02
        inp = {'x': jax.random.normal(ks[0], (N, D), jnp.float32), 'edge_index': jax.random.randint(ks[1], (2, E), 0, N, jnp.int32), 'edge_type': jax.random.randint(ks[2], (E,), 0, T, jnp.int32), 'Wq': jax.random.normal(ks[3], (D, D), jnp.float32) * s, 'bq': jnp.zeros((D,), jnp.float32), 'Wk': jax.random.normal(ks[4], (D, D), jnp.float32) * s, 'bk': jnp.zeros((D,), jnp.float32), 'Wv': jax.random.normal(ks[5], (D, D), jnp.float32) * s, 'bv': jnp.zeros((D,), jnp.float32), 'Wo': jax.random.normal(ks[6], (D, D), jnp.float32) * s, 'bo': jnp.zeros((D,), jnp.float32), 'edge_bias': jax.random.normal(ks[7], (T, H), jnp.float32) * s, 'W1': jax.random.normal(ks[8], (D, D), jnp.float32) * s, 'b1': jnp.zeros((D,), jnp.float32), 'W2': jax.random.normal(ks[9], (D, D), jnp.float32) * s, 'b2': jnp.zeros((D,), jnp.float32), 'g1': jnp.ones((D,), jnp.float32), 'be1': jnp.zeros((D,), jnp.float32), 'g2': jnp.ones((D,), jnp.float32), 'be2': jnp.zeros((D,), jnp.float32)}
        return inp
    _L2_gnn_all = _L2_gnn_setup()
    _L2_gnn_in = {k: v for k, v in _L2_gnn_all.items() if k in ('Wq', 'bq', 'Wk', 'bk', 'Wv', 'bv', 'Wo', 'bo', 'edge_bias', 'W1', 'b1', 'W2', 'b2', 'g1', 'be1', 'g2', 'be2')}
    del _L2_gnn_all

    def _L3_gnn_setup():
        import jax, jax.numpy as jnp
        import numpy as np
        N_NODES = 50000
        N_EDGES = 25000
        HID = 128
        key = jax.random.key(seed)
        ks = jax.random.split(key, 10)
        s_msg = 1.0 / np.sqrt(2 * HID + 1)
        s_u1 = 1.0 / np.sqrt(2 * HID)
        s_u2 = 1.0 / np.sqrt(HID)
        return {'z': jax.random.normal(ks[0], (N_NODES, HID), dtype=jnp.float32), 'edge_weight': jax.random.uniform(ks[1], (N_EDGES,), dtype=jnp.float32), 'edge_src': jax.random.randint(ks[2], (N_EDGES,), 0, N_NODES), 'edge_dst': jax.random.randint(ks[3], (N_EDGES,), 0, N_NODES), 'Wm': jax.random.normal(ks[4], (2 * HID + 1, HID), dtype=jnp.float32) * s_msg, 'bm': jax.random.normal(ks[5], (HID,), dtype=jnp.float32) * s_msg, 'W1': jax.random.normal(ks[6], (2 * HID, HID), dtype=jnp.float32) * s_u1, 'b1': jax.random.normal(ks[7], (HID,), dtype=jnp.float32) * s_u1, 'W2': jax.random.normal(ks[8], (HID, HID), dtype=jnp.float32) * s_u2, 'b2': jax.random.normal(ks[9], (HID,), dtype=jnp.float32) * s_u2}
    _L3_gnn_all = _L3_gnn_setup()
    _L3_gnn_in = {k: v for k, v in _L3_gnn_all.items() if k in ('Wm', 'bm', 'W1', 'b1', 'W2', 'b2')}
    del _L3_gnn_all
    return {'x': x, 'src': src, 'dst': dst, 'edge_type_8': edge_type_8, 'edge_weight': edge_weight, 'L0_gnn_p': _L0_gnn_in['p'], 'L0_gnn_w_ih': _L0_gnn_in['w_ih'], 'L0_gnn_w_hh': _L0_gnn_in['w_hh'], 'L0_gnn_b_ih': _L0_gnn_in['b_ih'], 'L0_gnn_b_hh': _L0_gnn_in['b_hh'], 'L0_gnn_W0': _L0_gnn_in['W0'], 'L1_gnn_W_pre': _L1_gnn_in['W_pre'], 'L1_gnn_b_pre': _L1_gnn_in['b_pre'], 'L1_gnn_W_post': _L1_gnn_in['W_post'], 'L1_gnn_b_post': _L1_gnn_in['b_post'], 'L1_gnn_W_lin': _L1_gnn_in['W_lin'], 'L1_gnn_b_lin': _L1_gnn_in['b_lin'], 'L2_gnn_Wq': _L2_gnn_in['Wq'], 'L2_gnn_bq': _L2_gnn_in['bq'], 'L2_gnn_Wk': _L2_gnn_in['Wk'], 'L2_gnn_bk': _L2_gnn_in['bk'], 'L2_gnn_Wv': _L2_gnn_in['Wv'], 'L2_gnn_bv': _L2_gnn_in['bv'], 'L2_gnn_Wo': _L2_gnn_in['Wo'], 'L2_gnn_bo': _L2_gnn_in['bo'], 'L2_gnn_edge_bias': _L2_gnn_in['edge_bias'], 'L2_gnn_W1': _L2_gnn_in['W1'], 'L2_gnn_b1': _L2_gnn_in['b1'], 'L2_gnn_W2': _L2_gnn_in['W2'], 'L2_gnn_b2': _L2_gnn_in['b2'], 'L2_gnn_g1': _L2_gnn_in['g1'], 'L2_gnn_be1': _L2_gnn_in['be1'], 'L2_gnn_g2': _L2_gnn_in['g2'], 'L2_gnn_be2': _L2_gnn_in['be2'], 'L3_gnn_Wm': _L3_gnn_in['Wm'], 'L3_gnn_bm': _L3_gnn_in['bm'], 'L3_gnn_W1': _L3_gnn_in['W1'], 'L3_gnn_b1': _L3_gnn_in['b1'], 'L3_gnn_W2': _L3_gnn_in['W2'], 'L3_gnn_b2': _L3_gnn_in['b2']}

def reference(x, src, dst, edge_type_8, edge_weight, L0_gnn_p, L0_gnn_w_ih, L0_gnn_w_hh, L0_gnn_b_ih, L0_gnn_b_hh, L0_gnn_W0, L1_gnn_W_pre, L1_gnn_b_pre, L1_gnn_W_post, L1_gnn_b_post, L1_gnn_W_lin, L1_gnn_b_lin, L2_gnn_Wq, L2_gnn_bq, L2_gnn_Wk, L2_gnn_bk, L2_gnn_Wv, L2_gnn_bv, L2_gnn_Wo, L2_gnn_bo, L2_gnn_edge_bias, L2_gnn_W1, L2_gnn_b1, L2_gnn_W2, L2_gnn_b2, L2_gnn_g1, L2_gnn_be1, L2_gnn_g2, L2_gnn_be2, L3_gnn_Wm, L3_gnn_bm, L3_gnn_W1, L3_gnn_b1, L3_gnn_W2, L3_gnn_b2):
    import jax
    import jax.numpy as jnp

    def _L0_gnn_ref(X, edge_index, edge_weight, p, w_ih, w_hh, b_ih, b_hh, W0):
        import jax, jax.numpy as jnp
        import numpy as np
        N = 3125
        C = 128
        E = 50000

        def _gru_step(x, h, w_ih, w_hh, b_ih, b_hh):
            gi = x @ w_ih.T + b_ih
            gh = h @ w_hh.T + b_hh
            i_r, i_z, i_n = jnp.split(gi, 3, axis=-1)
            h_r, h_z, h_n = jnp.split(gh, 3, axis=-1)
            r = jax.nn.sigmoid(i_r + h_r)
            z = jax.nn.sigmoid(i_z + h_z)
            n = jnp.tanh(i_n + r * h_n)
            return (1.0 - z) * n + z * h
        n, c = X.shape
        score = X @ p / jnp.linalg.norm(p)
        top_vals, top_idx = jax.lax.top_k(score, c)
        X_tilde = X[top_idx] * jnp.tanh(top_vals)[:, None]
        W = _gru_step(X_tilde, W0, w_ih, w_hh, b_ih, b_hh)
        XW = X @ W
        src, dst = (edge_index[0], edge_index[1])
        loop = jnp.arange(n)
        src_sl = jnp.concatenate([src, loop])
        dst_sl = jnp.concatenate([dst, loop])
        w_sl = jnp.concatenate([edge_weight, jnp.ones((n,), XW.dtype)])
        deg = jnp.zeros((n,), XW.dtype).at[dst_sl].add(w_sl)
        dinv = jnp.where(deg > 0, jax.lax.rsqrt(deg), 0.0)
        norm = dinv[src_sl] * w_sl * dinv[dst_sl]
        out = jnp.zeros_like(XW).at[dst_sl].add(norm[:, None] * XW[src_sl])
        return out

    def _L1_gnn_ref(x, edge_index, W_pre, b_pre, W_post, b_post, W_lin, b_lin):
        import jax, jax.numpy as jnp
        import numpy as np
        N, E, F = (50000, 25000, 128)
        DELTA = 1.0
        EPS = 1e-05

        def _pna_forward(x, edge_index, W_pre, b_pre, W_post, b_post, W_lin, b_lin):
            src, dst = (edge_index[0], edge_index[1])
            n = x.shape[0]
            h = jnp.concatenate([x[dst], x[src]], axis=-1)
            m = h @ W_pre.T + b_pre
            deg = jax.ops.segment_sum(jnp.ones((m.shape[0],), m.dtype), dst, num_segments=n)
            deg_c = jnp.maximum(deg, 1.0)[:, None]
            has_edge = (deg > 0)[:, None]
            mx = jax.ops.segment_max(m, dst, num_segments=n)
            mx = jnp.where(has_edge, mx, 0.0)
            mn = jax.ops.segment_min(m, dst, num_segments=n)
            mn = jnp.where(has_edge, mn, 0.0)
            s1 = jax.ops.segment_sum(m, dst, num_segments=n)
            s2 = jax.ops.segment_sum(m * m, dst, num_segments=n)
            mean = s1 / deg_c
            var = s2 / deg_c - mean * mean
            std = jnp.sqrt(jax.nn.relu(var) + EPS)
            agg = jnp.concatenate([mx, mn, mean, std], axis=-1)
            log_deg = jnp.log(deg_c + 1.0)
            amp = log_deg / DELTA
            att = DELTA / log_deg
            scaled = jnp.concatenate([agg, agg * amp, agg * att], axis=-1)
            out = jnp.concatenate([x, scaled], axis=-1) @ W_post.T + b_post
            return out @ W_lin.T + b_lin
        return _pna_forward(x, edge_index, W_pre, b_pre, W_post, b_post, W_lin, b_lin)

    def _L2_gnn_ref(x, edge_index, edge_type, Wq, bq, Wk, bk, Wv, bv, Wo, bo, edge_bias, W1, b1, W2, b2, g1, be1, g2, be2):
        import jax, jax.numpy as jnp
        import numpy as np
        N = 3125
        E = 50000
        D = 128
        H = 8
        HD = D // H
        T = 8

        def _layernorm(x, g, b, eps=1e-05):
            m = jnp.mean(x, axis=-1, keepdims=True)
            v = jnp.mean((x - m) ** 2, axis=-1, keepdims=True)
            return (x - m) * jax.lax.rsqrt(v + eps) * g + b
        n = x.shape[0]
        scale = HD ** (-0.5)
        Q = (x @ Wq + bq).reshape(n, H, HD)
        K = (x @ Wk + bk).reshape(n, H, HD)
        V = (x @ Wv + bv).reshape(n, H, HD)
        src, dst = (edge_index[0], edge_index[1])
        attn = jnp.sum(Q[dst] * K[src], axis=-1) * scale + edge_bias[edge_type]
        mx = jax.ops.segment_max(attn, dst, num_segments=n)
        ex = jnp.exp(attn - mx[dst])
        sm = jax.ops.segment_sum(ex, dst, num_segments=n)
        a = ex / (sm[dst] + 1e-16)
        out = jax.ops.segment_sum(a[..., None] * V[src], dst, num_segments=n)
        out = out.reshape(n, D) @ Wo + bo
        x = _layernorm(x + out, g1, be1)
        ffn = jax.nn.gelu(x @ W1 + b1, approximate=False) @ W2 + b2
        return _layernorm(x + ffn, g2, be2)

    def _L3_gnn_ref(z, edge_weight, edge_src, edge_dst, Wm, bm, W1, b1, W2, b2):
        import jax, jax.numpy as jnp
        import numpy as np
        N_NODES = 50000
        N_EDGES = 25000
        HID = 128
        n, H = z.shape
        Wd, Ws, ww = (Wm[:H], Wm[H:2 * H], Wm[2 * H])
        msgs = z[edge_dst] @ Wd + z[edge_src] @ Ws + edge_weight[:, None] * ww[None, :] + bm
        agg = jax.ops.segment_max(msgs, edge_dst, num_segments=n)
        deg = jax.ops.segment_sum(jnp.ones_like(edge_weight), edge_dst, num_segments=n)
        agg = jnp.where(deg[:, None] > 0, agg, jnp.zeros((), dtype=z.dtype))
        W1a, W1b = (W1[:H], W1[H:])
        hidden = jax.nn.relu(z @ W1a + agg @ W1b + b1)
        return hidden @ W2 + b2
    edge_index = jnp.stack([src, dst])
    x = _layernorm(x + _L0_gnn_ref(x, edge_index, edge_weight, L0_gnn_p, L0_gnn_w_ih, L0_gnn_w_hh, L0_gnn_b_ih, L0_gnn_b_hh, L0_gnn_W0), axis=-1)
    x = _layernorm(x + _L1_gnn_ref(x, edge_index, L1_gnn_W_pre, L1_gnn_b_pre, L1_gnn_W_post, L1_gnn_b_post, L1_gnn_W_lin, L1_gnn_b_lin), axis=-1)
    x = _layernorm(x + _L2_gnn_ref(x, edge_index, edge_type_8, L2_gnn_Wq, L2_gnn_bq, L2_gnn_Wk, L2_gnn_bk, L2_gnn_Wv, L2_gnn_bv, L2_gnn_Wo, L2_gnn_bo, L2_gnn_edge_bias, L2_gnn_W1, L2_gnn_b1, L2_gnn_W2, L2_gnn_b2, L2_gnn_g1, L2_gnn_be1, L2_gnn_g2, L2_gnn_be2), axis=-1)
    x = _layernorm(x + _L3_gnn_ref(x, edge_weight, src, dst, L3_gnn_Wm, L3_gnn_bm, L3_gnn_W1, L3_gnn_b1, L3_gnn_W2, L3_gnn_b2), axis=-1)
    return x

_drawn_inputs = setup_inputs


def setup_inputs(seed=0):
    import zlib

    import numpy as np

    out = dict(_drawn_inputs(seed))
    spreads = {'L1_gnn_b_pre': (0.0, 0.1),
     'L1_gnn_b_post': (0.0, 0.1),
     'L1_gnn_b_lin': (0.0, 0.1),
     'L2_gnn_bq': (0.0, 2.0),
     'L2_gnn_bk': (0.0, 2.0),
     'L2_gnn_bv': (0.0, 0.8),
     'L2_gnn_bo': (0.0, 0.1),
     'L2_gnn_b1': (0.0, 0.8),
     'L2_gnn_b2': (0.0, 0.1),
     'L2_gnn_g1': (1.0, 0.2),
     'L2_gnn_be1': (0.0, 0.1),
     'L2_gnn_g2': (1.0, 0.2),
     'L2_gnn_be2': (0.0, 0.1)}
    factors = {'L2_gnn_Wq': 8.0,
     'L2_gnn_Wk': 8.0,
     'L2_gnn_Wv': 4.156,
     'L2_gnn_Wo': 3.713,
     'L2_gnn_edge_bias': 183.207,
     'L2_gnn_W1': 4.248,
     'L2_gnn_W2': 3.865,
     'L3_gnn_bm': 3.09}
    for name, (base, spread) in spreads.items():
        noise = np.random.default_rng([zlib.crc32(name.encode()), seed]).standard_normal(out[name].shape)
        drawn = base * np.exp(spread * noise) if base else spread * noise
        out[name] = jnp.asarray(drawn.astype(out[name].dtype))
    for name, factor in factors.items():
        out[name] = (out[name] * factor).astype(out[name].dtype)
    return out
```

```python
from contextlib import ExitStack

import concourse.bass as bass
from concourse import mybir

F32 = mybir.dt.float32
BF16 = mybir.dt.bfloat16
I32 = mybir.dt.int32
U32 = mybir.dt.uint32
ALU = mybir.AluOpType
ACT = mybir.ActivationFunctionType
AX = mybir.AxisListType.X

P = 128
TPG = 4
GROUP = P * TPG
TOP = 128
HEADS = 8
TYPES = 8
LOW = -3.0e38
EPS = 1e-5
ROOT = float(P) ** -0.5


def ceil_to(n, m):
    return (n + m - 1) // m * m


class Plan:

    def __init__(self, nodes, edges):
        self.N, self.E = nodes, edges
        self.DS, self.ES = 4, 2
        self.EG = ceil_to((edges + GROUP - 1) // GROUP, self.ES)
        self.EP = self.EG * GROUP
        self.ET = self.EG * TPG
        self.NF = nodes // GROUP
        self.DG = ceil_to((nodes + GROUP - 1) // GROUP, self.DS)
        self.R = self.DG * GROUP
        self.C = (nodes + P - 1) // P
        self.LAST = nodes - (P - 1) * self.C
        assert 0 < self.LAST <= self.C and (nodes - self.NF * GROUP) % TPG == 0


def tiles(ap):
    return ap.rearrange("p (t f) -> p t f", t=TPG)


def over(ap, n):
    return ap.unsqueeze(2).to_broadcast([ap.shape[0], ap.shape[1], n])


def each(ap, n):
    return ap.unsqueeze(1).to_broadcast([ap.shape[0], n, ap.shape[1]])



def wait(eng, sem, count):
    if not (isinstance(count, int) and count == 0):
        eng.wait_ge(sem, count)


def each_round(eng, rounds, one_round):
    one_round(0)
    if rounds > 1:
        with eng.Fori(1, rounds) as i:
            one_round(i)


class Mem:

    def __init__(self, nc):
        self.nc = nc
        self.gate = None

    def settle(self, eng):
        if self.gate is None:
            self.gate = self.sem(f"settled_{eng.engine.name}_{self.nc.next_id()}")
        eng.sem_inc(self.gate, 1)

    def sb(self, name, shape, dt=F32):
        return self.nc.alloc_sbuf_tensor(name, shape, dt)

    def ps(self, name):
        return self.nc.alloc_psum_tensor(name, [P, 512], F32)

    def sem(self, name):
        return self.nc.alloc_semaphore(name)

    def sems(self, name, n):
        return [self.sem(f"{name}{k}") for k in range(n)]


class Norm:

    def __init__(self, mem, name, S, per, squares=True, stats=False):
        self.per, self.mem = per, mem
        if squares:
            self.sq = [mem.sb(f"{name}_sq{s}", [P, TPG, P + 1]) for s in range(S)]
            self.squared = mem.sems(name + "_squared", S)
        if stats:
            self.st = [mem.sb(f"{name}_st{s}", [P, TPG, 6]) for s in range(S)]
            self.mv = [mem.sb(f"{name}_mv{s}", [P, TPG, 2]) for s in range(S)]
            self.stats_made = mem.sems(name + "_stats_made", S)
        self.var = [mem.sb(f"{name}_var{s}", [P, TPG]) for s in range(S)]
        self.rstd = [mem.sb(f"{name}_rstd{s}", [P, TPG]) for s in range(S)]
        self.summed = mem.sems(name + "_summed", S)
        self.rooted = mem.sems(name + "_rooted", S)
        self.normed = mem.sems(name + "_normed", S)

    def nth(self, i, j):
        return i * self.per + j + 1

    def set_eps(self, dve, began):
        for sq in self.sq:
            dve.memset(sq[:, :, P:P + 1], EPS).then_inc(began, 1)

    def square(self, act, s, y):
        act.activation(self.sq[s][:, :, 0:P], y, ACT.Square, scale=ROOT).then_inc(self.squared[s], 1)

    def sums(self, dve, i, s, j):
        wait(dve, self.squared[s], self.nth(i, j))
        dve.tensor_reduce(self.var[s][:], self.sq[s][:], AX, ALU.add).then_inc(self.summed[s], 1)

    def moments(self, dve, i, s, y):
        for t in range(TPG):
            dve.bn_stats(self.st[s][:, t, :], y[:, t * P:(t + 1) * P]).then_inc(self.stats_made[s], 1)
        wait(dve, self.stats_made[s], i * 2 * TPG + TPG)
        self.mem.settle(dve)
        for t in range(TPG):
            dve.bn_aggr(self.mv[s][:, t, :], self.st[s][:, t, :]).then_inc(self.stats_made[s], 1)
        wait(dve, self.stats_made[s], i * 2 * TPG + 2 * TPG)
        dve.tensor_scalar(self.var[s][:], self.mv[s][:, :, 1], EPS, None, ALU.add).then_inc(self.summed[s], 1)

    def root(self, pool, i, s, j, minus_half):
        wait(pool, self.summed[s], self.nth(i, j))
        pool.tensor_tensor(self.rstd[s][:], self.var[s][:], minus_half[:], ALU.pow).then_inc(self.rooted[s], 1)

    def scale(self, dve, i, s, j, out, y):
        wait(dve, self.rooted[s], self.nth(i, j))
        dve.tensor_tensor(tiles(out), tiles(y), over(self.rstd[s][:], P), ALU.mult).then_inc(self.normed[s], 1)

    def scale_moments(self, dve, i, s, j, out, y):
        wait(dve, self.rooted[s], self.nth(i, j))
        for t in range(TPG):
            c = slice(t * P, (t + 1) * P)
            ins = dve.tensor_scalar(out[:, c], y[:, c], self.mv[s][:, t, 0:1], self.rstd[s][:, t:t + 1],
                                    ALU.subtract, ALU.mult)
        ins.then_inc(self.normed[s], 1)


def transpose_tiles(pe, out, rows, ident):
    for t in range(TPG):
        mm = pe.transpose(out[:, t:GROUP:TPG], rows[:, t * P:(t + 1) * P], ident[:])
    return mm


def rows_matmul(pe, out, cols, w, start=False, stop=False):
    for t in range(TPG):
        mm = pe.matmul(out[:, t * P:(t + 1) * P], cols[:, t:GROUP:TPG], w,
                       start=start, stop=stop, skip_group_check=True)
    return mm


def const_rows(pe, out, ones, const4):
    pe.matmul(out[:], ones[0:1, 0:P], const4[:], start=True, stop=False, skip_group_check=True)


def groups_of(ap):
    return ap.rearrange("(g p t) f -> g p (t f)", p=P, t=TPG)


class Weights:

    def __init__(self, nc):
        mem = Mem(nc)
        square = lambda name: mem.sb("w_" + name, [P, P])
        self.ident = square("ident")
        self.heads = square("heads")
        self.ones = square("ones")
        self.pna_src = square("pna_src")
        self.pna_dense = square("pna_dense")
        self.wq = square("wq")
        self.wk = square("wk")
        self.wv = square("wv")
        self.wo = square("wo")
        self.g1c = square("g1c")
        self.w1_ffn = square("w1_ffn")
        self.w2_ffn = square("w2_ffn")
        self.w1a = square("w1a")
        self.w1a_edge = square("w1a_edge")
        self.w1b = square("w1b")
        self.w2_msg = square("w2_msg")
        self.msg_src = square("msg_src")
        self.g2 = square("g2")
        self.be2 = square("be2")
        self.bo = square("bo")
        self.gru = square("gru")
        self.gru_dense = square("gru_dense")
        self.post = mem.sb("w_post", [P, 13, P])
        self.own = mem.sb("w_own", [P, 3, P])
        self.head_bias = mem.sb("w_head_bias", [TYPES, P])
        self.type_id = mem.sb("w_type_id", [TYPES, 1])
        self.msg_w = mem.sb("w_msg_w", [1, P])
        self.c_ffn = mem.sb("w_c_ffn", [1, 512])
        self.c_msg = mem.sb("w_c_msg", [1, 512])
        self.c_wo = mem.sb("w_c_wo", [1, 512])
        self.c_pna_dense = mem.sb("w_c_pna_dense", [1, 512])
        self.c_pna = [mem.sb(f"w_c_pna{k}", [1, 512]) for k in range(3)]
        self.minus_half = mem.sb("w_minus_half", [P, TPG])
        self.cols = mem.sb("w_cols", [P, 16])
        self.b1_ffn = mem.sb("w_b1_ffn", [P, 1])
        self.b1_msg = mem.sb("w_b1_msg", [P, 1])


G1, BE1, B1_FFN, BQ, BK, BV, B1_MSG, BM, B_POST, B_PRE = range(10)
R_BE1, R_B2_FFN, R_B2_MSG, R_B_LIN, R_BO, R_MADE = range(6)


def fold_weights(nc, A, W):
    mem = Mem(nc)
    raw_post = mem.sb("f_post", [P, 13 * P])
    raw = {n: mem.sb("f_" + n, [P, P]) for n in ("linT", "pre", "w1", "w2", "wo", "w1b", "w2m", "wdT")}
    bias8 = mem.sb("f_bias8", [TYPES, HEADS])
    id8 = mem.sb("f_id8", [TYPES, 1], I32)
    rows = mem.sb("f_rows", [1, 6, P])
    row = mem.sb("f_row", [1, P])
    sums = mem.sb("f_sums", [P, 1])
    csum = mem.sb("f_csum", [P, P])
    tmp = mem.sb("f_tmp", [P, P])
    bank = [mem.ps(f"f_bank{k}") for k in range(8)]
    loaded, made, step = mem.sem("f_loaded"), mem.sem("f_pool_made"), mem.sem("f_vector_step")
    linT_centred, block_made, block_copied = mem.sem("f_linT_centred"), mem.sem("f_block_made"), mem.sem("f_block_copied")
    csum_made, own_made = mem.sem("f_csum_made"), mem.sem("f_own_made")
    std_made, last_made = mem.sem("f_std_weight"), mem.sem("f_last_products")
    loads = [
        (raw_post[:], A["L1_W_post"]), (raw["linT"][:], A["L1_W_linT"]), (raw["pre"][:], A["L1_W_pre_dst"]),
        (raw["w1"][:], A["L2_W1"]), (raw["w2"][:], A["L2_W2"]), (raw["wo"][:], A["L2_Wo"]),
        (raw["w1b"][:], A["L3_W1"][P:2 * P, :]), (raw["w2m"][:], A["L3_W2"]), (raw["wdT"][:], A["L3_WdT"]),
        (bias8[:], A["L2_edge_bias"]), (W.pna_src[:], A["L1_W_pre_srcT"]), (W.wq[:], A["L2_Wq"]),
        (W.wk[:], A["L2_Wk"]), (W.wv[:], A["L2_Wv"]), (W.msg_src[:], A["L3_Ws"]),
        (W.w1a[:], A["L3_W1"][0:P, :]), (W.w1b[:], A["L3_W1"][P:2 * P, :]), (W.msg_w[:], A["L3_ww"]),
        (W.g2[:], A["L2_g2"].to_broadcast([P, P])), (W.be2[:], A["L2_be2"].to_broadcast([P, P])),
        (W.bo[:], A["L2_bo"].to_broadcast([P, P])), (W.cols[:, 0:10], A["columns"]),
    ] + [(rows[0:1, k, :], A["rows"][k:k + 1, :]) for k in range(5)]
    cols = W.cols

    with nc.Block() as block:
        @block.sync
        def _(sp):
            for out, src in loads:
                sp.dma_start(out, src).then_inc(loaded, 16)

        @block.gpsimd
        def _(pool):
            heads = W.heads[:].rearrange("p (h d) -> p h d", h=HEADS)
            depth = P // HEADS
            pool.memset(W.ident[:], 1.0).then_inc(made, 1)
            pool.memset(W.heads[:], float(depth) ** -0.5).then_inc(made, 1)
            pool.memset(W.minus_half[:], -0.5).then_inc(made, 1)
            pool.memset(W.ones[:], 1.0).then_inc(made, 1)
            pool.iota(id8[:], [[0, 1]], base=0, channel_multiplier=1).then_inc(made, 1)
            pool.wait_ge(made, 5)
            pool.affine_select(out=W.ident[:], in_=W.ident[:], compare_op=ALU.is_equal, fill=0.0,
                               base=0, pattern=[[1, P]], channel_multiplier=-1).then_inc(made, 1)
            pool.affine_select(out=heads, in_=heads, compare_op=ALU.is_ge, fill=0.0, base=0,
                               pattern=[[-depth, HEADS], [0, depth]], channel_multiplier=1).then_inc(made, 1)
            pool.wait_ge(made, 7)
            pool.affine_select(out=heads, in_=heads, compare_op=ALU.is_ge, fill=0.0, base=depth - 1,
                               pattern=[[depth, HEADS], [0, depth]], channel_multiplier=-1).then_inc(made, 1)

        @block.vector
        def _(dve):
            steps = [0]

            def then(ins):
                ins.then_inc(step, 1)
                steps[0] += 1
                dve.wait_ge(step, steps[0])

            def centre(out, src):
                mean = sums[0:src.shape[0], :]
                then(dve.tensor_reduce(mean, src, AX, ALU.add))
                then(dve.tensor_scalar(mean, mean, -1.0 / P, None, ALU.mult))
                then(dve.tensor_scalar(out, src, mean, None, ALU.add))

            def four(out, r):
                then(dve.tensor_copy(tiles(out[:]), each(r, TPG)))

            dve.wait_ge(loaded, 16 * len(loads))
            dve.wait_ge(made, 8)
            centre(raw["linT"][:], raw["linT"][:])
            dve.tensor_copy(row[:], rows[0:1, R_BO, :]).then_inc(linT_centred, 1)
            dve.wait_ge(linT_centred, 1)
            centre(row[:], row[:])
            four(W.c_wo, row[:])
            centre(W.w2_ffn[:], raw["w2"][:])
            centre(W.w2_msg[:], raw["w2m"][:])
            centre(W.wo[:], raw["wo"][:])
            centre(W.bo[:], W.bo[:])
            then(dve.tensor_scalar(W.g1c[:], W.ident[:], cols[:, G1:G1 + 1], None, ALU.mult))
            centre(W.g1c[:], W.g1c[:])
            then(dve.tensor_scalar(W.w1_ffn[:], raw["w1"][:], cols[:, G1:G1 + 1], None, ALU.mult))
            then(dve.tensor_tensor(row[:], rows[0:1, R_BE1, :], rows[0:1, R_B2_FFN, :], ALU.add))
            centre(row[:], row[:])
            four(W.c_ffn, row[:])
            centre(row[:], rows[0:1, R_B2_MSG, :])
            four(W.c_msg, row[:])
            then(dve.tensor_copy(W.head_bias[:].rearrange("p (h d) -> p h d", h=HEADS), over(bias8[:], P // HEADS)))
            then(dve.tensor_copy(W.type_id[:], id8[:]))

            for b in range(13):
                dve.wait_ge(block_made, b + 1)
                dve.tensor_copy(W.post[:, b, :], bank[b % 4][:, 0:P]).then_inc(block_copied, 1)
            dve.wait_ge(block_copied, 13)
            for k in range(3):
                mx, mn, mean = (W.post[:, 1 + 4 * k + n, :] for n in range(3))
                then(dve.tensor_tensor(csum[:], mx, mn, ALU.add))
                dve.tensor_tensor(csum[:], csum[:], mean, ALU.add).then_inc(csum_made, 1)
                then(dve.tensor_scalar(mn, mn, -1.0, None, ALU.mult))
                dve.wait_ge(own_made, k + 1)
                then(dve.tensor_copy(W.own[:, k, :], bank[4][:, 0:P]))
                then(dve.tensor_copy(row[:], bank[5][0:1, 0:P]))
                if k == 0:
                    centre(rows[0:1, R_B_LIN, :], rows[0:1, R_B_LIN, :])
                    then(dve.tensor_tensor(rows[0:1, R_B_LIN, :], rows[0:1, R_B_LIN, :], bank[5][0:1, P:2 * P], ALU.add))
                    then(dve.tensor_tensor(row[:], row[:], rows[0:1, R_B_LIN, :], ALU.add))
                four(W.c_pna[k], row[:])
            then(dve.tensor_scalar(tmp[:], W.ident[:], -1.0 / P, None, ALU.add))
            then(dve.tensor_tensor(W.pna_dense[:], W.post[:, 0, :], tmp[:], ALU.add))
            then(dve.tensor_tensor(W.own[:, 0, :], W.own[:, 0, :], W.pna_dense[:], ALU.add))
            ln2 = 0.6931471805599453
            then(dve.scalar_tensor_tensor(tmp[:], W.post[:, 8, :], ln2, W.post[:, 4, :], ALU.mult, ALU.add))
            then(dve.scalar_tensor_tensor(tmp[:], W.post[:, 12, :], 1.0 / ln2, tmp[:], ALU.mult, ALU.add))
            dve.tensor_scalar(tmp[:], tmp[:], EPS ** 0.5, None, ALU.mult).then_inc(std_made, 1)
            dve.wait_ge(last_made, 1)
            then(dve.tensor_tensor(row[:], rows[0:1, R_B_LIN, :], bank[6][0:1, 0:P], ALU.add))
            four(W.c_pna_dense, row[:])
            dve.tensor_tensor(W.b1_ffn[:], cols[:, B1_FFN:B1_FFN + 1], bank[7][:, 0:1], ALU.add)
            dve.tensor_tensor(W.b1_msg[:], cols[:, B1_MSG:B1_MSG + 1], bank[7][:, 1:2], ALU.add)
            dve.tensor_tensor(W.w1a_edge[:], W.w1a[:], bank[7][:, P:2 * P], ALU.add)

        @block.tensor
        def _(pe):
            pe.wait_ge(loaded, 16 * len(loads))
            pe.wait_ge(made, 8)
            pe.wait_ge(linT_centred, 1)
            for b in range(13):
                if b >= 4:
                    pe.wait_ge(block_copied, b - 3)
                pe.matmul(bank[b % 4][:, 0:P], raw_post[:, b * P:(b + 1) * P], raw["linT"][:],
                          start=True, stop=True).then_inc(block_made, 1)
            pe.matmul(bank[5][0:1, P:2 * P], cols[:, B_POST:B_POST + 1], raw["linT"][:], start=True, stop=True)
            for k in range(3):
                pe.wait_ge(csum_made, k + 1)
                pe.matmul(bank[5][0:1, 0:P], cols[:, B_PRE:B_PRE + 1], csum[:], start=True, stop=True)
                pe.matmul(bank[4][:, 0:P], raw["pre"][:], csum[:], start=True, stop=True).then_inc(own_made, 1)
            pe.wait_ge(std_made, 1)
            pe.matmul(bank[6][0:1, 0:P], W.ones[:, 0:1], tmp[:], start=True, stop=True)
            pe.matmul(bank[7][:, 0:1], raw["w1"][:], cols[:, BE1:BE1 + 1], start=True, stop=True)
            pe.matmul(bank[7][:, 1:2], raw["w1b"][:], cols[:, BM:BM + 1], start=True, stop=True)
            pe.matmul(bank[7][:, P:2 * P], raw["wdT"][:], raw["w1b"][:], start=True, stop=True).then_inc(last_made, 1)


class EdgeData:

    def __init__(self, nc, plan):
        mem = Mem(nc)
        self.keep = mem.sb("e_keep", [P, plan.EP], BF16)
        self.low = mem.sb("e_low", [P, plan.EP], BF16)
        self.src = mem.sb("e_src", [P, plan.ET], I32)
        self.dst = mem.sb("e_dst", [P, plan.ET], I32)
        self.out = mem.sb("e_out", [P, plan.ET], I32)
        self.src0 = mem.sb("e_src0", [P, plan.ET], I32)
        self.dst0 = mem.sb("e_dst0", [P, plan.ET], I32)
        self.coef = mem.sb("e_coef", [P, plan.ET])
        self.dinv = mem.sb("e_dinv", [P, plan.ET])
        self.amp = mem.sb("e_amp", [P, plan.ET])
        self.att = mem.sb("e_att", [P, plan.ET])


def scan_rows(nc, A, D, W, plan):
    EG = plan.EG
    mem = Mem(nc)
    dst, prev = mem.sb("r_dst", [EG, GROUP], I32), mem.sb("r_prev", [EG, GROUP], I32)
    wt = mem.sb("r_wt", [EG, GROUP])
    keep, low = mem.sb("r_keep", [EG, GROUP], BF16), mem.sb("r_low", [EG, GROUP], BF16)
    ones, zeros = mem.sb("r_ones", [EG, GROUP]), mem.sb("r_zeros", [EG, GROUP])
    whole = mem.sb("r_whole", [EG, GROUP])
    part = [mem.sb(f"r_part{k}", [EG, GROUP]) for k in range(2)]
    inv = mem.sb("r_inv", [EG, GROUP])
    line = mem.sb("r_line", [1, 3, EG])
    carry = mem.sb("r_carry", [1, 2, EG + 1])
    enter = mem.sb("r_enter", [EG, 2])
    turned, back = mem.ps("r_turned"), mem.ps("r_back")
    loaded, step, stored = mem.sem("r_loaded"), mem.sem("r_vector_step"), mem.sem("r_stored")
    ends, lined, carried, entered, full = (mem.sem("r_" + n) for n in ("ends", "lined", "carried", "entered", "full"))

    with nc.Block() as block:
        @block.sync
        def _(sp):
            sp.dma_start(dst[:], A["dst_row"]).then_inc(loaded, 16)
            sp.dma_start(prev[:], A["prev_row"]).then_inc(loaded, 16)
            sp.dma_start(wt[:], A["w_row"]).then_inc(loaded, 16)
            sp.wait_ge(full, 1)
            sp.dma_start(D["keep"], keep[:]).then_inc(stored, 16)
            sp.dma_start(D["low"], low[:]).then_inc(stored, 16)
            sp.dma_start(D["count"], part[0][:]).then_inc(stored, 16)
            sp.dma_start(D["wsum"], part[1][:]).then_inc(stored, 16)
            sp.dma_start(D["rcount"], inv[:]).then_inc(stored, 16)
            sp.wait_ge(stored, 80)

        @block.vector
        def _(dve):
            steps = [0]

            def then(ins):
                ins.then_inc(step, 1)
                steps[0] += 1
                dve.wait_ge(step, steps[0])

            then(dve.memset(ones[:], 1.0))
            then(dve.memset(zeros[:], 0.0))
            then(dve.memset(carry[:], 0.0))
            dve.wait_ge(loaded, 48)
            then(dve.tensor_tensor(keep[:], dst[:], prev[:], ALU.is_equal))
            then(dve.tensor_scalar(low[:], keep[:], -1.0, -LOW, ALU.add, ALU.mult))
            then(dve.tensor_tensor_scan(part[0][:], keep[:], ones[:], 0.0, ALU.mult, ALU.add))
            then(dve.tensor_tensor_scan(part[1][:], keep[:], wt[:], 0.0, ALU.mult, ALU.add))
            dve.tensor_tensor_scan(whole[:], keep[:], zeros[:], 1.0, ALU.mult, ALU.add).then_inc(ends, 1)
            dve.wait_ge(lined, 1)
            for k in range(3):
                then(dve.tensor_copy(line[:, k, :], turned[0:1, k * P:k * P + EG]))
            then(dve.tensor_tensor_scan(carry[:, 0, 1:], line[:, 2, :], line[:, 0, :], 0.0, ALU.mult, ALU.add))
            dve.tensor_tensor_scan(carry[:, 1, 1:], line[:, 2, :], line[:, 1, :], 0.0, ALU.mult, ALU.add).then_inc(carried, 1)
            dve.wait_ge(entered, 1)
            then(dve.tensor_copy(enter[:], back[0:EG, 0:2]))
            for k in range(2):
                then(dve.scalar_tensor_tensor(part[k][:], whole[:], enter[:, k:k + 1], part[k][:], ALU.mult, ALU.add))
            dve.reciprocal(inv[:], part[0][:]).then_inc(full, 1)

        @block.tensor
        def _(pe):
            pe.wait_ge(ends, 1)
            last = slice(GROUP - 1, GROUP)
            for k, rows in enumerate((part[0], part[1], whole)):
                mm = pe.transpose(turned[0:1, k * P:k * P + EG], rows[:, last], W.ident[0:EG, 0:EG])
            mm.then_inc(lined, 1)
            pe.wait_ge(carried, 1)
            for k in range(2):
                mm = pe.matmul(back[0:EG, k:k + 1], carry[0:1, k, 0:EG], W.ones[0:1, 0:1], start=True, stop=True)
            mm.then_inc(entered, 1)


def edge_tables(nc, A, D, W, Ed, plan):
    N, C, ET, EG, EP = plan.N, plan.C, plan.ET, plan.EG, plan.EP
    mem = Mem(nc)
    nxt = mem.sb("t_next", [P, ET], I32)
    dsti = mem.sb("t_dst", [P, ET], I32)
    wt, cnt, wsum = (mem.sb("t_" + n, [P, ET]) for n in ("wt", "cnt", "wsum"))
    half, none, end = (mem.sb("t_" + n, [P, ET]) for n in ("half", "none", "end"))
    pos = mem.sb("t_pos", [P, ET], I32)
    own = mem.sb("t_own", [P, ET, 2])
    base_i = mem.sb("t_base_i", [P, C], I32)
    base = mem.sb("t_base", [P, C, 2])
    found = mem.sb("t_found", [P, 2, ET, 2])
    slot = [mem.sb(f"t_slot{u}", [P, TPG], I32) for u in range(2)]
    send = [mem.sb(f"t_send{u}", [P, TPG, 2]) for u in range(2)]
    got = [mem.sb(f"t_got{u}", [P, TPG, 2]) for u in range(2)]
    loaded, step, stored = mem.sem("t_loaded"), mem.sem("t_vector_step"), mem.sem("t_stored")
    made, logged, tables = mem.sem("t_pool_made"), mem.sem("t_logged"), mem.sem("t_tables")
    counted, rooted = mem.sem("t_counted"), mem.sem("t_rooted")
    slotted, moved = mem.sems("t_slotted", 2), mem.sems("t_moved", 2)
    fetched, taken = mem.sems("t_fetched", 2), mem.sems("t_taken", 2)
    all_found, ends_made = mem.sem("t_all_found"), mem.sem("t_ends_made")
    NONE = float(1 << 22)

    with nc.Block() as block:
        @block.sync
        def _(sp):
            tok = lambda ap: ap.rearrange("g (p t) -> p g t", t=TPG)
            flat = lambda ap: ap.rearrange("p (g t) -> p g t", t=TPG)
            for out, src in ((dsti, "dst_tok"), (nxt, "next_tok"), (wt, "w_tok"), (Ed.src0, "src_tok"), (Ed.dst0, "dst0_tok")):
                sp.dma_start(out[:], A[src]).then_inc(loaded, 16)
            sp.dma_start(flat(cnt[:]), tok(D["count"])).then_inc(loaded, 16)
            sp.dma_start(flat(wsum[:]), tok(D["wsum"])).then_inc(loaded, 16)
            for out, src in ((Ed.keep, "keep"), (Ed.low, "low")):
                sp.dma_start(out[:], D[src].rearrange("(o g) p -> o (g p)", o=1).to_broadcast([P, EP])).then_inc(loaded, 16)
            sp.wait_ge(tables, 1)
            sp.dma_start(D["node_row"].rearrange("(p c) k -> p c k", p=P), base[:]).then_inc(stored, 16)
            sp.wait_ge(loaded, 16 * 9)

        @block.vector
        def _(dve):
            steps = [0]

            def then(ins):
                ins.then_inc(step, 1)
                steps[0] += 1
                dve.wait_ge(step, steps[0])

            dve.wait_ge(made, 4)
            then(dve.tensor_copy(base[:, :, 0], base_i[:]))
            dve.memset(base[:, :, 1], 1.0).then_inc(tables, 1)
            dve.wait_ge(loaded, 16 * 9)
            then(dve.tensor_scalar(wsum[:], wsum[:], 1.0, None, ALU.add))
            dve.tensor_copy(own[:, :, 0], pos[:]).then_inc(counted, 1)
            then(dve.tensor_tensor(end[:], dsti[:], nxt[:], ALU.not_equal))
            then(dve.tensor_scalar(end[:], end[:], -NONE, NONE, ALU.mult, ALU.add))
            then(dve.tensor_tensor(end[:], end[:], dsti[:], ALU.add))
            dve.tensor_copy(Ed.out[:], end[:]).then_inc(ends_made, 1)
            dve.wait_ge(logged, 1)
            then(dve.reciprocal(Ed.att[:], Ed.amp[:]))
            dve.wait_ge(rooted, 1)
            dve.tensor_copy(own[:, :, 1], Ed.dinv[:]).then_inc(counted, 1)
            dve.wait_ge(all_found, 2 * EG)
            then(dve.tensor_copy(Ed.src[:], found[:, 0, :, 0]))
            then(dve.tensor_copy(Ed.dst[:], found[:, 1, :, 0]))
            then(dve.tensor_tensor(Ed.coef[:], wt[:], found[:, 0, :, 1], ALU.mult))

        @block.scalar
        def _(act):
            act.wait_ge(loaded, 16 * 9)
            act.activation(Ed.amp[:], cnt[:], ACT.Ln, bias=1.0).then_inc(logged, 1)

        @block.gpsimd
        def _(pool):
            pool.iota(pos[:].rearrange("p (g t) -> p g t", t=TPG), [[GROUP, EG], [1, TPG]], base=plan.R,
                      channel_multiplier=TPG).then_inc(made, 1)
            pool.iota(base_i[:], [[1, C]], base=0, channel_multiplier=C).then_inc(made, 1)
            pool.memset(half[:], -0.5).then_inc(made, 1)
            pool.memset(none[:], NONE).then_inc(made, 1)
            pool.wait_ge(counted, 1)
            pool.wait_ge(made, 4)
            pool.tensor_tensor(Ed.dinv[:], wsum[:], half[:], ALU.pow).then_inc(rooted, 1)
            pool.wait_ge(counted, 2)
            pool.wait_ge(stored, 16)
            pool.wait_ge(ends_made, 1)

            def one_round(i):
                for u in range(2):
                    at = bass.ds((i * 2 + u) * TPG, TPG)
                    wait(pool, moved[u], i * 16 * TPG)
                    pool.tensor_copy(slot[u][:], Ed.out[:, at]).then_inc(slotted[u], 1)
                    pool.tensor_copy(send[u][:], own[:, at, :]).then_inc(slotted[u], 1)
                    wait(pool, slotted[u], i * 2 + 2)
                    mem.settle(pool)
                    for t in range(TPG):
                        pool.indirect_dma_start(
                            out=D["node_row"], out_offset=bass.IndirectOffsetOnAxis(ap=slot[u][:, t:t + 1], axis=0),
                            in_=send[u][:, t, :], in_offset=None, bounds_check=N - 1, oob_is_err=False,
                        ).then_inc(moved[u], 16)

            each_round(pool, EG // 2, one_round)
            for u in range(2):
                pool.wait_ge(moved[u], EG // 2 * 16 * TPG)

            for k, node in enumerate((Ed.src0, Ed.dst0)):
                def one_round(i):
                    for u in range(2):
                        at = bass.ds((i * 2 + u) * TPG, TPG)
                        r = i + k * (EG // 2)
                        pool.tensor_copy(slot[u][:], node[:, at]).then_inc(taken[u], 1)
                        pool.wait_ge(taken[u], r * 2 + 1)
                        mem.settle(pool)
                        for t in range(TPG):
                            pool.indirect_dma_start(
                                out=got[u][:, t, :], out_offset=None, in_=D["node_row"],
                                in_offset=bass.IndirectOffsetOnAxis(ap=slot[u][:, t:t + 1], axis=0),
                            ).then_inc(fetched[u], 16)
                    for u in range(2):
                        at = bass.ds((i * 2 + u) * TPG, TPG)
                        r = i + k * (EG // 2)
                        pool.wait_ge(fetched[u], (r + 1) * 16 * TPG)
                        pool.tensor_copy(found[:, k, at, :], got[u][:]).then_inc(taken[u], 1)
                        pool.wait_ge(taken[u], r * 2 + 2)
                        pool.sem_inc(all_found, 1)

                each_round(pool, EG // 2, one_round)

def scores(nc, A, D, W, plan, score):
    C, LAST = plan.C, plan.LAST
    mem = Mem(nc)
    wide = (C + 7) // 8
    chunks = [(c, min(c + wide, LAST), P) for c in range(0, LAST, wide)]
    chunks += [(c, min(c + wide, C), P - 1) for c in range(LAST, C, wide)]
    BUFS = 3
    buf = [mem.sb(f"s_x{k}", [P, wide * P]) for k in range(BUFS)]
    pb = mem.sb("s_p", [P, P])
    loaded, used = mem.sems("s_loaded", BUFS), mem.sem("s_used")
    p_loaded, weighted, cleared = mem.sem("s_p_loaded"), mem.sem("s_weighted"), mem.sem("s_cleared")

    def pieces(parts):
        return [(0, parts)] if parts % 16 == 0 else [(0, parts // 16 * 16), (parts // 16 * 16, parts)]

    with nc.Block() as block:
        @block.sync
        def _(sp):
            sp.dma_start(pb[:], A["L0_p"].to_broadcast([P, P])).then_inc(p_loaded, 16)
            for n, (a, b, parts) in enumerate(chunks):
                if n >= BUFS:
                    sp.wait_ge(used, n - BUFS + 1)
                for lo, hi in pieces(parts):
                    src = bass.AP(tensor=A["x"].tensor, offset=(lo * C + a) * P,
                                  ap=[[C * P, hi - lo], [1, (b - a) * P]])
                    sp.dma_start(buf[n % BUFS][lo:hi, 0:(b - a) * P], src).then_inc(loaded[n % BUFS], 16)

        @block.vector
        def _(dve):
            dve.memset(score[:], LOW).then_inc(cleared, 1)
            dve.wait_ge(p_loaded, 16)
            dve.wait_ge(cleared, 1)
            total = [0] * BUFS
            for n, (a, b, parts) in enumerate(chunks):
                total[n % BUFS] += 16 * len(pieces(parts))
                dve.wait_ge(loaded[n % BUFS], total[n % BUFS])
                rows = buf[n % BUFS][0:parts, 0:(b - a) * P].rearrange("p (c f) -> p c f", f=P)
                dve.tensor_tensor(rows, rows, each(pb[0:parts, :], b - a), ALU.mult).then_inc(weighted, 1)
                dve.wait_ge(weighted, n + 1)
                dve.tensor_reduce(score[0:parts, a:b], rows, AX, ALU.add).then_inc(used, 1)


def top_nodes(nc, A, D, W, plan, score, weight):
    C = plan.C
    SC = score.shape[1]
    mem = Mem(nc)
    L2R = 16
    v1, i1, n1 = mem.sb("k_v1", [P, TOP]), mem.sb("k_i1", [P, TOP], U32), mem.sb("k_n1", [P, TOP])
    n1i = mem.sb("k_n1i", [P, TOP], I32)
    basei, basef = mem.sb("k_basei", [P, 2], I32), mem.sb("k_basef", [P, 2])
    m2 = mem.sb("k_m2", [L2R, P // L2R * TOP])
    v2, i2, f2 = mem.sb("k_v2", [L2R, TOP]), mem.sb("k_i2", [L2R, TOP], U32), mem.sb("k_f2", [L2R, TOP])
    f2i = mem.sb("k_f2i", [L2R, TOP], I32)
    m3 = mem.sb("k_m3", [1, L2R * TOP])
    v3, i3 = mem.sb("k_v3", [1, TOP]), mem.sb("k_i3", [1, TOP], U32)
    ids = mem.sb("k_ids", [P, 3], I32)
    val = mem.sb("k_val", [P, 1])
    xt, pb = mem.sb("k_xt", [P, P]), mem.sb("k_pb", [P, P])
    pp, norm2, rnorm, th = mem.sb("k_pp", [P, P]), mem.sb("k_norm2", [P, 1]), mem.sb("k_rnorm", [P, 1]), mem.sb("k_th", [P, 1])
    w_ih, w_hh, w0t, w0 = mem.sb("k_w_ih", [P, 3 * P]), mem.sb("k_w_hh", [P, 3 * P]), mem.sb("k_w0t", [P, P]), mem.sb("k_w0", [P, P])
    b_ih, b_hh = mem.sb("k_b_ih", [1, 3 * P]), mem.sb("k_b_hh", [1, 3 * P])
    xtT = mem.sb("k_xtT", [P, P])
    rz, nn = mem.sb("k_rz", [P, 2 * P]), mem.sb("k_nn", [P, P])
    ssum = mem.sb("k_ssum", [P, 1])
    pt, prz, pin, phn = mem.ps("k_pt"), mem.ps("k_prz"), mem.ps("k_pin"), mem.ps("k_phn")
    step, loaded, made = mem.sem("k_step"), mem.sem("k_loaded"), mem.sem("k_made")
    l1_done, l1_stored, l2_loaded = mem.sem("k_l1_done"), mem.sem("k_l1_stored"), mem.sem("k_l2_loaded")
    l2_done, l2_stored, l3_loaded = mem.sem("k_l2_done"), mem.sem("k_l2_stored"), mem.sem("k_l3_loaded")
    l3_done, l3_stored, val_loaded = mem.sem("k_l3_done"), mem.sem("k_l3_stored"), mem.sem("k_val_loaded")
    found, rooted, tanhed = mem.sem("k_found"), mem.sem("k_rooted"), mem.sem("k_tanhed")
    normed, weighted, turned, copied, gates, opened, inner, newed = (
        mem.sem("k_" + n) for n in ("normed", "weighted", "turned", "copied", "gates", "opened", "inner", "newed"))
    row = lambda ap, p: ap.rearrange("(p c) k -> p (c k)", p=p)

    with nc.Block() as block:
        @block.sync
        def _(sp):
            for out, src in ((w_ih, A["L0_w_ihT"]), (w_hh, A["L0_w_hhT"]), (w0t, A["L0_W0T"]), (w0, A["L0_W0"]),
                             (b_ih, A["L0_b_ih"]), (b_hh, A["L0_b_hh"]), (pb, A["L0_p"].to_broadcast([P, P]))):
                sp.dma_start(out[:], src).then_inc(loaded, 16)
            sp.wait_ge(l1_done, 1)
            sp.dma_start(row(D["top_val1"], P), v1[:]).then_inc(l1_stored, 16)
            sp.dma_start(row(D["top_node"], P), n1i[:]).then_inc(l1_stored, 16)
            sp.wait_ge(l1_stored, 32)
            sp.dma_start(m2[:], row(D["top_val1"], L2R)).then_inc(l2_loaded, 16)
            sp.wait_ge(l2_done, 1)
            sp.dma_start(row(D["top_val2"], L2R), v2[:]).then_inc(l2_stored, 16)
            sp.dma_start(row(D["top_place"], L2R), f2i[:]).then_inc(l2_stored, 16)
            sp.wait_ge(l2_stored, 32)
            sp.dma_start(m3[:], row(D["top_val2"], 1)).then_inc(l3_loaded, 16)
            sp.wait_ge(l3_done, 1)
            sp.dma_start(row(D["top_val3"], 1), v3[:]).then_inc(l3_stored, 16)
            sp.dma_start(row(D["top_place3"], 1), i3[:].bitcast(I32)).then_inc(l3_stored, 16)
            sp.wait_ge(l3_stored, 32)
            sp.dma_start(val[:], D["top_val3"]).then_inc(val_loaded, 16)
            sp.dma_start(ids[:, 0:1], D["top_place3"]).then_inc(val_loaded, 16)
            sp.wait_ge(val_loaded, 32)

        @block.gpsimd
        def _(pool):
            pool.iota(basei[:], [[0, 2]], base=0, channel_multiplier=C).then_inc(made, 1)
            pool.wait_ge(made, 1)
            pool.iota(basei[0:L2R, 1:2], [[0, 1]], base=0, channel_multiplier=P // L2R * TOP).then_inc(made, 1)
            pool.wait_ge(normed, 1)
            pool.tensor_tensor(rnorm[:], norm2[:], W.minus_half[:, 0:1], ALU.pow).then_inc(rooted, 1)
            pool.wait_ge(val_loaded, 32)
            pool.wait_ge(l2_stored, 32)
            for k, table in enumerate(("top_place", "top_node")):
                pool.indirect_dma_start(out=ids[:, k + 1:k + 2], out_offset=None, in_=D[table],
                                        in_offset=bass.IndirectOffsetOnAxis(ap=ids[:, k:k + 1], axis=0)).then_inc(found, 16)
                pool.wait_ge(found, 16 * (k + 1))
            pool.indirect_dma_start(out=xt[:], out_offset=None, in_=A["x"],
                                    in_offset=bass.IndirectOffsetOnAxis(ap=ids[:, 2:3], axis=0)).then_inc(found, 16)
            pool.wait_ge(found, 48)

        @block.scalar
        def _(act):
            act.wait_ge(rooted, 1)
            act.wait_ge(val_loaded, 32)
            act.activation(th[:], val[:], ACT.Tanh, scale=rnorm[:, 0:1]).then_inc(tanhed, 1)
            act.wait_ge(gates, 1)
            act.activation(rz[:], prz[:, 0:2 * P], ACT.Sigmoid).then_inc(opened, 1)
            act.wait_ge(inner, 1)
            act.activation(nn[:], nn[:], ACT.Tanh).then_inc(newed, 1)

        @block.tensor
        def _(pe):
            pe.wait_ge(loaded, 16 * 7)
            pe.matmul(prz[:, 0:2 * P], w0t[:], w_hh[:, 0:2 * P], start=True, stop=False)
            pe.matmul(prz[:, 0:2 * P], W.ones[0:1, :], b_hh[0:1, 0:2 * P], start=False, stop=False)
            pe.matmul(prz[:, 0:2 * P], W.ones[0:1, :], b_ih[0:1, 0:2 * P], start=False, stop=False)
            pe.matmul(phn[:, 0:P], w0t[:], w_hh[:, 2 * P:], start=True, stop=False)
            pe.matmul(phn[:, 0:P], W.ones[0:1, :], b_hh[0:1, 2 * P:], start=False, stop=True)
            pe.matmul(pin[:, 0:P], W.ones[0:1, :], b_ih[0:1, 2 * P:], start=True, stop=False)
            pe.wait_ge(weighted, 1)
            pe.transpose(pt[:, 0:P], xt[:], W.ident[:]).then_inc(turned, 1)
            pe.wait_ge(copied, 1)
            pe.matmul(prz[:, 0:2 * P], xtT[:], w_ih[:, 0:2 * P], start=False, stop=True)
            pe.matmul(pin[:, 0:P], xtT[:], w_ih[:, 2 * P:], start=False, stop=True).then_inc(gates, 1)

        @block.vector
        def _(dve):
            steps = [0]

            def then(ins):
                ins.then_inc(step, 1)
                steps[0] += 1
                dve.wait_ge(step, steps[0])

            def best(values, out, place):
                for r in range(TOP // 8):
                    c = slice(8 * r, 8 * r + 8)
                    then(dve.max(out[:, c], values[:]))
                    then(dve.max_index(place[:, c], out[:, c], values[:]))
                    then(dve.match_replace(values[:], out[:, c], values[:], LOW))

            dve.wait_ge(loaded, 16 * 7)
            then(dve.tensor_tensor(pp[:], pb[:], pb[:], ALU.mult))
            dve.tensor_reduce(norm2[:], pp[:], AX, ALU.add).then_inc(normed, 1)
            dve.wait_ge(made, 2)
            then(dve.tensor_copy(basef[:], basei[:]))
            best(score, v1, i1)
            then(dve.tensor_copy(n1[:], i1[:]))
            then(dve.tensor_scalar(n1[:], n1[:], basef[:, 0:1], None, ALU.add))
            dve.tensor_copy(n1i[:], n1[:]).then_inc(l1_done, 1)
            dve.wait_ge(l2_loaded, 16)
            best(m2, v2, i2)
            then(dve.tensor_copy(f2[:], i2[:]))
            then(dve.tensor_scalar(f2[:], f2[:], basef[0:L2R, 1:2], None, ALU.add))
            dve.tensor_copy(f2i[:], f2[:]).then_inc(l2_done, 1)
            dve.wait_ge(l3_loaded, 16)
            best(m3, v3, i3)
            dve.tensor_copy(ssum[0:1, :], v3[0:1, 0:1]).then_inc(l3_done, 1)
            dve.wait_ge(l3_done, 1)
            dve.wait_ge(tanhed, 1)
            dve.wait_ge(found, 48)
            dve.tensor_scalar(xt[:], xt[:], th[:, 0:1], None, ALU.mult).then_inc(weighted, 1)
            dve.wait_ge(turned, 1)
            dve.tensor_copy(xtT[:], pt[:, 0:P]).then_inc(copied, 1)
            dve.wait_ge(opened, 1)
            then(dve.tensor_tensor(nn[:], rz[:, 0:P], phn[:, 0:P], ALU.mult))
            dve.tensor_tensor(nn[:], nn[:], pin[:, 0:P], ALU.add).then_inc(inner, 1)
            dve.wait_ge(newed, 1)
            then(dve.tensor_tensor(weight[:], w0[:], nn[:], ALU.subtract))
            then(dve.tensor_tensor(weight[:], weight[:], rz[:, P:2 * P], ALU.mult))
            then(dve.tensor_tensor(weight[:], weight[:], nn[:], ALU.add))
            then(dve.tensor_reduce(ssum[:], weight[:], AX, ALU.add))
            then(dve.tensor_scalar(ssum[:], ssum[:], -1.0 / P, None, ALU.mult))
            then(dve.tensor_copy(W.gru[:], weight[:]))
            then(dve.tensor_scalar(weight[:], weight[:], ssum[:, 0:1], -1.0 / P, ALU.add, ALU.add))
            then(dve.tensor_tensor(W.gru_dense[:], weight[:], W.ident[:], ALU.add))


class FeedForward:

    def __init__(self, mem, name, S, W, norm, j, last, jl, bank_wide, bank_rows, n, nT, h, y3):
        self.n, self.nT, self.h, self.y3 = n, nT, h, y3
        self.S, self.W, self.norm, self.j, self.last, self.jl = S, W, norm, j, last, jl
        self.bw, self.br = bank_wide, bank_rows
        self.turned, self.copied, self.hidden, self.gelued, self.rows_made, self.joined, self.added = (
            mem.sems(name + "_" + n, S)
            for n in ("turned", "copied", "hidden", "gelued", "rows_made", "joined", "added"))

    def pe(self, pe, i):
        W = self.W
        for s in range(self.S):
            wait(pe, self.norm.normed[s], self.norm.nth(i, self.j))
            transpose_tiles(pe, self.bw[s], self.n[s], W.ident).then_inc(self.turned[s], 1)
        for s in range(self.S):
            wait(pe, self.copied[s], i + 1)
            pe.matmul(self.bw[s][:], W.w1_ffn[:], self.nT[s][:], start=True, stop=True).then_inc(self.hidden[s], 1)
        for s in range(self.S):
            const_rows(pe, self.br[s], W.ones, W.c_ffn)
            rows_matmul(pe, self.br[s], self.nT[s], W.g1c[:])
            wait(pe, self.gelued[s], i + 1)
            rows_matmul(pe, self.br[s], self.h[s], W.w2_ffn[:], stop=True).then_inc(self.rows_made[s], 1)

    def act(self, act, i):
        for s in range(self.S):
            wait(act, self.turned[s], i + 1)
            act.copy(self.nT[s][:], self.bw[s][:]).then_inc(self.copied[s], 1)
        for s in range(self.S):
            wait(act, self.hidden[s], i + 1)
            act.activation(self.h[s][:], self.bw[s][:], ACT.Gelu, bias=self.W.b1_ffn[:, 0:1]).then_inc(self.gelued[s], 1)
        for s in range(self.S):
            wait(act, self.rows_made[s], i + 1)
            self.norm.square(act, s, tiles(self.br[s][:]))

    def dve(self, dve, i, x, out):
        for s in range(self.S):
            self.norm.sums(dve, i, s, self.j + 1)
        for s in range(self.S):
            wait(dve, self.added[s], i + 1)
            wait(dve, self.norm.rooted[s], self.norm.nth(i, self.j + 1))
            for t in range(TPG):
                c = slice(t * P, (t + 1) * P)
                ins = dve.scalar_tensor_tensor(self.n[s][:, c], self.br[s][:, c], self.norm.rstd[s][:, t:t + 1],
                                               self.W.g2[:], ALU.mult, ALU.mult)
            ins.then_inc(self.norm.normed[s], 1)
        for s in range(self.S):
            wait(dve, self.norm.normed[s], self.norm.nth(i, self.j + 1))
            dve.tensor_tensor(self.y3[s][:], self.n[s][:], x[s][:], ALU.add).then_inc(self.joined[s], 1)
        for s in range(self.S):
            wait(dve, self.joined[s], i + 1)
            self.last.moments(dve, i, s, self.y3[s])
        for s in range(self.S):
            self.last.scale_moments(dve, i, s, self.jl, out[s], self.y3[s])

    def pool(self, pool, i):
        for s in range(self.S):
            self.norm.root(pool, i, s, self.j + 1, self.W.minus_half)
        for s in range(self.S):
            self.last.root(pool, i, s, self.jl, self.W.minus_half)


def dense_pass(nc, A, D, W, plan):
    S, N, DG = plan.DS, plan.N, plan.DG
    mem = Mem(nc)
    sb4 = lambda n: [mem.sb(f"d_{n}{s}", [P, GROUP]) for s in range(S)]
    x, xT, x1, x2, y, x2b, x3, x4 = (sb4(n) for n in ("x", "xT", "x1", "x2", "y", "x2b", "x3", "x4"))
    bank_wide = [mem.ps(f"d_wide{s}") for s in range(S)]
    bank_rows = [mem.ps(f"d_rows{s}") for s in range(S)]
    norm = Norm(mem, "dn", S, 5)
    last = Norm(Mem(nc), "dl", S, 1, squares=False, stats=True)
    ff = FeedForward(mem, "df", S, W, norm, 2, last, 0, bank_wide, bank_rows,
                     sb4("n"), sb4("nT"), sb4("h"), sb4("y3"))
    names = ("loaded", "turned", "copied", "rows_made", "residual", "hidden", "relued", "st1", "st2", "st3", "st4", "biased")
    sem = {n: mem.sems("d_" + n, S) for n in names}
    loaded, turned, copied, rows_made, residual, hidden, relued, st1, st2, st3, st4, biased = (sem[n] for n in names)
    began = mem.sem("d_began")
    rounds = DG // S
    xg = A["x"]
    out_g = D["out"]

    def load(sp, g, s):
        full = g < plan.NF if isinstance(g, int) else True
        if full:
            sp.dma_start(x[s][:], bass.AP(tensor=xg.tensor, offset=g * GROUP * P, ap=[[TPG * P, P], [1, TPG * P]])).then_inc(loaded[s], 16)
        elif g * GROUP < N:
            parts = (N - g * GROUP) // TPG
            sp.dma_start(x[s][0:parts, :], bass.AP(tensor=xg.tensor, offset=g * GROUP * P,
                                                   ap=[[TPG * P, parts], [1, TPG * P]])).then_inc(loaded[s], 16)
        else:
            sp.dma_start(x[s][:], bass.AP(tensor=xg.tensor, offset=0, ap=[[TPG * P, P], [1, TPG * P]])).then_inc(loaded[s], 16)

    def store(eng, g, s):
        if not isinstance(g, int) or g < plan.NF:
            eng.dma_start(bass.AP(tensor=out_g.tensor, offset=g * GROUP * P, ap=[[TPG * P, P], [1, TPG * P]]), x4[s][:]).then_inc(st4[s], 16)
        elif g * GROUP < N:
            parts = (N - g * GROUP) // TPG
            eng.dma_start(bass.AP(tensor=out_g.tensor, offset=g * GROUP * P, ap=[[TPG * P, parts], [1, TPG * P]]),
                          x4[s][0:parts, :]).then_inc(st4[s], 16)

    with nc.Block() as block:
        @block.sync
        def _(sp):
            t1, t2, t3 = (groups_of(D[f"x{k}"]) for k in (1, 2, 3))

            def body(i, first, peeled):
                for s in range(S):
                    if not first:
                        wait(sp, turned[s], i * 3 - 2)
                    load(sp, i * S + s, s)
                for k, table, rows, stored in ((0, t1, x1, st1), (1, t2, x2, st2)):
                    for s in range(S):
                        wait(sp, norm.normed[s], norm.nth(i, k))
                        sp.dma_start(table[i * S + s], rows[s][:]).then_inc(stored[s], 16)
                for s in range(S):
                    wait(sp, last.normed[s], i + 1)
                    sp.dma_start(t3[i * S + s], x3[s][:]).then_inc(st3[s], 16)
                for s in range(S):
                    wait(sp, norm.normed[s], norm.nth(i, 4))
                    store(sp, i * S + s, s)

            body(0, True, True)
            if rounds > 2:
                with sp.Fori(1, rounds - 1) as i:
                    body(i, False, False)
            if rounds > 1:
                body(rounds - 1, False, True)
            for s in range(S):
                for st in (st1, st2, st3):
                    sp.wait_ge(st[s], 16 * rounds)
                sp.wait_ge(st4[s], 16 * (rounds - 1 if ((rounds - 1) * S + s) * GROUP >= N else rounds))

        @block.tensor
        def _(pe):
            def one_round(i):
                for s in range(S):
                    wait(pe, loaded[s], 16 * i + 16)
                    transpose_tiles(pe, bank_wide[s], x[s], W.ident).then_inc(turned[s], 1)
                for s in range(S):
                    wait(pe, copied[s], 3 * i + 1)
                    wait(pe, residual[s], i)
                    rows_matmul(pe, bank_rows[s], xT[s], W.gru_dense[:], start=True, stop=True).then_inc(rows_made[s], 1)
                for s in range(S):
                    wait(pe, norm.normed[s], norm.nth(i, 0))
                    transpose_tiles(pe, bank_wide[s], x1[s], W.ident).then_inc(turned[s], 1)
                for s in range(S):
                    wait(pe, copied[s], 3 * i + 2)
                    const_rows(pe, bank_rows[s], W.ones, W.c_pna_dense)
                    rows_matmul(pe, bank_rows[s], xT[s], W.pna_dense[:], stop=True).then_inc(rows_made[s], 1)
                ff.pe(pe, i)
                for s in range(S):
                    wait(pe, last.normed[s], i + 1)
                    transpose_tiles(pe, bank_wide[s], x3[s], W.ident).then_inc(turned[s], 1)
                for s in range(S):
                    wait(pe, copied[s], 3 * i + 3)
                    pe.matmul(bank_wide[s][:], W.w1a[:], xT[s][:], start=True, stop=True).then_inc(hidden[s], 1)
                for s in range(S):
                    const_rows(pe, bank_rows[s], W.ones, W.c_msg)
                    wait(pe, relued[s], i + 1)
                    rows_matmul(pe, bank_rows[s], ff.h[s], W.w2_msg[:], stop=True).then_inc(rows_made[s], 1)

            each_round(pe, rounds, one_round)

        @block.scalar
        def _(act):
            def one_round(i):
                def copy(j):
                    for s in range(S):
                        wait(act, turned[s], 3 * i + j + 1)
                        act.copy(xT[s][:], bank_wide[s][:]).then_inc(copied[s], 1)

                for j in range(2):
                    copy(j)
                    for s in range(S):
                        wait(act, rows_made[s], 3 * i + j + 1)
                        norm.square(act, s, tiles(bank_rows[s][:]))
                for s in range(S):
                    wait(act, biased[s], i + 1)
                    norm.square(act, s, tiles(y[s][:]))
                ff.act(act, i)
                copy(2)
                for s in range(S):
                    wait(act, hidden[s], i + 1)
                    act.activation(ff.h[s][:], bank_wide[s][:], ACT.Relu, bias=W.cols[:, B1_MSG:B1_MSG + 1]).then_inc(relued[s], 1)
                for s in range(S):
                    wait(act, residual[s], i + 1)
                    norm.square(act, s, tiles(y[s][:]))

            each_round(act, rounds, one_round)

        @block.gpsimd
        def _(pool):
            def one_round(i):
                for j in range(2):
                    for s in range(S):
                        norm.root(pool, i, s, j, W.minus_half)
                for s in range(S):
                    wait(pool, norm.normed[s], norm.nth(i, 1))
                    pool.tensor_tensor(tiles(y[s][:]), tiles(x2[s][:]), each(W.bo[:], TPG), ALU.add).then_inc(biased[s], 1)
                for s in range(S):
                    norm.root(pool, i, s, 2, W.minus_half)
                for s in range(S):
                    pool.tensor_tensor(tiles(x2b[s][:]), tiles(x2[s][:]), each(W.be2[:], TPG), ALU.add).then_inc(ff.added[s], 1)
                ff.pool(pool, i)
                for s in range(S):
                    norm.root(pool, i, s, 4, W.minus_half)

            each_round(pool, rounds, one_round)

        @block.vector
        def _(dve):
            norm.set_eps(dve, began)
            dve.wait_ge(began, S)
            def one_round(i):
                for j, out, stored in ((0, x1, st1), (1, x2, st2)):
                    for s in range(S):
                        norm.sums(dve, i, s, j)
                    for s in range(S):
                        wait(dve, stored[s], 16 * i)
                        norm.scale(dve, i, s, j, out[s][:], bank_rows[s][:])
                for s in range(S):
                    norm.sums(dve, i, s, 2)
                for s in range(S):
                    norm.scale(dve, i, s, 2, ff.n[s][:], y[s][:])
                for s in range(S):
                    wait(dve, st3[s], 16 * i)
                ff.dve(dve, i, x2b, x3)
                for s in range(S):
                    wait(dve, rows_made[s], 3 * i + 3)
                    dve.tensor_tensor(y[s][:], bank_rows[s][:], x3[s][:], ALU.add).then_inc(residual[s], 1)
                for s in range(S):
                    norm.sums(dve, i, s, 4)
                    wait(dve, residual[s], i + 1)
                for s in range(S):
                    wait(dve, st4[s], 16 * i)
                    norm.scale(dve, i, s, 4, x4[s][:], y[s][:])

            each_round(dve, rounds, one_round)

class Gather:

    def __init__(self, mem, name, S, index, table, rows):
        self.index, self.table, self.rows, self.mem = index, table, rows, mem
        self.slot = [mem.sb(f"{name}_slot{s}", [P, TPG], I32) for s in range(S)]
        self.slotted = mem.sems(name + "_slotted", S)
        self.landed = mem.sems(name + "_landed", S)

    def fetch(self, pool, i, s, g):
        pool.tensor_copy(self.slot[s][:], self.index[:, bass.ds(g * TPG, TPG)]).then_inc(self.slotted[s], 1)
        wait(pool, self.slotted[s], i + 1)
        self.mem.settle(pool)
        for t in range(TPG):
            pool.indirect_dma_start(
                out=self.rows[s][:, t * P:(t + 1) * P], out_offset=None, in_=self.table,
                in_offset=bass.IndirectOffsetOnAxis(ap=self.slot[s][:, t:t + 1], axis=0),
            ).then_inc(self.landed[s], 16)

    def arrived(self, eng, i, s):
        wait(eng, self.landed[s], (i + 1) * 16 * TPG)


def tok(ap, g):
    return over(ap[:, bass.ds(g * TPG, TPG)], P)


def pos(ap, g):
    return ap[:, bass.ds(g * GROUP, GROUP)]


def gcn_edges(nc, A, D, W, Ed, plan):
    S, rounds = plan.ES, plan.EG // plan.ES
    mem = Mem(nc)
    rows = lambda n: [mem.sb(f"g_{n}{s}", [P, GROUP]) for s in range(S)]
    src, own, scaled, ownd, run, u, y, x1 = (rows(n) for n in ("src", "own", "scaled", "ownd", "run", "u", "y", "x1"))
    bank_src, bank_own, bank_out = ([mem.ps(f"g_{n}{s}") for s in range(S)] for n in ("bsrc", "bown", "bout"))
    last = Norm(Mem(nc), "gl", S, 1, squares=False, stats=True)
    gsrc = Gather(mem, "gs", S, Ed.src0, A["x"], src)
    gown = Gather(mem, "go", S, Ed.dst0, A["x"], own)
    weighted, turned, scanned, summed, made, mixed, stored = (
        mem.sems("g_" + n, S) for n in ("weighted", "turned", "scanned", "summed", "made", "mixed", "stored"))
    began = mem.sem("g_began")
    table = groups_of(D["x1"])

    with nc.Block() as block:
        @block.gpsimd
        def _(pool):
            def one_round(i):
                for s in range(S):
                    wait(pool, weighted[s], 2 * i)
                    gsrc.fetch(pool, i, s, i * S + s)
                    wait(pool, mixed[s], 2 * i)
                    gown.fetch(pool, i, s, i * S + s)
                for s in range(S):
                    last.root(pool, i, s, 0, W.minus_half)

            each_round(pool, rounds, one_round)

        @block.vector
        def _(dve):
            dve.memset(run[S - 1][:], 0.0).then_inc(began, 1)
            dve.wait_ge(began, 1)
            def one_round(i):
                for s in range(S):
                    g = i * S + s
                    gsrc.arrived(dve, i, s)
                    dve.tensor_tensor(tiles(scaled[s][:]), tiles(src[s][:]), tok(Ed.coef, g), ALU.mult).then_inc(weighted[s], 1)
                    gown.arrived(dve, i, s)
                    dve.tensor_tensor(tiles(ownd[s][:]), tiles(own[s][:]), tok(Ed.dinv, g), ALU.mult).then_inc(weighted[s], 1)
                for s in range(S):
                    wait(dve, turned[s], i + 1)
                    wait(dve, scanned[s - 1], i + 1 if s else i)
                    dve.tensor_tensor_scan(run[s][:], pos(Ed.keep, i * S + s), bank_src[s][:], run[s - 1][:, GROUP - 1:GROUP],
                                           ALU.mult, ALU.add).then_inc(scanned[s], 1)
                for s in range(S):
                    wait(dve, scanned[s], i + 1)
                    dve.tensor_tensor(u[s][:], run[s][:], bank_own[s][:], ALU.add).then_inc(summed[s], 1)
                for s in range(S):
                    wait(dve, made[s], i + 1)
                    dve.tensor_tensor(tiles(y[s][:]), tiles(bank_out[s][:]), tok(Ed.dinv, i * S + s), ALU.mult).then_inc(mixed[s], 1)
                for s in range(S):
                    wait(dve, mixed[s], 2 * i + 1)
                    dve.tensor_tensor(y[s][:], y[s][:], own[s][:], ALU.add).then_inc(mixed[s], 1)
                for s in range(S):
                    wait(dve, mixed[s], 2 * i + 2)
                    last.moments(dve, i, s, y[s])
                for s in range(S):
                    wait(dve, stored[s], 16 * i)
                    last.scale_moments(dve, i, s, 0, x1[s], y[s])

            each_round(dve, rounds, one_round)

        @block.tensor
        def _(pe):
            def one_round(i):
                for s in range(S):
                    wait(pe, weighted[s], 2 * i + 2)
                    wait(pe, summed[s], i)
                    transpose_tiles(pe, bank_src[s], scaled[s], W.ident)
                    transpose_tiles(pe, bank_own[s], ownd[s], W.ident).then_inc(turned[s], 1)
                for s in range(S):
                    wait(pe, summed[s], i + 1)
                    wait(pe, mixed[s], 2 * i)
                    rows_matmul(pe, bank_out[s], u[s], W.gru[:], start=True, stop=True).then_inc(made[s], 1)

            each_round(pe, rounds, one_round)

        @block.sync
        def _(sp):
            def one_round(i):
                for s in range(S):
                    wait(sp, last.normed[s], i + 1)
                    sp.dma_start(table[i * S + s + plan.DG], x1[s][:]).then_inc(stored[s], 16)

            each_round(sp, rounds, one_round)
            for s in range(S):
                sp.wait_ge(stored[s], 16 * rounds)


def pna_edges(nc, A, D, W, Ed, plan):
    S, rounds = plan.ES, plan.EG // plan.ES
    mem = Mem(nc)
    rows = lambda n: [mem.sb(f"p_{n}{s}", [P, GROUP]) for s in range(S)]
    src, own, srcT, ownT, neg, sqr, rc = (rows(n) for n in ("src", "own", "srcT", "ownT", "neg", "sqr", "rc"))
    mx, mn, s1, s2, mean, var = (rows(n) for n in ("mx", "mn", "s1", "s2", "mean", "var"))
    y, x2 = (rows(n) for n in ("y", "x2"))
    m2, std, ya = sqr, var, neg
    bank = [[mem.ps(f"p_b{s}{k}") for k in range(4)] for s in range(S)]
    norm = Norm(mem, "pn", S, 1)
    gsrc = Gather(mem, "pg", S, Ed.src, D["x1"], src)
    (turned, copied, made, negated, squared, scanned, averaged, m2_made, var_made, rooted, mixed,
     loaded, stored) = (mem.sems("p_" + n, S) for n in (
        "turned", "copied", "made", "negated", "squared", "scanned", "averaged", "m2_made", "var_made", "rooted",
        "mixed", "loaded", "stored"))
    sums_made = mem.sems("p_sums_made", S)
    began = mem.sem("p_began")
    tin, tout = groups_of(D["x1"]), groups_of(D["x2"])
    prev = lambda s, i: (i + 1 if s else i)

    with nc.Block() as block:
        @block.sync
        def _(sp):
            def one_round(i):
                for s in range(S):
                    wait(sp, turned[s], 2 * i)
                    sp.dma_start(own[s][:], tin[i * S + s + plan.DG]).then_inc(loaded[s], 16)
                    wait(sp, averaged[s], 2 * i)
                    sp.dma_start(rc[s][:], D["rcount"][bass.ds(i * S + s, 1), :].to_broadcast([P, GROUP])).then_inc(loaded[s], 16)
                for s in range(S):
                    wait(sp, norm.normed[s], i + 1)
                    sp.dma_start(tout[i * S + s + plan.DG], x2[s][:]).then_inc(stored[s], 16)

            each_round(sp, rounds, one_round)
            for s in range(S):
                sp.wait_ge(stored[s], 16 * rounds)

        @block.gpsimd
        def _(pool):
            def one_round(i):
                for s in range(S):
                    wait(pool, turned[s], 2 * i)
                    gsrc.fetch(pool, i, s, i * S + s)
                for s in range(S):
                    norm.root(pool, i, s, 0, W.minus_half)

            each_round(pool, rounds, one_round)

        @block.tensor
        def _(pe):
            def one_round(i):
                for s in range(S):
                    gsrc.arrived(pe, i, s)
                    wait(pe, mixed[s], 4 * i)
                    transpose_tiles(pe, bank[s][0], src[s], W.ident).then_inc(turned[s], 1)
                    wait(pe, loaded[s], 32 * i + 32)
                    transpose_tiles(pe, bank[s][1], own[s], W.ident).then_inc(turned[s], 1)
                for s in range(S):
                    wait(pe, copied[s], 2 * i + 1)
                    pe.matmul(bank[s][0][:], W.pna_src[:], srcT[s][:], start=True, stop=True).then_inc(made[s], 1)
                for s in range(S):
                    wait(pe, copied[s], 2 * i + 2)
                    for k in range(3):
                        const_rows(pe, bank[s][1 + k], W.ones, W.c_pna[k])
                        rows_matmul(pe, bank[s][1 + k], ownT[s], W.own[:, k, :])
                for s in range(S):
                    for k in range(3):
                        for n, cols in enumerate((mx, mn, mean, std)):
                            if k == 0:
                                if n == 0:
                                    wait(pe, averaged[s], 2 * i + 2)
                                if n == 3:
                                    wait(pe, rooted[s], i + 1)
                            mm = rows_matmul(pe, bank[s][1 + k], cols[s], W.post[:, 1 + 4 * k + n, :], stop=(n == 3))
                    mm.then_inc(sums_made[s], 1)

            each_round(pe, rounds, one_round)

        @block.scalar
        def _(act):
            def one_round(i):
                for s in range(S):
                    wait(act, turned[s], 2 * i + 1)
                    act.copy(srcT[s][:], bank[s][0][:]).then_inc(copied[s], 1)
                    wait(act, turned[s], 2 * i + 2)
                    act.copy(ownT[s][:], bank[s][1][:]).then_inc(copied[s], 1)
                for s in range(S):
                    wait(act, made[s], i + 1)
                    act.activation(neg[s][:], bank[s][0][:], ACT.Copy, scale=-1.0).then_inc(negated[s], 1)
                    act.activation(sqr[s][:], bank[s][0][:], ACT.Square).then_inc(squared[s], 1)
                for s in range(S):
                    wait(act, averaged[s], 2 * i + 1)
                    act.activation(m2[s][:], mean[s][:], ACT.Square).then_inc(m2_made[s], 1)
                for s in range(S):
                    wait(act, var_made[s], 2 * i + 2)
                    act.activation(std[s][:], var[s][:], ACT.Sqrt).then_inc(rooted[s], 1)
                for s in range(S):
                    wait(act, mixed[s], 4 * i + 4)
                    norm.square(act, s, tiles(y[s][:]))

            each_round(act, rounds, one_round)

        @block.vector
        def _(dve):
            norm.set_eps(dve, began)
            for k, rows_ in enumerate((mx, mn, s1, s2)):
                dve.memset(rows_[S - 1][:], 0.0).then_inc(began, 1)
            dve.wait_ge(began, S + 4)
            end = slice(GROUP - 1, GROUP)
            def one_round(i):
                for s in range(S):
                    g = i * S + s
                    wait(dve, made[s], i + 1)
                    wait(dve, negated[s], i + 1)
                    wait(dve, squared[s], i + 1)
                    wait(dve, scanned[s - 1], 4 * prev(s, i))
                    dve.tensor_tensor_scan(s1[s][:], pos(Ed.keep, g), bank[s][0][:], s1[s - 1][:, end], ALU.mult, ALU.add).then_inc(scanned[s], 1)
                    dve.tensor_tensor_scan(s2[s][:], pos(Ed.keep, g), sqr[s][:], s2[s - 1][:, end], ALU.mult, ALU.add).then_inc(scanned[s], 1)
                    dve.tensor_tensor_scan(mx[s][:], pos(Ed.low, g), bank[s][0][:], mx[s - 1][:, end], ALU.add, ALU.max).then_inc(scanned[s], 1)
                    dve.tensor_tensor_scan(mn[s][:], pos(Ed.low, g), neg[s][:], mn[s - 1][:, end], ALU.add, ALU.max).then_inc(scanned[s], 1)
                for s in range(S):
                    wait(dve, loaded[s], 32 * i + 32)
                    wait(dve, scanned[s], 4 * i + 4)
                    dve.tensor_tensor(mean[s][:], s1[s][:], rc[s][:], ALU.mult).then_inc(averaged[s], 1)
                    dve.tensor_tensor(var[s][:], s2[s][:], rc[s][:], ALU.mult).then_inc(averaged[s], 1)
                for s in range(S):
                    wait(dve, averaged[s], 2 * i + 2)
                    wait(dve, m2_made[s], i + 1)
                    dve.tensor_tensor(var[s][:], var[s][:], m2[s][:], ALU.subtract).then_inc(var_made[s], 1)
                for s in range(S):
                    wait(dve, var_made[s], 2 * i + 1)
                    dve.tensor_scalar(var[s][:], var[s][:], 0.0, EPS, ALU.max, ALU.add).then_inc(var_made[s], 1)
                for s in range(S):
                    g = i * S + s
                    wait(dve, sums_made[s], i + 1)
                    dve.tensor_tensor(tiles(ya[s][:]), tiles(bank[s][2][:]), tok(Ed.amp, g), ALU.mult).then_inc(mixed[s], 1)
                    dve.tensor_tensor(tiles(y[s][:]), tiles(bank[s][3][:]), tok(Ed.att, g), ALU.mult).then_inc(mixed[s], 1)
                for s in range(S):
                    wait(dve, mixed[s], 4 * i + 2)
                    dve.tensor_tensor(ya[s][:], ya[s][:], bank[s][1][:], ALU.add).then_inc(mixed[s], 1)
                for s in range(S):
                    wait(dve, mixed[s], 4 * i + 3)
                    dve.tensor_tensor(y[s][:], y[s][:], ya[s][:], ALU.add).then_inc(mixed[s], 1)
                for s in range(S):
                    norm.sums(dve, i, s, 0)
                for s in range(S):
                    wait(dve, mixed[s], 4 * i + 4)
                    wait(dve, stored[s], 16 * i)
                    wait(dve, norm.rooted[s], i + 1)
                    norm.scale(dve, i, s, 0, x2[s][:], y[s][:])

            each_round(dve, rounds, one_round)

def attention_edges(nc, A, D, W, Ed, plan):
    S, rounds = plan.ES, plan.EG // plan.ES
    mem = Mem(nc)
    rows = lambda n: [mem.sb(f"a_{n}{s}", [P, GROUP]) for s in range(S)]
    src, own, srcT, ownT, q, qk = (rows(n) for n in ("src", "own", "srcT", "ownT", "q", "qk"))
    fade, prob, pv, den, acc, x2b = (rows(n) for n in ("fade", "prob", "pv", "den", "acc", "x2b"))
    o, y, x3 = q, qk, pv
    m = [mem.sb(f"a_m{s}", [P, GROUP + 1]) for s in range(S)]
    typ = [mem.sb(f"a_typ{s}", [TYPES, GROUP], I32) for s in range(S)]
    hot = [mem.sb(f"a_hot{s}", [TYPES, GROUP]) for s in range(S)]
    bank = [[mem.ps(f"a_b{s}{k}") for k in range(4)] for s in range(S)]
    norm = Norm(mem, "an", S, 2)
    last = Norm(Mem(nc), "al", S, 1, squares=False, stats=True)
    ff = FeedForward(mem, "af", S, W, norm, 0, last, 0, [b[2] for b in bank], [b[3] for b in bank],
                     n=prob, nT=srcT, h=ownT, y3=fade)
    gsrc = Gather(mem, "as", S, Ed.src, D["x2"], src)
    gown = Gather(mem, "ao", S, Ed.dst, D["x2"], own)
    (turned, copied, q_made, q_moved, kv_made, matched, hot_made, logits, peaked, differed, exped, valued,
     scanned, divided, out_made, residual, loaded, stored) = (mem.sems("a_" + n, S) for n in (
        "turned", "copied", "q_made", "q_moved", "kv_made", "matched", "hot_made", "logits", "peaked", "differed",
        "exped", "valued", "scanned", "divided", "out_made", "residual", "loaded", "stored"))
    began = mem.sem("a_began")
    tout = groups_of(D["x3"])
    BQc, BKc, BVc = (W.cols[:, k:k + 1] for k in (BQ, BK, BV))

    with nc.Block() as block:
        @block.sync
        def _(sp):
            def one_round(i):
                for s in range(S):
                    wait(sp, hot_made[s], i)
                    sp.dma_start(typ[s][:], A["type_row"][bass.ds(i * S + s, 1), :].to_broadcast([TYPES, GROUP])).then_inc(loaded[s], 16)
                for s in range(S):
                    wait(sp, last.normed[s], i + 1)
                    sp.dma_start(tout[i * S + s + plan.DG], x3[s][:]).then_inc(stored[s], 16)

            each_round(sp, rounds, one_round)
            for s in range(S):
                sp.wait_ge(stored[s], 16 * rounds)

        @block.gpsimd
        def _(pool):
            def one_round(i):
                for s in range(S):
                    wait(pool, turned[s], 2 * i)
                    gsrc.fetch(pool, i, s, i * S + s)
                    wait(pool, residual[s], i)
                    gown.fetch(pool, i, s, i * S + s)
                for s in range(S):
                    gown.arrived(pool, i, s)
                    pool.tensor_tensor(tiles(x2b[s][:]), tiles(own[s][:]), each(W.be2[:], TPG), ALU.add).then_inc(ff.added[s], 1)
                for s in range(S):
                    norm.root(pool, i, s, 0, W.minus_half)
                ff.pool(pool, i)

            each_round(pool, rounds, one_round)

        @block.tensor
        def _(pe):
            def one_round(i):
                for s in range(S):
                    gsrc.arrived(pe, i, s)
                    wait(pe, norm.normed[s], 2 * i)
                    transpose_tiles(pe, bank[s][0], src[s], W.ident).then_inc(turned[s], 1)
                    gown.arrived(pe, i, s)
                    transpose_tiles(pe, bank[s][1], own[s], W.ident).then_inc(turned[s], 1)
                for s in range(S):
                    wait(pe, copied[s], 2 * i + 2)
                    pe.matmul(bank[s][2][:], W.wq[:], ownT[s][:], start=True, stop=True).then_inc(q_made[s], 1)
                    pe.matmul(bank[s][3][:], W.wk[:], srcT[s][:], start=True, stop=True)
                    pe.matmul(bank[s][0][:], W.wv[:], srcT[s][:], start=True, stop=True).then_inc(kv_made[s], 1)
                for s in range(S):
                    wait(pe, hot_made[s], i + 1)
                    pe.matmul(bank[s][1][:], W.head_bias[:], hot[s][:], start=True, stop=False)
                    wait(pe, matched[s], i + 1)
                    pe.matmul(bank[s][1][:], W.heads[:], qk[s][:], start=False, stop=True).then_inc(logits[s], 1)
                for s in range(S):
                    const_rows(pe, bank[s][3], W.ones, W.c_wo)
                    wait(pe, divided[s], 3 * i + 3)
                    rows_matmul(pe, bank[s][3], o[s], W.wo[:], stop=True).then_inc(out_made[s], 1)
                ff.pe(pe, i)

            each_round(pe, rounds, one_round)

        @block.scalar
        def _(act):
            def one_round(i):
                for s in range(S):
                    wait(act, turned[s], 2 * i + 1)
                    act.copy(srcT[s][:], bank[s][0][:]).then_inc(copied[s], 1)
                    wait(act, turned[s], 2 * i + 2)
                    act.copy(ownT[s][:], bank[s][1][:]).then_inc(copied[s], 1)
                for s in range(S):
                    wait(act, q_made[s], i + 1)
                    act.activation(q[s][:], bank[s][2][:], ACT.Identity, bias=BQc).then_inc(q_moved[s], 1)
                for s in range(S):
                    wait(act, differed[s], 3 * i + 2)
                    act.activation(fade[s][:], fade[s][:], ACT.Exp).then_inc(exped[s], 1)
                    wait(act, differed[s], 3 * i + 3)
                    act.activation(prob[s][:], prob[s][:], ACT.Exp).then_inc(exped[s], 1)
                for s in range(S):
                    wait(act, residual[s], i + 1)
                    norm.square(act, s, tiles(y[s][:]))
                ff.act(act, i)

            each_round(act, rounds, one_round)

        @block.vector
        def _(dve):
            norm.set_eps(dve, began)
            dve.memset(m[S - 1][:], 0.0).then_inc(began, 1)
            dve.memset(den[S - 1][:], 0.0).then_inc(began, 1)
            dve.memset(acc[S - 1][:], 0.0).then_inc(began, 1)
            dve.wait_ge(began, S + 3)
            end = slice(GROUP - 1, GROUP)
            def one_round(i):
                for s in range(S):
                    wait(dve, loaded[s], 16 * i + 16)
                    dve.tensor_scalar(hot[s][:], typ[s][:], W.type_id[:, 0:1], None, ALU.is_equal).then_inc(hot_made[s], 1)
                for s in range(S):
                    wait(dve, q_moved[s], i + 1)
                    wait(dve, kv_made[s], i + 1)
                    dve.scalar_tensor_tensor(qk[s][:], bank[s][3][:], BKc, q[s][:], ALU.add, ALU.mult).then_inc(matched[s], 1)
                for s in range(S):
                    g = i * S + s
                    before = i + 1 if s else i
                    wait(dve, logits[s], i + 1)
                    wait(dve, peaked[s - 1], 2 * before)
                    dve.tensor_copy(m[s][:, 0:1], m[s - 1][:, GROUP:]).then_inc(peaked[s], 1)
                    dve.tensor_tensor_scan(m[s][:, 1:], pos(Ed.low, g), bank[s][1][:], m[s - 1][:, GROUP:], ALU.add, ALU.max).then_inc(peaked[s], 1)
                    wait(dve, peaked[s], 2 * i + 2)
                    dve.tensor_tensor(fade[s][:], m[s][:, 0:GROUP], pos(Ed.low, g), ALU.add).then_inc(differed[s], 1)
                    dve.tensor_tensor(prob[s][:], bank[s][1][:], m[s][:, 1:], ALU.subtract)
                    wait(dve, differed[s], 3 * i + 1)
                    dve.tensor_tensor(fade[s][:], fade[s][:], m[s][:, 1:], ALU.subtract).then_inc(differed[s], 2)
                for s in range(S):
                    before = i + 1 if s else i
                    wait(dve, exped[s], 2 * i + 2)
                    wait(dve, stored[s], 16 * i)
                    dve.scalar_tensor_tensor(pv[s][:], bank[s][0][:], BVc, prob[s][:], ALU.add, ALU.mult).then_inc(valued[s], 1)
                    wait(dve, scanned[s - 1], 2 * before)
                    dve.tensor_tensor_scan(den[s][:], fade[s][:], prob[s][:], den[s - 1][:, end], ALU.mult, ALU.add).then_inc(scanned[s], 1)
                    wait(dve, valued[s], i + 1)
                    dve.tensor_tensor_scan(acc[s][:], fade[s][:], pv[s][:], acc[s - 1][:, end], ALU.mult, ALU.add).then_inc(scanned[s], 1)
                for s in range(S):
                    wait(dve, scanned[s], 2 * i + 2)
                    dve.tensor_scalar(pv[s][:], den[s][:], 1e-16, None, ALU.add).then_inc(divided[s], 1)
                for s in range(S):
                    wait(dve, divided[s], 3 * i + 1)
                    dve.reciprocal(o[s][:], pv[s][:]).then_inc(divided[s], 1)
                for s in range(S):
                    wait(dve, divided[s], 3 * i + 2)
                    dve.tensor_tensor(o[s][:], acc[s][:], o[s][:], ALU.mult).then_inc(divided[s], 1)
                for s in range(S):
                    gown.arrived(dve, i, s)
                    wait(dve, out_made[s], i + 1)
                    dve.tensor_tensor(y[s][:], bank[s][3][:], own[s][:], ALU.add).then_inc(residual[s], 1)
                for s in range(S):
                    norm.sums(dve, i, s, 0)
                for s in range(S):
                    wait(dve, residual[s], i + 1)
                    norm.scale(dve, i, s, 0, ff.n[s][:], y[s][:])
                ff.dve(dve, i, x2b, x3)

            each_round(dve, rounds, one_round)

def message_edges(nc, A, D, W, Ed, plan):
    S, rounds = plan.ES, plan.EG // plan.ES
    mem = Mem(nc)
    rows = lambda n: [mem.sb(f"m_{n}{s}", [P, GROUP]) for s in range(S)]
    src, own, srcT, ownT, mx, h, y, x4 = (rows(n) for n in ("src", "own", "srcT", "ownT", "mx", "h", "y", "x4"))
    wrow = [mem.sb(f"m_wrow{s}", [1, GROUP]) for s in range(S)]
    oslot = [mem.sb(f"m_oslot{s}", [P, TPG], I32) for s in range(S)]
    bank = [[mem.ps(f"m_b{s}{k}") for k in range(4)] for s in range(S)]
    norm = Norm(mem, "mn", S, 1)
    gsrc = Gather(mem, "mg", S, Ed.src, D["x3"], src)
    turned, copied, made, scanned, hidden, relued, out_made, residual, loaded, oslotted, stored = (
        mem.sems("m_" + n, S) for n in ("turned", "copied", "made", "scanned", "hidden", "relued", "out_made",
                                        "residual", "loaded", "oslotted", "stored"))
    began = mem.sem("m_began")
    tin = groups_of(D["x3"])

    with nc.Block() as block:
        @block.sync
        def _(sp):
            def one_round(i):
                for s in range(S):
                    wait(sp, residual[s], i)
                    sp.dma_start(own[s][:], tin[i * S + s + plan.DG]).then_inc(loaded[s], 16)
                    wait(sp, made[s], i)
                    sp.dma_start(wrow[s][:], A["w_row"][bass.ds(i * S + s, 1), :]).then_inc(loaded[s], 16)

            each_round(sp, rounds, one_round)

        @block.gpsimd
        def _(pool):
            def one_round(i):
                for s in range(S):
                    wait(pool, turned[s], 2 * i)
                    gsrc.fetch(pool, i, s, i * S + s)
                for s in range(S):
                    norm.root(pool, i, s, 0, W.minus_half)
                for s in range(S):
                    wait(pool, stored[s], i * 16 * TPG)
                    pool.tensor_copy(oslot[s][:], Ed.out[:, bass.ds((i * S + s) * TPG, TPG)]).then_inc(oslotted[s], 1)
                    wait(pool, oslotted[s], i + 1)
                    wait(pool, norm.normed[s], i + 1)
                    mem.settle(pool)
                    for t in range(TPG):
                        pool.indirect_dma_start(
                            out=D["out"], out_offset=bass.IndirectOffsetOnAxis(ap=oslot[s][:, t:t + 1], axis=0),
                            in_=x4[s][:, t * P:(t + 1) * P], in_offset=None, bounds_check=plan.N - 1, oob_is_err=False,
                        ).then_inc(stored[s], 16)

            each_round(pool, rounds, one_round)
            for s in range(S):
                pool.wait_ge(stored[s], rounds * 16 * TPG)

        @block.tensor
        def _(pe):
            def one_round(i):
                for s in range(S):
                    gsrc.arrived(pe, i, s)
                    wait(pe, residual[s], i)
                    transpose_tiles(pe, bank[s][0], src[s], W.ident).then_inc(turned[s], 1)
                    wait(pe, loaded[s], 32 * i + 32)
                    transpose_tiles(pe, bank[s][1], own[s], W.ident).then_inc(turned[s], 1)
                for s in range(S):
                    wait(pe, copied[s], 2 * i + 1)
                    pe.matmul(bank[s][0][:], W.msg_src[:], srcT[s][:], start=True, stop=False)
                    pe.matmul(bank[s][0][:], W.msg_w[:], wrow[s][:], start=False, stop=True).then_inc(made[s], 1)
                for s in range(S):
                    wait(pe, copied[s], 2 * i + 2)
                    pe.matmul(bank[s][2][:], W.w1a_edge[:], ownT[s][:], start=True, stop=False)
                    wait(pe, scanned[s], i + 1)
                    pe.matmul(bank[s][2][:], W.w1b[:], mx[s][:], start=False, stop=True).then_inc(hidden[s], 1)
                for s in range(S):
                    const_rows(pe, bank[s][3], W.ones, W.c_msg)
                    wait(pe, relued[s], i + 1)
                    rows_matmul(pe, bank[s][3], h[s], W.w2_msg[:], stop=True).then_inc(out_made[s], 1)

            each_round(pe, rounds, one_round)

        @block.scalar
        def _(act):
            def one_round(i):
                for s in range(S):
                    wait(act, turned[s], 2 * i + 1)
                    act.copy(srcT[s][:], bank[s][0][:]).then_inc(copied[s], 1)
                    wait(act, turned[s], 2 * i + 2)
                    act.copy(ownT[s][:], bank[s][1][:]).then_inc(copied[s], 1)
                for s in range(S):
                    wait(act, hidden[s], i + 1)
                    act.activation(h[s][:], bank[s][2][:], ACT.Relu, bias=W.b1_msg[:, 0:1]).then_inc(relued[s], 1)
                for s in range(S):
                    wait(act, residual[s], i + 1)
                    norm.square(act, s, tiles(y[s][:]))

            each_round(act, rounds, one_round)

        @block.vector
        def _(dve):
            norm.set_eps(dve, began)
            dve.memset(mx[S - 1][:], 0.0).then_inc(began, 1)
            dve.wait_ge(began, S + 1)
            def one_round(i):
                for s in range(S):
                    wait(dve, made[s], i + 1)
                    wait(dve, scanned[s - 1], i + 1 if s else i)
                    dve.tensor_tensor_scan(mx[s][:], pos(Ed.low, i * S + s), bank[s][0][:], mx[s - 1][:, GROUP - 1:],
                                           ALU.add, ALU.max).then_inc(scanned[s], 1)
                for s in range(S):
                    wait(dve, loaded[s], 32 * i + 32)
                    wait(dve, out_made[s], i + 1)
                    dve.tensor_tensor(y[s][:], bank[s][3][:], own[s][:], ALU.add).then_inc(residual[s], 1)
                for s in range(S):
                    norm.sums(dve, i, s, 0)
                for s in range(S):
                    wait(dve, residual[s], i + 1)
                    wait(dve, stored[s], i * 16 * TPG)
                    norm.scale(dve, i, s, 0, x4[s][:], y[s][:])

            each_round(dve, rounds, one_round)

def build(nc, A, out, nodes, edges):
    plan = Plan(nodes, edges)
    EG, R, EP = plan.EG, plan.R, plan.EP
    D = {"out": out}
    for k in (1, 2, 3):
        D[f"x{k}"] = nc.dram_tensor(f"table_x{k}", (R + EP, P), F32, kind="Internal").ap()
    for n, shape, dt in (
        ("node_row", (P * plan.C, 2), F32), ("keep", (EG, GROUP), BF16), ("low", (EG, GROUP), BF16),
        ("count", (EG, GROUP), F32), ("wsum", (EG, GROUP), F32), ("rcount", (EG, GROUP), F32),
        ("top_val1", (P * TOP, 1), F32), ("top_node", (P * TOP, 1), I32), ("top_val2", (16 * TOP, 1), F32),
        ("top_place", (16 * TOP, 1), I32), ("top_val3", (TOP, 1), F32), ("top_place3", (TOP, 1), I32),
    ):
        D[n] = nc.dram_tensor("scratch_" + n, shape, dt, kind="Internal").ap()
    W = Weights(nc)
    with nc.cleanup_on_exit():
        fold_weights(nc, A, W)
    with nc.cleanup_on_exit():
        mem = Mem(nc)
        score, weight = mem.sb("score", [P, max(plan.C, TOP)]), mem.sb("gru_weight", [P, P])
        with nc.cleanup_on_exit():
            scores(nc, A, D, W, plan, score)
        with nc.cleanup_on_exit():
            top_nodes(nc, A, D, W, plan, score, weight)
    with nc.cleanup_on_exit():
        dense_pass(nc, A, D, W, plan)
    Ed = EdgeData(nc, plan)
    with nc.cleanup_on_exit():
        scan_rows(nc, A, D, W, plan)
    with nc.cleanup_on_exit():
        edge_tables(nc, A, D, W, Ed, plan)
    for layer in (gcn_edges, pna_edges, attention_edges, message_edges):
        with nc.cleanup_on_exit():
            layer(nc, A, D, W, Ed, plan)


def laid_out(inputs):
    import numpy as np

    a = {k: np.asarray(v) for k, v in inputs.items()}
    nodes, edges = a["x"].shape[0], a["src"].shape[0]
    plan = Plan(nodes, edges)

    def by_row(v, fill, shift=0):
        flat = np.full(plan.EP + 2, fill, v.dtype)
        flat[1:edges + 1] = v
        if shift < 0:
            flat[0] = -1
        return np.ascontiguousarray(flat[1 + shift:1 + shift + plan.EP].reshape(plan.EG, GROUP))

    def by_tile(v):
        return np.ascontiguousarray(v.reshape(plan.EG, P, TPG).transpose(1, 0, 2).reshape(P, plan.ET))

    col = lambda n: a[n].reshape(P, 1)
    row = lambda n: a[n].reshape(1, -1)
    T = np.ascontiguousarray
    out = {
        "x": a["x"],
        "dst_row": by_row(a["dst"], nodes), "prev_row": by_row(a["dst"], nodes, -1), "w_row": by_row(a["edge_weight"], 0),
        "type_row": by_row(a["edge_type_8"], 0),
        "dst_tok": by_tile(by_row(a["dst"], nodes)), "next_tok": by_tile(by_row(a["dst"], nodes, 1)),
        "dst0_tok": by_tile(by_row(a["dst"], 0)), "src_tok": by_tile(by_row(a["src"], 0)),
        "w_tok": by_tile(by_row(a["edge_weight"], 0)),
        "L0_p": row("L0_gnn_p"), "L0_w_ihT": T(a["L0_gnn_w_ih"].T), "L0_w_hhT": T(a["L0_gnn_w_hh"].T),
        "L0_b_ih": row("L0_gnn_b_ih"), "L0_b_hh": row("L0_gnn_b_hh"), "L0_W0": a["L0_gnn_W0"], "L0_W0T": T(a["L0_gnn_W0"].T),
        "L1_W_post": a["L1_gnn_W_post"], "L1_W_linT": T(a["L1_gnn_W_lin"].T),
        "L1_W_pre_dst": T(a["L1_gnn_W_pre"][:, :P]), "L1_W_pre_srcT": T(a["L1_gnn_W_pre"][:, P:].T),
        "L2_Wq": a["L2_gnn_Wq"], "L2_Wk": a["L2_gnn_Wk"], "L2_Wv": a["L2_gnn_Wv"], "L2_Wo": a["L2_gnn_Wo"],
        "L2_W1": a["L2_gnn_W1"], "L2_W2": a["L2_gnn_W2"], "L2_edge_bias": a["L2_gnn_edge_bias"],
        "L2_g2": row("L2_gnn_g2"), "L2_be2": row("L2_gnn_be2"), "L2_bo": row("L2_gnn_bo"),
        "L3_Ws": T(a["L3_gnn_Wm"][P:2 * P]), "L3_WdT": T(a["L3_gnn_Wm"][:P].T), "L3_ww": T(a["L3_gnn_Wm"][2 * P:]),
        "L3_W1": a["L3_gnn_W1"], "L3_W2": a["L3_gnn_W2"],
        "columns": np.concatenate([col(n) for n in (
            "L2_gnn_g1", "L2_gnn_be1", "L2_gnn_b1", "L2_gnn_bq", "L2_gnn_bk", "L2_gnn_bv", "L3_gnn_b1", "L3_gnn_bm",
            "L1_gnn_b_post", "L1_gnn_b_pre")], axis=1),
        "rows": np.concatenate([row(n) for n in (
            "L2_gnn_be1", "L2_gnn_b2", "L3_gnn_b2", "L1_gnn_b_lin", "L2_gnn_bo")], axis=0),
    }
    return out, nodes, edges


def kernel(**inputs):
    import numpy as np
    import concourse.bacc as bacc
    from concourse.bass_utils import run_bass_kernel_spmd

    arrays, nodes, edges = laid_out(inputs)
    nc = bacc.Bacc("TRN2", target_bir_lowering=False, num_devices=1)
    A, fed = {}, {}
    for name, v in arrays.items():
        fed["in_" + name] = v
        A[name] = nc.dram_tensor("in_" + name, v.shape, mybir.dt.from_np(v.dtype), kind="ExternalInput").ap()
    out = nc.dram_tensor("out_rows", (nodes, P), F32, kind="ExternalOutput").ap()
    build(nc, A, out, nodes, edges)
    r = run_bass_kernel_spmd(nc, [fed], core_ids=[0])
    return r.results[0]["out_rows"]
```

```python
from contextlib import ExitStack

import concourse.bass as bass
from concourse import mybir

F32 = mybir.dt.float32
BF16 = mybir.dt.bfloat16
I32 = mybir.dt.int32
U32 = mybir.dt.uint32
ALU = mybir.AluOpType
ACT = mybir.ActivationFunctionType
AX = mybir.AxisListType.X

P = 128
TPG = 4
GROUP = P * TPG
TOP = 128
HEADS = 8
TYPES = 8
LOW = -3.0e38
EPS = 1e-5
ROOT = float(P) ** -0.5


def ceil_to(n, m):
    return (n + m - 1) // m * m


class Plan:

    def __init__(self, nodes, edges):
        self.N, self.E = nodes, edges
        self.DS, self.ES = 4, 2
        self.EG = ceil_to((edges + GROUP - 1) // GROUP, self.ES)
        self.EP = self.EG * GROUP
        self.ET = self.EG * TPG
        self.NF = nodes // GROUP
        self.DG = ceil_to((nodes + GROUP - 1) // GROUP, self.DS)
        self.R = self.DG * GROUP
        self.EARLY = self.EG // 6 * 2
        self.LOOKUPS = ceil_to(self.EG, self.DG // self.DS) // (self.DG // self.DS) * TPG
        self.LT = self.LOOKUPS * (self.DG // self.DS)
        self.C = (nodes + P - 1) // P
        self.LAST = nodes - (P - 1) * self.C
        assert 0 < self.LAST <= self.C and (nodes - self.NF * GROUP) % TPG == 0


def tiles(ap):
    return ap.rearrange("p (t f) -> p t f", t=TPG)


def over(ap, n):
    return ap.unsqueeze(2).to_broadcast([ap.shape[0], ap.shape[1], n])


def each(ap, n):
    return ap.unsqueeze(1).to_broadcast([ap.shape[0], n, ap.shape[1]])



def wait(eng, sem, count):
    if not (isinstance(count, int) and count == 0):
        eng.wait_ge(sem, count)


def each_round(eng, rounds, one_round):
    one_round(0)
    if rounds > 1:
        with eng.Fori(1, rounds) as i:
            one_round(i)


def in_turns(eng, rounds, lag, steps, step, tail=0):
    def one_round(i, begins=True, ends=True):
        for t in range(steps):
            for s, late in enumerate(lag):
                if t >= late:
                    if begins:
                        step(t - late, s, i)
                elif ends:
                    step(t - late + steps, s, i - 1)

    one_round(0, ends=False)
    if rounds > 1:
        one_round(1)
    if rounds - tail > 2:
        with eng.Fori(2, rounds - tail) as i:
            one_round(i)
    for i in range(max(2, rounds - tail), rounds):
        one_round(i)
    one_round(rounds, begins=False)


class Mem:

    def __init__(self, nc):
        self.nc = nc
        self.gate = None

    def settle(self, eng):
        if self.gate is None:
            self.gate = self.sem(f"settled_{eng.engine.name}_{self.nc.next_id()}")
        eng.sem_inc(self.gate, 1)

    def sb(self, name, shape, dt=F32):
        return self.nc.alloc_sbuf_tensor(name, shape, dt)

    def ps(self, name):
        return self.nc.alloc_psum_tensor(name, [P, 512], F32)

    def sem(self, name):
        return self.nc.alloc_semaphore(name)

    def sems(self, name, n):
        return [self.sem(f"{name}{k}") for k in range(n)]


class Norm:

    def __init__(self, mem, name, S, per, squares=True, stats=False):
        self.per, self.mem = per, mem
        if squares:
            self.sq = [mem.sb(f"{name}_sq{s}", [P, TPG, P + 1]) for s in range(S)]
            self.squared = mem.sems(name + "_squared", S)
        if stats:
            self.st = [mem.sb(f"{name}_st{s}", [P, TPG, 6]) for s in range(S)]
            self.mv = [mem.sb(f"{name}_mv{s}", [P, TPG, 2]) for s in range(S)]
            self.stats_made = mem.sems(name + "_stats_made", S)
        self.var = [mem.sb(f"{name}_var{s}", [P, TPG]) for s in range(S)]
        self.rstd = [mem.sb(f"{name}_rstd{s}", [P, TPG]) for s in range(S)]
        self.summed = mem.sems(name + "_summed", S)
        self.rooted = mem.sems(name + "_rooted", S)
        self.normed = mem.sems(name + "_normed", S)

    def nth(self, i, j):
        return i * self.per + j + 1

    def set_eps(self, dve, began):
        for sq in self.sq:
            dve.memset(sq[:, :, P:P + 1], EPS).then_inc(began, 1)

    def square(self, act, s, y):
        act.activation(self.sq[s][:, :, 0:P], y, ACT.Square, scale=ROOT).then_inc(self.squared[s], 1)

    def sums(self, dve, i, s, j):
        wait(dve, self.squared[s], self.nth(i, j))
        dve.tensor_reduce(self.var[s][:], self.sq[s][:], AX, ALU.add).then_inc(self.summed[s], 1)

    def moments(self, dve, i, s, y):
        for t in range(TPG):
            dve.bn_stats(self.st[s][:, t, :], y[:, t * P:(t + 1) * P]).then_inc(self.stats_made[s], 1)
        wait(dve, self.stats_made[s], i * 2 * TPG + TPG)
        self.mem.settle(dve)
        for t in range(TPG):
            dve.bn_aggr(self.mv[s][:, t, :], self.st[s][:, t, :]).then_inc(self.stats_made[s], 1)
        wait(dve, self.stats_made[s], i * 2 * TPG + 2 * TPG)
        dve.tensor_scalar(self.var[s][:], self.mv[s][:, :, 1], EPS, None, ALU.add).then_inc(self.summed[s], 1)

    def root(self, pool, i, s, j, minus_half):
        wait(pool, self.summed[s], self.nth(i, j))
        pool.tensor_tensor(self.rstd[s][:], self.var[s][:], minus_half[:], ALU.pow).then_inc(self.rooted[s], 1)

    def scale(self, dve, i, s, j, out, y):
        wait(dve, self.rooted[s], self.nth(i, j))
        dve.tensor_tensor(tiles(out), tiles(y), over(self.rstd[s][:], P), ALU.mult).then_inc(self.normed[s], 1)

    def scale_moments(self, dve, i, s, j, out, y):
        wait(dve, self.rooted[s], self.nth(i, j))
        for t in range(TPG):
            c = slice(t * P, (t + 1) * P)
            ins = dve.tensor_scalar(out[:, c], y[:, c], self.mv[s][:, t, 0:1], self.rstd[s][:, t:t + 1],
                                    ALU.subtract, ALU.mult)
        ins.then_inc(self.normed[s], 1)


def transpose_tiles(pe, out, rows, ident):
    for t in range(TPG):
        mm = pe.transpose(out[:, t:GROUP:TPG], rows[:, t * P:(t + 1) * P], ident[:])
    return mm


def rows_matmul(pe, out, cols, w, start=False, stop=False):
    for t in range(TPG):
        mm = pe.matmul(out[:, t * P:(t + 1) * P], cols[:, t:GROUP:TPG], w,
                       start=start, stop=stop, skip_group_check=True)
    return mm


def const_rows(pe, out, W, c):
    pe.matmul(out[:], W.ones3[:], W.const[:, c, :, :], start=True, stop=False, skip_group_check=True)


def groups_of(ap):
    return ap.rearrange("(g p t) f -> g p (t f)", p=P, t=TPG)


class Weights:

    def __init__(self, nc):
        mem = Mem(nc)
        square = lambda name: mem.sb("w_" + name, [P, P])
        self.ident = square("ident")
        self.heads = square("heads")
        self.ones = square("ones")
        self.pna_src = square("pna_src")
        self.pna_dense = square("pna_dense")
        self.wq = square("wq")
        self.wk = square("wk")
        self.wv = square("wv")
        self.wo = square("wo")
        self.g1c = square("g1c")
        self.w1_ffn = square("w1_ffn")
        self.w2_ffn = square("w2_ffn")
        self.w1a = square("w1a")
        self.w1a_edge = square("w1a_edge")
        self.w1b = square("w1b")
        self.w2_msg = square("w2_msg")
        self.msg_src = square("msg_src")
        self.g2 = square("g2")
        self.be2 = square("be2")
        self.bo = square("bo")
        self.gru = square("gru")
        self.gru_dense = square("gru_dense")
        self.post = mem.sb("w_post", [P, 13, P])
        self.own = mem.sb("w_own", [P, 3, P])
        self.head_bias = mem.sb("w_head_bias", [3 * TYPES, P], BF16)
        self.split = mem.sb("w_split", [3 * TYPES, 4])
        self.msg_w = mem.sb("w_msg_w", [1, P])
        self.const = mem.sb("w_const", [3, C_ROWS, TPG, P], BF16)
        self.ones3 = mem.sb("w_ones3", [3, P], BF16)
        self.minus_half = mem.sb("w_minus_half", [P, TPG])
        self.cols = mem.sb("w_cols", [P, 16])
        self.b1_ffn = mem.sb("w_b1_ffn", [P, 1])
        self.b1_msg = mem.sb("w_b1_msg", [P, 1])


G1, BE1, B1_FFN, BQ, BK, BV, B1_MSG, BM, B_POST, B_PRE = range(10)
C_FFN, C_MSG, C_WO, C_PNA_DENSE, C_PNA = range(5)
C_ROWS = C_PNA + 3
R_BE1, R_B2_FFN, R_B2_MSG, R_B_LIN, R_BO, R_MADE = range(6)


def fold_weights(nc, A, W):
    mem = Mem(nc)
    raw_post = mem.sb("f_post", [P, 13 * P])
    raw = {n: mem.sb("f_" + n, [P, P]) for n in ("linT", "pre", "w1", "w2", "wo", "w1b", "w2m", "wdT")}
    bias8 = mem.sb("f_bias8", [3 * TYPES, HEADS])
    bias_wide = mem.sb("f_bias_wide", [3 * TYPES, P])
    crow = mem.sb("f_crow", [1, C_ROWS * P])
    crow3 = mem.sb("f_crow3", [3, C_ROWS * P])
    part3 = [mem.sb(f"f_part{k}", [3 * TYPES, C_ROWS * P], BF16) for k in range(4)]
    rows = mem.sb("f_rows", [1, 6, P])
    row = mem.sb("f_row", [1, P])
    sums = mem.sb("f_sums", [P, 1])
    csum = mem.sb("f_csum", [P, P])
    tmp = mem.sb("f_tmp", [P, P])
    bank = [mem.ps(f"f_bank{k}") for k in range(8)]
    loaded, made, step = mem.sem("f_loaded"), mem.sem("f_pool_made"), mem.sem("f_vector_step")
    linT_centred, block_made, block_copied = mem.sem("f_linT_centred"), mem.sem("f_block_made"), mem.sem("f_block_copied")
    csum_made, own_made = mem.sem("f_csum_made"), mem.sem("f_own_made")
    rows_done, thrice_made = mem.sem("f_rows_done"), mem.sem("f_thrice_made")
    std_made, last_made = mem.sem("f_std_weight"), mem.sem("f_last_products")
    loads = [
        (raw_post[:], A["L1_W_post"]), (raw["linT"][:], A["L1_W_linT"]), (raw["pre"][:], A["L1_W_pre_dst"]),
        (raw["w1"][:], A["L2_W1"]), (raw["w2"][:], A["L2_W2"]), (raw["wo"][:], A["L2_Wo"]),
        (raw["w1b"][:], A["L3_W1"][P:2 * P, :]), (raw["w2m"][:], A["L3_W2"]), (raw["wdT"][:], A["L3_WdT"]),
        (W.pna_src[:], A["L1_W_pre_srcT"]), (W.wq[:], A["L2_Wq"]),
        (W.wk[:], A["L2_Wk"]), (W.wv[:], A["L2_Wv"]), (W.msg_src[:], A["L3_Ws"]),
        (W.w1a[:], A["L3_W1"][0:P, :]), (W.w1b[:], A["L3_W1"][P:2 * P, :]), (W.msg_w[:], A["L3_ww"]),
        (W.g2[:], A["L2_g2"].to_broadcast([P, P])), (W.be2[:], A["L2_be2"].to_broadcast([P, P])),
        (W.bo[:], A["L2_bo"].to_broadcast([P, P])), (W.cols[:, 0:10], A["columns"]),
    ] + [(rows[0:1, k, :], A["rows"][k:k + 1, :]) for k in range(5)]
    loads += [(bias8[k * TYPES:(k + 1) * TYPES, :], A["L2_edge_bias"]) for k in range(3)] + [(W.split[:], A["split"])]
    cols = W.cols

    with nc.Block() as block:
        @block.sync
        def _(sp):
            for out, src in loads:
                sp.dma_start(out, src).then_inc(loaded, 16)

        @block.gpsimd
        def _(pool):
            heads = W.heads[:].rearrange("p (h d) -> p h d", h=HEADS)
            depth = P // HEADS
            pool.memset(W.ident[:], 1.0).then_inc(made, 1)
            pool.memset(W.heads[:], float(depth) ** -0.5).then_inc(made, 1)
            pool.memset(W.minus_half[:], -0.5).then_inc(made, 1)
            pool.memset(W.ones[:], 1.0).then_inc(made, 1)
            pool.memset(W.ones3[:], 1.0).then_inc(made, 1)
            pool.wait_ge(made, 5)
            pool.affine_select(out=W.ident[:], in_=W.ident[:], compare_op=ALU.is_equal, fill=0.0,
                               base=0, pattern=[[1, P]], channel_multiplier=-1).then_inc(made, 1)
            pool.affine_select(out=heads, in_=heads, compare_op=ALU.is_ge, fill=0.0, base=0,
                               pattern=[[-depth, HEADS], [0, depth]], channel_multiplier=1).then_inc(made, 1)
            pool.wait_ge(made, 7)
            pool.affine_select(out=heads, in_=heads, compare_op=ALU.is_ge, fill=0.0, base=depth - 1,
                               pattern=[[depth, HEADS], [0, depth]], channel_multiplier=-1).then_inc(made, 1)

        @block.vector
        def _(dve):
            steps = [0]

            def then(ins):
                ins.then_inc(step, 1)
                steps[0] += 1
                dve.wait_ge(step, steps[0])

            def centre(out, src):
                mean = sums[0:src.shape[0], :]
                then(dve.tensor_reduce(mean, src, AX, ALU.add))
                then(dve.tensor_scalar(mean, mean, -1.0 / P, None, ALU.mult))
                then(dve.tensor_scalar(out, src, mean, None, ALU.add))

            def constant(c, r):
                then(dve.tensor_copy(crow[:, c * P:(c + 1) * P], r))

            def split(out, x, member):
                n, m = x.shape
                high, middle, low, sum_ = (part3[k][0:n, 0:m] for k in range(4))
                then(dve.tensor_copy(high, x))
                then(dve.tensor_tensor(x, x, high, ALU.subtract))
                then(dve.tensor_copy(middle, x))
                then(dve.tensor_tensor(x, x, middle, ALU.subtract))
                then(dve.tensor_copy(low, x))
                then(dve.tensor_scalar(sum_, high, member[0], None, ALU.mult))
                then(dve.scalar_tensor_tensor(sum_, middle, member[1], sum_, ALU.mult, ALU.add))
                then(dve.scalar_tensor_tensor(sum_, low, member[2], sum_, ALU.mult, ALU.add))
                then(dve.tensor_copy(out, sum_.rearrange("p (c f) -> p c f", f=P).unsqueeze(2).to_broadcast([n, m // P, TPG, P])
                                     if m > P else sum_))

            dve.wait_ge(loaded, 16 * len(loads))
            dve.wait_ge(made, 8)
            centre(raw["linT"][:], raw["linT"][:])
            dve.tensor_copy(row[:], rows[0:1, R_BO, :]).then_inc(linT_centred, 1)
            dve.wait_ge(linT_centred, 1)
            centre(row[:], row[:])
            constant(C_WO, row[:])
            centre(W.w2_ffn[:], raw["w2"][:])
            centre(W.w2_msg[:], raw["w2m"][:])
            centre(W.wo[:], raw["wo"][:])
            centre(W.bo[:], W.bo[:])
            then(dve.tensor_scalar(W.g1c[:], W.ident[:], cols[:, G1:G1 + 1], None, ALU.mult))
            centre(W.g1c[:], W.g1c[:])
            then(dve.tensor_scalar(W.w1_ffn[:], raw["w1"][:], cols[:, G1:G1 + 1], None, ALU.mult))
            then(dve.tensor_tensor(row[:], rows[0:1, R_BE1, :], rows[0:1, R_B2_FFN, :], ALU.add))
            centre(row[:], row[:])
            constant(C_FFN, row[:])
            centre(row[:], rows[0:1, R_B2_MSG, :])
            constant(C_MSG, row[:])
            then(dve.tensor_copy(bias_wide[:].rearrange("p (h d) -> p h d", h=HEADS), over(bias8[:], P // HEADS)))
            split(W.head_bias[:], bias_wide[:], [W.split[:, k + 1:k + 2] for k in range(3)])

            for b in range(13):
                dve.wait_ge(block_made, b + 1)
                dve.tensor_copy(W.post[:, b, :], bank[b % 4][:, 0:P]).then_inc(block_copied, 1)
            dve.wait_ge(block_copied, 13)
            for k in range(3):
                mx, mn, mean = (W.post[:, 1 + 4 * k + n, :] for n in range(3))
                then(dve.tensor_tensor(csum[:], mx, mn, ALU.add))
                dve.tensor_tensor(csum[:], csum[:], mean, ALU.add).then_inc(csum_made, 1)
                then(dve.tensor_scalar(mn, mn, -1.0, None, ALU.mult))
                dve.wait_ge(own_made, k + 1)
                then(dve.tensor_copy(W.own[:, k, :], bank[4][:, 0:P]))
                then(dve.tensor_copy(row[:], bank[5][0:1, 0:P]))
                if k == 0:
                    centre(rows[0:1, R_B_LIN, :], rows[0:1, R_B_LIN, :])
                    then(dve.tensor_tensor(rows[0:1, R_B_LIN, :], rows[0:1, R_B_LIN, :], bank[5][0:1, P:2 * P], ALU.add))
                    then(dve.tensor_tensor(row[:], row[:], rows[0:1, R_B_LIN, :], ALU.add))
                constant(C_PNA + k, row[:])
            then(dve.tensor_scalar(tmp[:], W.ident[:], -1.0 / P, None, ALU.add))
            then(dve.tensor_tensor(W.pna_dense[:], W.post[:, 0, :], tmp[:], ALU.add))
            then(dve.tensor_tensor(W.own[:, 0, :], W.own[:, 0, :], W.pna_dense[:], ALU.add))
            ln2 = 0.6931471805599453
            then(dve.scalar_tensor_tensor(tmp[:], W.post[:, 8, :], ln2, W.post[:, 4, :], ALU.mult, ALU.add))
            then(dve.scalar_tensor_tensor(tmp[:], W.post[:, 12, :], 1.0 / ln2, tmp[:], ALU.mult, ALU.add))
            dve.tensor_scalar(tmp[:], tmp[:], EPS ** 0.5, None, ALU.mult).then_inc(std_made, 1)
            dve.wait_ge(last_made, 1)
            then(dve.tensor_tensor(row[:], rows[0:1, R_B_LIN, :], bank[6][0:1, 0:P], ALU.add))
            constant(C_PNA_DENSE, row[:])
            dve.tensor_tensor(W.b1_ffn[:], cols[:, B1_FFN:B1_FFN + 1], bank[7][:, 0:1], ALU.add)
            dve.tensor_tensor(W.b1_msg[:], cols[:, B1_MSG:B1_MSG + 1], bank[7][:, 1:2], ALU.add)
            dve.tensor_tensor(W.w1a_edge[:], W.w1a[:], bank[7][:, P:2 * P], ALU.add).then_inc(rows_done, 1)
            dve.wait_ge(thrice_made, 1)
            then(dve.tensor_copy(crow3[:, 0:GROUP], bank[0][0:3, :]))
            then(dve.tensor_copy(crow3[:, GROUP:], bank[1][0:3, 0:C_ROWS * P - GROUP]))
            split(W.const[:], crow3[:], [W.ident[0:3, k:k + 1] for k in range(3)])

        @block.tensor
        def _(pe):
            pe.wait_ge(loaded, 16 * len(loads))
            pe.wait_ge(made, 8)
            pe.wait_ge(linT_centred, 1)
            for b in range(13):
                if b >= 4:
                    pe.wait_ge(block_copied, b - 3)
                pe.matmul(bank[b % 4][:, 0:P], raw_post[:, b * P:(b + 1) * P], raw["linT"][:],
                          start=True, stop=True).then_inc(block_made, 1)
            pe.matmul(bank[5][0:1, P:2 * P], cols[:, B_POST:B_POST + 1], raw["linT"][:], start=True, stop=True)
            for k in range(3):
                pe.wait_ge(csum_made, k + 1)
                pe.matmul(bank[5][0:1, 0:P], cols[:, B_PRE:B_PRE + 1], csum[:], start=True, stop=True)
                pe.matmul(bank[4][:, 0:P], raw["pre"][:], csum[:], start=True, stop=True).then_inc(own_made, 1)
            pe.wait_ge(std_made, 1)
            pe.matmul(bank[6][0:1, 0:P], W.ones[:, 0:1], tmp[:], start=True, stop=True)
            pe.matmul(bank[7][:, 0:1], raw["w1"][:], cols[:, BE1:BE1 + 1], start=True, stop=True)
            pe.matmul(bank[7][:, 1:2], raw["w1b"][:], cols[:, BM:BM + 1], start=True, stop=True)
            pe.matmul(bank[7][:, P:2 * P], raw["wdT"][:], raw["w1b"][:], start=True, stop=True).then_inc(last_made, 1)
            pe.wait_ge(rows_done, 1)
            pe.matmul(bank[0][0:3, :], W.ones[0:1, 0:3], crow[:, 0:GROUP], start=True, stop=True)
            pe.matmul(bank[1][0:3, 0:C_ROWS * P - GROUP], W.ones[0:1, 0:3], crow[:, GROUP:], start=True, stop=True).then_inc(thrice_made, 1)


class EdgeData:

    def __init__(self, nc, plan):
        mem = Mem(nc)
        self.src0 = mem.sb("e_src0", [P, plan.LT], I32)
        self.src = mem.sb("e_src", [P, plan.LT], I32)
        self.coef = mem.sb("e_coef", [P, plan.LT])
        self.dst0 = mem.sb("e_dst0", [P, plan.ET], I32)
        self.dst = mem.sb("e_dst", [P, plan.ET], I32)
        self.out = mem.sb("e_out", [P, plan.ET], I32)
        self.dinv = mem.sb("e_dinv", [P, plan.ET])
        self.amp = mem.sb("e_amp", [P, plan.ET])
        self.att = mem.sb("e_att", [P, plan.ET])

    def add_masks(self, nc, plan):
        mem = Mem(nc)
        self.keep = mem.sb("e_keep", [P, plan.EP], BF16)
        self.low = mem.sb("e_low", [P, plan.EP], BF16)


class OwnRows:

    def __init__(self, nc, plan):
        mem = Mem(nc)
        self.own = mem.sb("o_own", [P, plan.ET, 2])
        self.deg = mem.sb("o_deg", [P, plan.ET])
        self.half = mem.sb("o_half", [P, plan.ET])

    def root(self, mem, pool, Ed):
        rooted = mem.sem("o_rooted")
        pool.tensor_tensor(Ed.dinv[:], self.deg[:], self.half[:], ALU.pow).then_inc(rooted, 1)
        pool.wait_ge(rooted, 1)
        pool.tensor_copy(self.own[:, :, 1], Ed.dinv[:]).then_inc(rooted, 1)
        pool.wait_ge(rooted, 2)

    def scatter(self, mem, pool, D, Ed, plan, first, last):
        slot = [mem.sb(f"o_slot{u}_{first}", [P, TPG], I32) for u in range(2)]
        send = [mem.sb(f"o_send{u}_{first}", [P, TPG, 2]) for u in range(2)]
        slotted, moved = mem.sems(f"o_slotted_{first}_", 2), mem.sems(f"o_moved_{first}_", 2)

        def one_round(i):
            for u in range(2):
                at = bass.ds((i * 2 + u + first) * TPG, TPG)
                wait(pool, moved[u], i * 16 * TPG)
                pool.tensor_copy(slot[u][:], Ed.out[:, at]).then_inc(slotted[u], 1)
                pool.tensor_copy(send[u][:], self.own[:, at, :]).then_inc(slotted[u], 1)
            for u in range(2):
                wait(pool, slotted[u], i * 2 + 2)
                mem.settle(pool)
                for t in range(TPG):
                    pool.indirect_dma_start(
                        out=D["node_row"], out_offset=bass.IndirectOffsetOnAxis(ap=slot[u][:, t:t + 1], axis=0),
                        in_=send[u][:, t, :], in_offset=None, bounds_check=plan.N - 1, oob_is_err=False,
                    ).then_inc(moved[u], 16)

        rounds = (last - first) // 2
        if rounds:
            each_round(pool, rounds, one_round)
            for u in range(2):
                pool.wait_ge(moved[u], rounds * 16 * TPG)


class Lookup:

    def __init__(self, mem, name, node, table, n):
        self.mem, self.node, self.table, self.n = mem, node, table, n
        self.slot = mem.sb(name + "_slot", [P, n], I32)
        self.got = mem.sb(name + "_got", [P, n, 2])
        self.taken, self.fetched = mem.sem(name + "_taken"), mem.sem(name + "_fetched")

    def begin(self, pool, i, first, steps):
        pool.tensor_copy(self.slot[:], self.node[:, bass.ds(first, self.n)]).then_inc(self.taken, 1)
        wait(pool, self.taken, i * steps + 1)
        self.mem.settle(pool)

    def fetch(self, pool, t):
        pool.indirect_dma_start(out=self.got[:, t, :], out_offset=None, in_=self.table,
                                in_offset=bass.IndirectOffsetOnAxis(ap=self.slot[:, t:t + 1], axis=0)).then_inc(self.fetched, 16)

    def take(self, pool, i, first, row, factor=None):
        at = bass.ds(first, self.n)
        wait(pool, self.fetched, (i + 1) * 16 * self.n)
        pool.tensor_copy(row[:, at], self.got[:, :, 0]).then_inc(self.taken, 1)
        if factor is not None:
            pool.tensor_tensor(factor[:, at], factor[:, at], self.got[:, :, 1], ALU.mult).then_inc(self.taken, 1)


def scan_rows(nc, A, D, W, plan):
    EG = plan.EG
    mem = Mem(nc)
    dst, prev = mem.sb("r_dst", [EG, GROUP], I32), mem.sb("r_prev", [EG, GROUP], I32)
    wt = mem.sb("r_wt", [EG, GROUP])
    keep, low = mem.sb("r_keep", [EG, GROUP], BF16), mem.sb("r_low", [EG, GROUP], BF16)
    ones, zeros = mem.sb("r_ones", [EG, GROUP]), mem.sb("r_zeros", [EG, GROUP])
    whole = mem.sb("r_whole", [EG, GROUP])
    part = [mem.sb(f"r_part{k}", [EG, GROUP]) for k in range(2)]
    inv = mem.sb("r_inv", [EG, GROUP])
    line = mem.sb("r_line", [1, 3, EG])
    carry = mem.sb("r_carry", [1, 2, EG + 1])
    enter = mem.sb("r_enter", [EG, 2])
    turned, back = mem.ps("r_turned"), mem.ps("r_back")
    loaded, step, stored = mem.sem("r_loaded"), mem.sem("r_vector_step"), mem.sem("r_stored")
    ends, lined, carried, entered, full = (mem.sem("r_" + n) for n in ("ends", "lined", "carried", "entered", "full"))

    with nc.Block() as block:
        @block.sync
        def _(sp):
            sp.dma_start(dst[:], A["dst_row"]).then_inc(loaded, 16)
            sp.dma_start(prev[:], A["prev_row"]).then_inc(loaded, 16)
            sp.dma_start(wt[:], A["w_row"]).then_inc(loaded, 16)
            sp.wait_ge(full, 1)
            sp.dma_start(D["keep"], keep[:]).then_inc(stored, 16)
            sp.dma_start(D["low"], low[:]).then_inc(stored, 16)
            sp.dma_start(D["count"], part[0][:]).then_inc(stored, 16)
            sp.dma_start(D["wsum"], part[1][:]).then_inc(stored, 16)
            sp.dma_start(D["rcount"], inv[:]).then_inc(stored, 16)
            sp.wait_ge(stored, 80)

        @block.vector
        def _(dve):
            steps = [0]

            def then(ins):
                ins.then_inc(step, 1)
                steps[0] += 1
                dve.wait_ge(step, steps[0])

            then(dve.memset(ones[:], 1.0))
            then(dve.memset(zeros[:], 0.0))
            then(dve.memset(carry[:], 0.0))
            dve.wait_ge(loaded, 48)
            then(dve.tensor_tensor(keep[:], dst[:], prev[:], ALU.is_equal))
            then(dve.tensor_scalar(low[:], keep[:], -1.0, -LOW, ALU.add, ALU.mult))
            then(dve.tensor_tensor_scan(part[0][:], keep[:], ones[:], 0.0, ALU.mult, ALU.add))
            then(dve.tensor_tensor_scan(part[1][:], keep[:], wt[:], 0.0, ALU.mult, ALU.add))
            dve.tensor_tensor_scan(whole[:], keep[:], zeros[:], 1.0, ALU.mult, ALU.add).then_inc(ends, 1)
            dve.wait_ge(lined, 1)
            for k in range(3):
                then(dve.tensor_copy(line[:, k, :], turned[0:1, k * P:k * P + EG]))
            then(dve.tensor_tensor_scan(carry[:, 0, 1:], line[:, 2, :], line[:, 0, :], 0.0, ALU.mult, ALU.add))
            dve.tensor_tensor_scan(carry[:, 1, 1:], line[:, 2, :], line[:, 1, :], 0.0, ALU.mult, ALU.add).then_inc(carried, 1)
            dve.wait_ge(entered, 1)
            then(dve.tensor_copy(enter[:], back[0:EG, 0:2]))
            for k in range(2):
                then(dve.scalar_tensor_tensor(part[k][:], whole[:], enter[:, k:k + 1], part[k][:], ALU.mult, ALU.add))
            dve.reciprocal(inv[:], part[0][:]).then_inc(full, 1)

        @block.tensor
        def _(pe):
            pe.wait_ge(ends, 1)
            last = slice(GROUP - 1, GROUP)
            for k, rows in enumerate((part[0], part[1], whole)):
                mm = pe.transpose(turned[0:1, k * P:k * P + EG], rows[:, last], W.ident[0:EG, 0:EG])
            mm.then_inc(lined, 1)
            pe.wait_ge(carried, 1)
            for k in range(2):
                mm = pe.matmul(back[0:EG, k:k + 1], carry[0:1, k, 0:EG], W.ones[0:1, 0:1], start=True, stop=True)
            mm.then_inc(entered, 1)


def edge_tables(nc, A, D, W, Ed, Own, plan):
    N, C, ET, EG, EP = plan.N, plan.C, plan.ET, plan.EG, plan.EP
    mem = Mem(nc)
    nxt = mem.sb("t_next", [P, ET], I32)
    dsti = mem.sb("t_dst", [P, ET], I32)
    cnt, end = mem.sb("t_cnt", [P, ET]), mem.sb("t_end", [P, ET])
    pos = mem.sb("t_pos", [P, ET], I32)
    base_i = mem.sb("t_base_i", [P, C], I32)
    base = mem.sb("t_base", [P, C, 2])
    loaded, step, stored = mem.sem("t_loaded"), mem.sem("t_vector_step"), mem.sem("t_stored")
    made, logged, tables = mem.sem("t_pool_made"), mem.sem("t_logged"), mem.sem("t_tables")
    NONE = float(1 << 22)
    LOADS = 7

    with nc.Block() as block:
        @block.sync
        def _(sp):
            tok = lambda ap: ap.rearrange("g (p t) -> p g t", t=TPG)
            flat = lambda ap: ap.rearrange("p (g t) -> p g t", t=TPG)
            for out, src in ((dsti[:], "dst_tok"), (nxt[:], "next_tok"), (Ed.coef[:, 0:ET], "w_tok"), (Ed.src0[:, 0:ET], "src_tok"),
                             (Ed.dst0[:], "dst0_tok")):
                sp.dma_start(out, A[src]).then_inc(loaded, 16)
            sp.dma_start(flat(cnt[:]), tok(D["count"])).then_inc(loaded, 16)
            sp.dma_start(flat(Own.deg[:]), tok(D["wsum"])).then_inc(loaded, 16)
            sp.wait_ge(tables, 2)
            sp.dma_start(D["node_row"].rearrange("(p c) k -> p c k", p=P), base[:]).then_inc(stored, 16)
            sp.wait_ge(loaded, 16 * LOADS)
            sp.wait_ge(stored, 16)

        @block.vector
        def _(dve):
            steps = [0]

            def then(ins):
                ins.then_inc(step, 1)
                steps[0] += 1
                dve.wait_ge(step, steps[0])

            dve.wait_ge(made, 3)
            dve.tensor_copy(base[:, :, 0], base_i[:]).then_inc(tables, 1)
            dve.memset(base[:, :, 1], 1.0).then_inc(tables, 1)
            dve.tensor_copy(Own.own[:, :, 0], pos[:])
            dve.wait_ge(loaded, 16 * LOADS)
            then(dve.tensor_scalar(Own.deg[:], Own.deg[:], 1.0, None, ALU.add))
            then(dve.tensor_tensor(end[:], dsti[:], nxt[:], ALU.not_equal))
            then(dve.tensor_scalar(end[:], end[:], -NONE, NONE, ALU.mult, ALU.add))
            then(dve.tensor_tensor(end[:], end[:], dsti[:], ALU.add))
            then(dve.tensor_copy(Ed.out[:], end[:]))
            dve.wait_ge(logged, 1)
            then(dve.reciprocal(Ed.att[:], Ed.amp[:]))

        @block.scalar
        def _(act):
            act.wait_ge(loaded, 16 * LOADS)
            act.activation(Ed.amp[:], cnt[:], ACT.Ln, bias=1.0).then_inc(logged, 1)

        @block.gpsimd
        def _(pool):
            pool.iota(pos[:].rearrange("p (g t) -> p g t", t=TPG), [[GROUP, EG], [1, TPG]], base=plan.R,
                      channel_multiplier=TPG).then_inc(made, 1)
            pool.iota(base_i[:], [[1, C]], base=0, channel_multiplier=C).then_inc(made, 1)
            pool.memset(Own.half[:], -0.5).then_inc(made, 1)
            if plan.LT > ET:
                pool.memset(Ed.src0[:, ET:], 0)
                pool.memset(Ed.coef[:, ET:], 0.0)


def scores(nc, A, D, W, Ed, Own, plan, score):
    C, LAST = plan.C, plan.LAST
    mem = Mem(nc)
    wide = (C + 7) // 8
    chunks = [(c, min(c + wide, LAST), P) for c in range(0, LAST, wide)]
    chunks += [(c, min(c + wide, C), P - 1) for c in range(LAST, C, wide)]
    BUFS = 3
    buf = [mem.sb(f"s_x{k}", [P, wide * P]) for k in range(BUFS)]
    pb = mem.sb("s_p", [P, P])
    loaded, used = mem.sems("s_loaded", BUFS), mem.sem("s_used")
    p_loaded, weighted, cleared = mem.sem("s_p_loaded"), mem.sem("s_weighted"), mem.sem("s_cleared")

    def pieces(parts):
        return [(0, parts)] if parts % 16 == 0 else [(0, parts // 16 * 16), (parts // 16 * 16, parts)]

    with nc.Block() as block:
        @block.sync
        def _(sp):
            sp.dma_start(pb[:], A["L0_p"].to_broadcast([P, P])).then_inc(p_loaded, 16)
            for n, (a, b, parts) in enumerate(chunks):
                if n >= BUFS:
                    sp.wait_ge(used, n - BUFS + 1)
                for lo, hi in pieces(parts):
                    src = bass.AP(tensor=A["x"].tensor, offset=(lo * C + a) * P,
                                  ap=[[C * P, hi - lo], [1, (b - a) * P]])
                    sp.dma_start(buf[n % BUFS][lo:hi, 0:(b - a) * P], src).then_inc(loaded[n % BUFS], 16)

        @block.gpsimd
        def _(pool):
            Own.root(mem, pool, Ed)
            Own.scatter(mem, pool, D, Ed, plan, 0, plan.EARLY)

        @block.vector
        def _(dve):
            dve.memset(score[:], LOW).then_inc(cleared, 1)
            dve.wait_ge(p_loaded, 16)
            dve.wait_ge(cleared, 1)
            total = [0] * BUFS
            for n, (a, b, parts) in enumerate(chunks):
                total[n % BUFS] += 16 * len(pieces(parts))
                dve.wait_ge(loaded[n % BUFS], total[n % BUFS])
                rows = buf[n % BUFS][0:parts, 0:(b - a) * P].rearrange("p (c f) -> p c f", f=P)
                dve.tensor_tensor(rows, rows, each(pb[0:parts, :], b - a), ALU.mult).then_inc(weighted, 1)
                dve.wait_ge(weighted, n + 1)
                dve.tensor_reduce(score[0:parts, a:b], rows, AX, ALU.add).then_inc(used, 1)


def top_nodes(nc, A, D, W, Ed, Own, plan, score, weight):
    C = plan.C
    SC = score.shape[1]
    mem = Mem(nc)
    L2R = 16
    v1, i1, n1 = mem.sb("k_v1", [P, TOP]), mem.sb("k_i1", [P, TOP], U32), mem.sb("k_n1", [P, TOP])
    n1i = mem.sb("k_n1i", [P, TOP], I32)
    basei, basef = mem.sb("k_basei", [P, 2], I32), mem.sb("k_basef", [P, 2])
    m2 = mem.sb("k_m2", [L2R, P // L2R * TOP])
    v2, i2, f2 = mem.sb("k_v2", [L2R, TOP]), mem.sb("k_i2", [L2R, TOP], U32), mem.sb("k_f2", [L2R, TOP])
    f2i = mem.sb("k_f2i", [L2R, TOP], I32)
    m3 = mem.sb("k_m3", [1, L2R * TOP])
    v3, i3 = mem.sb("k_v3", [1, TOP]), mem.sb("k_i3", [1, TOP], U32)
    ids = mem.sb("k_ids", [P, 3], I32)
    val = mem.sb("k_val", [P, 1])
    xt, pb = mem.sb("k_xt", [P, P]), mem.sb("k_pb", [P, P])
    pp, norm2, rnorm, th = mem.sb("k_pp", [P, P]), mem.sb("k_norm2", [P, 1]), mem.sb("k_rnorm", [P, 1]), mem.sb("k_th", [P, 1])
    w_ih, w_hh, w0t, w0 = mem.sb("k_w_ih", [P, 3 * P]), mem.sb("k_w_hh", [P, 3 * P]), mem.sb("k_w0t", [P, P]), mem.sb("k_w0", [P, P])
    b_ih, b_hh = mem.sb("k_b_ih", [1, 3 * P]), mem.sb("k_b_hh", [1, 3 * P])
    xtT = mem.sb("k_xtT", [P, P])
    rz, nn = mem.sb("k_rz", [P, 2 * P]), mem.sb("k_nn", [P, P])
    ssum = mem.sb("k_ssum", [P, 1])
    pt, prz, pin, phn = mem.ps("k_pt"), mem.ps("k_prz"), mem.ps("k_pin"), mem.ps("k_phn")
    step, loaded, made = mem.sem("k_step"), mem.sem("k_loaded"), mem.sem("k_made")
    l1_done, l1_stored, l2_loaded = mem.sem("k_l1_done"), mem.sem("k_l1_stored"), mem.sem("k_l2_loaded")
    l2_done, l2_stored, l3_loaded = mem.sem("k_l2_done"), mem.sem("k_l2_stored"), mem.sem("k_l3_loaded")
    l3_done, l3_stored, val_loaded = mem.sem("k_l3_done"), mem.sem("k_l3_stored"), mem.sem("k_val_loaded")
    found, rooted, tanhed = mem.sem("k_found"), mem.sem("k_rooted"), mem.sem("k_tanhed")
    normed, weighted, turned, copied, gates, opened, inner, newed = (
        mem.sem("k_" + n) for n in ("normed", "weighted", "turned", "copied", "gates", "opened", "inner", "newed"))
    row = lambda ap, p: ap.rearrange("(p c) k -> p (c k)", p=p)

    with nc.Block() as block:
        @block.sync
        def _(sp):
            for out, src in ((w_ih, A["L0_w_ihT"]), (w_hh, A["L0_w_hhT"]), (w0t, A["L0_W0T"]), (w0, A["L0_W0"]),
                             (b_ih, A["L0_b_ih"]), (b_hh, A["L0_b_hh"]), (pb, A["L0_p"].to_broadcast([P, P]))):
                sp.dma_start(out[:], src).then_inc(loaded, 16)
            sp.wait_ge(l1_done, 1)
            sp.dma_start(row(D["top_val1"], P), v1[:]).then_inc(l1_stored, 16)
            sp.dma_start(row(D["top_node"], P), n1i[:]).then_inc(l1_stored, 16)
            sp.wait_ge(l1_stored, 32)
            sp.dma_start(m2[:], row(D["top_val1"], L2R)).then_inc(l2_loaded, 16)
            sp.wait_ge(l2_done, 1)
            sp.dma_start(row(D["top_val2"], L2R), v2[:]).then_inc(l2_stored, 16)
            sp.dma_start(row(D["top_place"], L2R), f2i[:]).then_inc(l2_stored, 16)
            sp.wait_ge(l2_stored, 32)
            sp.dma_start(m3[:], row(D["top_val2"], 1)).then_inc(l3_loaded, 16)
            sp.wait_ge(l3_done, 1)
            sp.dma_start(row(D["top_val3"], 1), v3[:]).then_inc(l3_stored, 16)
            sp.dma_start(row(D["top_place3"], 1), i3[:].bitcast(I32)).then_inc(l3_stored, 16)
            sp.wait_ge(l3_stored, 32)
            sp.dma_start(val[:], D["top_val3"]).then_inc(val_loaded, 16)
            sp.dma_start(ids[:, 0:1], D["top_place3"]).then_inc(val_loaded, 16)
            sp.wait_ge(val_loaded, 32)

        @block.gpsimd
        def _(pool):
            pool.iota(basei[:], [[0, 2]], base=0, channel_multiplier=C).then_inc(made, 1)
            pool.wait_ge(made, 1)
            pool.iota(basei[0:L2R, 1:2], [[0, 1]], base=0, channel_multiplier=P // L2R * TOP).then_inc(made, 1)
            pool.wait_ge(normed, 1)
            pool.tensor_tensor(rnorm[:], norm2[:], W.minus_half[:, 0:1], ALU.pow).then_inc(rooted, 1)
            Own.scatter(mem, pool, D, Ed, plan, plan.EARLY, plan.EG)
            pool.wait_ge(val_loaded, 32)
            pool.wait_ge(l2_stored, 32)
            for k, table in enumerate(("top_place", "top_node")):
                pool.indirect_dma_start(out=ids[:, k + 1:k + 2], out_offset=None, in_=D[table],
                                        in_offset=bass.IndirectOffsetOnAxis(ap=ids[:, k:k + 1], axis=0)).then_inc(found, 16)
                pool.wait_ge(found, 16 * (k + 1))
            pool.indirect_dma_start(out=xt[:], out_offset=None, in_=A["x"],
                                    in_offset=bass.IndirectOffsetOnAxis(ap=ids[:, 2:3], axis=0)).then_inc(found, 16)
            pool.wait_ge(found, 48)

        @block.scalar
        def _(act):
            act.wait_ge(rooted, 1)
            act.wait_ge(val_loaded, 32)
            act.activation(th[:], val[:], ACT.Tanh, scale=rnorm[:, 0:1]).then_inc(tanhed, 1)
            act.wait_ge(gates, 1)
            act.activation(rz[:], prz[:, 0:2 * P], ACT.Sigmoid).then_inc(opened, 1)
            act.wait_ge(inner, 1)
            act.activation(nn[:], nn[:], ACT.Tanh).then_inc(newed, 1)

        @block.tensor
        def _(pe):
            pe.wait_ge(loaded, 16 * 7)
            pe.matmul(prz[:, 0:2 * P], w0t[:], w_hh[:, 0:2 * P], start=True, stop=False)
            pe.matmul(prz[:, 0:2 * P], W.ones[0:1, :], b_hh[0:1, 0:2 * P], start=False, stop=False)
            pe.matmul(prz[:, 0:2 * P], W.ones[0:1, :], b_ih[0:1, 0:2 * P], start=False, stop=False)
            pe.matmul(phn[:, 0:P], w0t[:], w_hh[:, 2 * P:], start=True, stop=False)
            pe.matmul(phn[:, 0:P], W.ones[0:1, :], b_hh[0:1, 2 * P:], start=False, stop=True)
            pe.matmul(pin[:, 0:P], W.ones[0:1, :], b_ih[0:1, 2 * P:], start=True, stop=False)
            pe.wait_ge(weighted, 1)
            pe.transpose(pt[:, 0:P], xt[:], W.ident[:]).then_inc(turned, 1)
            pe.wait_ge(copied, 1)
            pe.matmul(prz[:, 0:2 * P], xtT[:], w_ih[:, 0:2 * P], start=False, stop=True)
            pe.matmul(pin[:, 0:P], xtT[:], w_ih[:, 2 * P:], start=False, stop=True).then_inc(gates, 1)

        @block.vector
        def _(dve):
            steps = [0]

            def then(ins):
                ins.then_inc(step, 1)
                steps[0] += 1
                dve.wait_ge(step, steps[0])

            def best(values, out, place):
                for r in range(TOP // 8):
                    c = slice(8 * r, 8 * r + 8)
                    then(dve.max(out[:, c], values[:]))
                    then(dve.max_index(place[:, c], out[:, c], values[:]))
                    then(dve.match_replace(values[:], out[:, c], values[:], LOW))

            dve.wait_ge(loaded, 16 * 7)
            then(dve.tensor_tensor(pp[:], pb[:], pb[:], ALU.mult))
            dve.tensor_reduce(norm2[:], pp[:], AX, ALU.add).then_inc(normed, 1)
            dve.wait_ge(made, 2)
            then(dve.tensor_copy(basef[:], basei[:]))
            best(score, v1, i1)
            then(dve.tensor_copy(n1[:], i1[:]))
            then(dve.tensor_scalar(n1[:], n1[:], basef[:, 0:1], None, ALU.add))
            dve.tensor_copy(n1i[:], n1[:]).then_inc(l1_done, 1)
            dve.wait_ge(l2_loaded, 16)
            best(m2, v2, i2)
            then(dve.tensor_copy(f2[:], i2[:]))
            then(dve.tensor_scalar(f2[:], f2[:], basef[0:L2R, 1:2], None, ALU.add))
            dve.tensor_copy(f2i[:], f2[:]).then_inc(l2_done, 1)
            dve.wait_ge(l3_loaded, 16)
            best(m3, v3, i3)
            dve.tensor_copy(ssum[0:1, :], v3[0:1, 0:1]).then_inc(l3_done, 1)
            dve.wait_ge(l3_done, 1)
            dve.wait_ge(tanhed, 1)
            dve.wait_ge(found, 48)
            dve.tensor_scalar(xt[:], xt[:], th[:, 0:1], None, ALU.mult).then_inc(weighted, 1)
            dve.wait_ge(turned, 1)
            dve.tensor_copy(xtT[:], pt[:, 0:P]).then_inc(copied, 1)
            dve.wait_ge(opened, 1)
            then(dve.tensor_tensor(nn[:], rz[:, 0:P], phn[:, 0:P], ALU.mult))
            dve.tensor_tensor(nn[:], nn[:], pin[:, 0:P], ALU.add).then_inc(inner, 1)
            dve.wait_ge(newed, 1)
            then(dve.tensor_tensor(weight[:], w0[:], nn[:], ALU.subtract))
            then(dve.tensor_tensor(weight[:], weight[:], rz[:, P:2 * P], ALU.mult))
            then(dve.tensor_tensor(weight[:], weight[:], nn[:], ALU.add))
            then(dve.tensor_reduce(ssum[:], weight[:], AX, ALU.add))
            then(dve.tensor_scalar(ssum[:], ssum[:], -1.0 / P, None, ALU.mult))
            then(dve.tensor_copy(W.gru[:], weight[:]))
            then(dve.tensor_scalar(weight[:], weight[:], ssum[:, 0:1], -1.0 / P, ALU.add, ALU.add))
            then(dve.tensor_tensor(W.gru_dense[:], weight[:], W.ident[:], ALU.add))


class FeedForward:

    TURN, COPY, HIDDEN, GELU, PRODUCT, SQUARE, SUM, SCALE, JOIN, MOMENTS, LAST, STEPS = range(12)

    def __init__(self, mem, name, S, W, norm, j, last, jl, bank_wide, bank_rows, n, nT, h, y3, x, out):
        self.n, self.nT, self.h, self.y3, self.x, self.out = n, nT, h, y3, x, out
        self.S, self.W, self.norm, self.j, self.last, self.jl = S, W, norm, j, last, jl
        self.bw, self.br = bank_wide, bank_rows
        self.turned, self.copied, self.hidden, self.gelued, self.rows_made, self.joined, self.added = (
            mem.sems(name + "_" + n, S)
            for n in ("turned", "copied", "hidden", "gelued", "rows_made", "joined", "added"))

    def pe(self, pe, k, s, i):
        W = self.W
        if k == self.TURN:
            wait(pe, self.norm.normed[s], self.norm.nth(i, self.j))
            transpose_tiles(pe, self.bw[s], self.n[s], W.ident).then_inc(self.turned[s], 1)
        if k == self.HIDDEN:
            wait(pe, self.copied[s], i + 1)
            pe.matmul(self.bw[s][:], W.w1_ffn[:], self.nT[s][:], start=True, stop=True).then_inc(self.hidden[s], 1)
            const_rows(pe, self.br[s], W, C_FFN)
            rows_matmul(pe, self.br[s], self.nT[s], W.g1c[:])
        if k == self.PRODUCT:
            wait(pe, self.gelued[s], i + 1)
            rows_matmul(pe, self.br[s], self.h[s], W.w2_ffn[:], stop=True).then_inc(self.rows_made[s], 1)

    def act(self, act, k, s, i):
        if k == self.COPY:
            wait(act, self.turned[s], i + 1)
            act.copy(self.nT[s][:], self.bw[s][:]).then_inc(self.copied[s], 1)
        if k == self.GELU:
            wait(act, self.hidden[s], i + 1)
            act.activation(self.h[s][:], self.bw[s][:], ACT.Gelu, bias=self.W.b1_ffn[:, 0:1]).then_inc(self.gelued[s], 1)
        if k == self.SQUARE:
            wait(act, self.rows_made[s], i + 1)
            self.norm.square(act, s, tiles(self.br[s][:]))

    def dve(self, dve, k, s, i):
        if k == self.SUM:
            self.norm.sums(dve, i, s, self.j + 1)
        if k == self.SCALE:
            wait(dve, self.norm.rooted[s], self.norm.nth(i, self.j + 1))
            for t in range(TPG):
                c = slice(t * P, (t + 1) * P)
                ins = dve.scalar_tensor_tensor(self.n[s][:, c], self.br[s][:, c], self.norm.rstd[s][:, t:t + 1],
                                               self.W.g2[:], ALU.mult, ALU.mult)
            ins.then_inc(self.norm.normed[s], 1)
        if k == self.JOIN:
            wait(dve, self.added[s], i + 1)
            wait(dve, self.norm.normed[s], self.norm.nth(i, self.j + 1))
            dve.tensor_tensor(self.y3[s][:], self.n[s][:], self.x[s][:], ALU.add).then_inc(self.joined[s], 1)
        if k == self.MOMENTS:
            wait(dve, self.joined[s], i + 1)
            self.last.moments(dve, i, s, self.y3[s])
        if k == self.LAST:
            self.last.scale_moments(dve, i, s, self.jl, self.out[s], self.y3[s])

    def pool(self, pool, k, s, i):
        if k == self.SUM:
            self.norm.root(pool, i, s, self.j + 1, self.W.minus_half)
        if k == self.MOMENTS:
            self.last.root(pool, i, s, self.jl, self.W.minus_half)


def dense_pass(nc, A, D, W, Ed, plan):
    S, N, DG = plan.DS, plan.N, plan.DG
    mem = Mem(nc)
    sb4 = lambda n: [mem.sb(f"d_{n}{s}", [P, GROUP]) for s in range(S)]
    x, xT, x1, x2, y, x2b, x3, x4 = (sb4(n) for n in ("x", "xT", "x1", "x2", "y", "x2b", "x3", "x4"))
    bank_wide = [mem.ps(f"d_wide{s}") for s in range(S)]
    bank_rows = [mem.ps(f"d_rows{s}") for s in range(S)]
    norm = Norm(mem, "dn", S, 5)
    last = Norm(Mem(nc), "dl", S, 1, squares=False, stats=True)
    ff = FeedForward(mem, "df", S, W, norm, 2, last, 0, bank_wide, bank_rows,
                     sb4("n"), sb4("nT"), sb4("h"), sb4("y3"), x=x2b, out=x3)
    names = ("loaded", "turned", "copied", "rows_made", "residual", "hidden", "relued", "st1", "st2", "st3", "st4", "biased")
    sem = {n: mem.sems("d_" + n, S) for n in names}
    loaded, turned, copied, rows_made, residual, hidden, relued, st1, st2, st3, st4, biased = (sem[n] for n in names)
    began = mem.sem("d_began")
    rounds = DG // S
    LOAD, LAYER0 = 0, 3
    LAYER1 = LAYER0 + 6
    BIAS = LAYER1 + 6
    SUM2, SCALE2 = BIAS + 1, BIAS + 2
    FF = SCALE2 + 1
    TURN3 = FF + ff.STEPS
    COPY3, HIDDEN, RELU, PRODUCT, RESIDUAL, SQUARE4, SUM4, SCALE4, STEPS = range(TURN3 + 1, TURN3 + 10)
    LAG = (0, 17, 23, 31)
    look = Lookup(mem, "dk", Ed.src0, D["node_row"], plan.LOOKUPS)
    look_at = [1 + q * (STEPS - 3) // plan.LOOKUPS for q in range(plan.LOOKUPS)]

    def part(ap, g):
        parts = P
        if isinstance(g, int) and g >= plan.NF:
            parts = max(0, (N - g * GROUP) // TPG)
        return bass.AP(tensor=ap.tensor, offset=g * GROUP * P, ap=[[TPG * P, parts], [1, TPG * P]]), parts

    with nc.Block() as block:
        @block.sync
        def _(sp):
            t1, t2, t3 = (groups_of(D[f"x{k}"]) for k in (1, 2, 3))

            def step(k, s, i):
                g = i * S + s
                if k == LOAD:
                    wait(sp, turned[s], i * 3 - 2 if not isinstance(i, int) or i else 0)
                    src, parts = part(A["x"], g)
                    if parts == 0:
                        src, parts = part(A["x"], 0)
                    sp.dma_start(x[s][0:parts, :], src).then_inc(loaded[s], 16)
                if k == LAYER0 + 5:
                    wait(sp, norm.normed[s], norm.nth(i, 0))
                    sp.dma_start(t1[g], x1[s][:]).then_inc(st1[s], 16)
                if k == LAYER1 + 5:
                    wait(sp, norm.normed[s], norm.nth(i, 1))
                    sp.dma_start(t2[g], x2[s][:]).then_inc(st2[s], 16)
                if k == FF + ff.LAST:
                    wait(sp, last.normed[s], i + 1)
                    sp.dma_start(t3[g], x3[s][:]).then_inc(st3[s], 16)
                if k == SCALE4:
                    wait(sp, norm.normed[s], norm.nth(i, 4))
                    dst, parts = part(D["out"], g)
                    if parts:
                        sp.dma_start(dst, x4[s][0:parts, :]).then_inc(st4[s], 16)

            in_turns(sp, rounds, LAG, STEPS, step, tail=1)
            for s in range(S):
                for st in (st1, st2, st3):
                    sp.wait_ge(st[s], 16 * rounds)
                sp.wait_ge(st4[s], 16 * (rounds - 1 if ((rounds - 1) * S + s) * GROUP >= N else rounds))

        @block.tensor
        def _(pe):
            def step(k, s, i):
                if k == LAYER0:
                    wait(pe, loaded[s], 16 * i + 16)
                    transpose_tiles(pe, bank_wide[s], x[s], W.ident).then_inc(turned[s], 1)
                if k == LAYER0 + 2:
                    wait(pe, copied[s], 3 * i + 1)
                    wait(pe, residual[s], i)
                    rows_matmul(pe, bank_rows[s], xT[s], W.gru_dense[:], start=True, stop=True).then_inc(rows_made[s], 1)
                if k == LAYER1:
                    wait(pe, norm.normed[s], norm.nth(i, 0))
                    transpose_tiles(pe, bank_wide[s], x1[s], W.ident).then_inc(turned[s], 1)
                if k == LAYER1 + 2:
                    wait(pe, copied[s], 3 * i + 2)
                    const_rows(pe, bank_rows[s], W, C_PNA_DENSE)
                    rows_matmul(pe, bank_rows[s], xT[s], W.pna_dense[:], stop=True).then_inc(rows_made[s], 1)
                ff.pe(pe, k - FF, s, i)
                if k == TURN3:
                    wait(pe, last.normed[s], i + 1)
                    transpose_tiles(pe, bank_wide[s], x3[s], W.ident).then_inc(turned[s], 1)
                if k == HIDDEN:
                    wait(pe, copied[s], 3 * i + 3)
                    pe.matmul(bank_wide[s][:], W.w1a[:], xT[s][:], start=True, stop=True).then_inc(hidden[s], 1)
                if k == PRODUCT:
                    const_rows(pe, bank_rows[s], W, C_MSG)
                    wait(pe, relued[s], i + 1)
                    rows_matmul(pe, bank_rows[s], ff.h[s], W.w2_msg[:], stop=True).then_inc(rows_made[s], 1)

            in_turns(pe, rounds, LAG, STEPS, step)

        @block.scalar
        def _(act):
            def step(k, s, i):
                for j, copy in enumerate((LAYER0 + 1, LAYER1 + 1, COPY3)):
                    if k == copy:
                        wait(act, turned[s], 3 * i + j + 1)
                        act.copy(xT[s][:], bank_wide[s][:]).then_inc(copied[s], 1)
                for j, square in enumerate((LAYER0 + 3, LAYER1 + 3)):
                    if k == square:
                        wait(act, rows_made[s], 3 * i + j + 1)
                        norm.square(act, s, tiles(bank_rows[s][:]))
                if k == BIAS:
                    wait(act, biased[s], i + 1)
                    norm.square(act, s, tiles(y[s][:]))
                ff.act(act, k - FF, s, i)
                if k == RELU:
                    wait(act, hidden[s], i + 1)
                    act.activation(ff.h[s][:], bank_wide[s][:], ACT.Relu, bias=W.cols[:, B1_MSG:B1_MSG + 1]).then_inc(relued[s], 1)
                if k == SQUARE4:
                    wait(act, residual[s], i + 1)
                    norm.square(act, s, tiles(y[s][:]))

            in_turns(act, rounds, LAG, STEPS, step)

        @block.gpsimd
        def _(pool):
            def step(k, s, i):
                if s == 0:
                    if k == 0:
                        look.begin(pool, i, i * plan.LOOKUPS, 3)
                    for t in range(plan.LOOKUPS):
                        if k == look_at[t]:
                            look.fetch(pool, t)
                    if k == STEPS - 1:
                        look.take(pool, i, i * plan.LOOKUPS, Ed.src, Ed.coef)
                for j, sum_ in enumerate((LAYER0 + 4, LAYER1 + 4, SUM2)):
                    if k == sum_:
                        norm.root(pool, i, s, j, W.minus_half)
                if k == BIAS:
                    wait(pool, norm.normed[s], norm.nth(i, 1))
                    pool.tensor_tensor(tiles(y[s][:]), tiles(x2[s][:]), each(W.bo[:], TPG), ALU.add).then_inc(biased[s], 1)
                if k == SCALE2:
                    pool.tensor_tensor(tiles(x2b[s][:]), tiles(x2[s][:]), each(W.be2[:], TPG), ALU.add).then_inc(ff.added[s], 1)
                ff.pool(pool, k - FF, s, i)
                if k == SUM4:
                    norm.root(pool, i, s, 4, W.minus_half)

            in_turns(pool, rounds, LAG, STEPS, step)

        @block.vector
        def _(dve):
            norm.set_eps(dve, began)
            dve.wait_ge(began, S)

            def step(k, s, i):
                for j, layer, out, stored in ((0, LAYER0, x1, st1), (1, LAYER1, x2, st2)):
                    if k == layer + 4:
                        norm.sums(dve, i, s, j)
                    if k == layer + 5:
                        wait(dve, stored[s], 16 * i)
                        norm.scale(dve, i, s, j, out[s][:], bank_rows[s][:])
                if k == SUM2:
                    norm.sums(dve, i, s, 2)
                if k == SCALE2:
                    norm.scale(dve, i, s, 2, ff.n[s][:], y[s][:])
                if k == FF + ff.LAST:
                    wait(dve, st3[s], 16 * i)
                ff.dve(dve, k - FF, s, i)
                if k == RESIDUAL:
                    wait(dve, rows_made[s], 3 * i + 3)
                    dve.tensor_tensor(y[s][:], bank_rows[s][:], x3[s][:], ALU.add).then_inc(residual[s], 1)
                if k == SUM4:
                    norm.sums(dve, i, s, 4)
                if k == SCALE4:
                    wait(dve, residual[s], i + 1)
                    wait(dve, st4[s], 16 * i)
                    norm.scale(dve, i, s, 4, x4[s][:], y[s][:])

            in_turns(dve, rounds, LAG, STEPS, step)

class Gather:

    def __init__(self, mem, name, S, index, table, rows):
        self.index, self.table, self.rows, self.mem = index, table, rows, mem
        self.slot = [mem.sb(f"{name}_slot{s}", [P, TPG], I32) for s in range(S)]
        self.slotted = mem.sems(name + "_slotted", S)
        self.landed = mem.sems(name + "_landed", S)

    def fetch(self, pool, i, s, g):
        pool.tensor_copy(self.slot[s][:], self.index[:, bass.ds(g * TPG, TPG)]).then_inc(self.slotted[s], 1)
        wait(pool, self.slotted[s], i + 1)
        self.mem.settle(pool)
        for t in range(TPG):
            pool.indirect_dma_start(
                out=self.rows[s][:, t * P:(t + 1) * P], out_offset=None, in_=self.table,
                in_offset=bass.IndirectOffsetOnAxis(ap=self.slot[s][:, t:t + 1], axis=0),
            ).then_inc(self.landed[s], 16)

    def arrived(self, eng, i, s):
        wait(eng, self.landed[s], (i + 1) * 16 * TPG)


def tok(ap, g):
    return over(ap[:, bass.ds(g * TPG, TPG)], P)


def pos(ap, g):
    return ap[:, bass.ds(g * GROUP, GROUP)]


def gcn_edges(nc, A, D, W, Ed, plan):
    S, rounds = plan.ES, plan.EG // plan.ES
    mem = Mem(nc)
    rows = lambda n: [mem.sb(f"g_{n}{s}", [P, GROUP]) for s in range(S)]
    src, own, scaled, ownd, run, u, y, x1 = (rows(n) for n in ("src", "own", "scaled", "ownd", "run", "u", "y", "x1"))
    bank_src, bank_own, bank_out = ([mem.ps(f"g_{n}{s}") for s in range(S)] for n in ("bsrc", "bown", "bout"))
    last = Norm(Mem(nc), "gl", S, 1, squares=False, stats=True)
    gsrc = Gather(mem, "gs", S, Ed.src0, A["x"], src)
    gown = Gather(mem, "go", S, Ed.dst0, A["x"], own)
    weighted, turned, scanned, summed, made, mixed, masked, stored = (
        mem.sems("g_" + n, S) for n in ("weighted", "turned", "scanned", "summed", "made", "mixed", "masked", "stored"))
    began = mem.sem("g_began")
    table = groups_of(D["x1"])
    GATHER, WEIGH = 0, 8
    TURN, SCAN, SUM, PRODUCT, OUTER, ADD, MOMENTS, SCALE, STEPS = range(WEIGH + 1, WEIGH + 10)
    LAG = (0, 8)

    with nc.Block() as block:
        @block.gpsimd
        def _(pool):
            def step(k, s, i):
                if k == GATHER:
                    wait(pool, weighted[s], 2 * i)
                    gsrc.fetch(pool, i, s, i * S + s)
                    wait(pool, mixed[s], 2 * i)
                    gown.fetch(pool, i, s, i * S + s)
                if k == MOMENTS:
                    last.root(pool, i, s, 0, W.minus_half)

            in_turns(pool, rounds, LAG, STEPS, step)

        @block.vector
        def _(dve):
            dve.memset(run[S - 1][:], 0.0).then_inc(began, 1)
            dve.wait_ge(began, 1)

            def step(k, s, i):
                g = i * S + s
                if k == WEIGH:
                    gsrc.arrived(dve, i, s)
                    dve.tensor_tensor(tiles(scaled[s][:]), tiles(src[s][:]), tok(Ed.coef, g), ALU.mult).then_inc(weighted[s], 1)
                    gown.arrived(dve, i, s)
                    dve.tensor_tensor(tiles(ownd[s][:]), tiles(own[s][:]), tok(Ed.dinv, g), ALU.mult).then_inc(weighted[s], 1)
                if k == SCAN:
                    wait(dve, masked[s], 32 * i + 32)
                    wait(dve, turned[s], i + 1)
                    wait(dve, scanned[s - 1], i + 1 if s else i)
                    dve.tensor_tensor_scan(run[s][:], pos(Ed.keep, g), bank_src[s][:], run[s - 1][:, GROUP - 1:GROUP],
                                           ALU.mult, ALU.add).then_inc(scanned[s], 1)
                if k == SUM:
                    wait(dve, scanned[s], i + 1)
                    dve.tensor_tensor(u[s][:], run[s][:], bank_own[s][:], ALU.add).then_inc(summed[s], 1)
                if k == OUTER:
                    wait(dve, made[s], i + 1)
                    dve.tensor_tensor(tiles(y[s][:]), tiles(bank_out[s][:]), tok(Ed.dinv, g), ALU.mult).then_inc(mixed[s], 1)
                if k == ADD:
                    wait(dve, mixed[s], 2 * i + 1)
                    dve.tensor_tensor(y[s][:], y[s][:], own[s][:], ALU.add).then_inc(mixed[s], 1)
                if k == MOMENTS:
                    wait(dve, mixed[s], 2 * i + 2)
                    last.moments(dve, i, s, y[s])
                if k == SCALE:
                    wait(dve, stored[s], 16 * i)
                    last.scale_moments(dve, i, s, 0, x1[s], y[s])

            in_turns(dve, rounds, LAG, STEPS, step)

        @block.tensor
        def _(pe):
            def step(k, s, i):
                if k == TURN:
                    wait(pe, weighted[s], 2 * i + 2)
                    wait(pe, summed[s], i)
                    transpose_tiles(pe, bank_src[s], scaled[s], W.ident)
                    transpose_tiles(pe, bank_own[s], ownd[s], W.ident).then_inc(turned[s], 1)
                if k == PRODUCT:
                    wait(pe, summed[s], i + 1)
                    wait(pe, mixed[s], 2 * i)
                    rows_matmul(pe, bank_out[s], u[s], W.gru[:], start=True, stop=True).then_inc(made[s], 1)

            in_turns(pe, rounds, LAG, STEPS, step)

        @block.sync
        def _(sp):
            def step(k, s, i):
                g = i * S + s
                if k == GATHER:
                    for mask, row in ((Ed.keep, D["keep"]), (Ed.low, D["low"])):
                        sp.dma_start(pos(mask, g), row[bass.ds(g, 1), :].to_broadcast([P, GROUP])).then_inc(masked[s], 16)
                if k == SCALE:
                    wait(sp, last.normed[s], i + 1)
                    sp.dma_start(table[g + plan.DG], x1[s][:]).then_inc(stored[s], 16)

            in_turns(sp, rounds, LAG, STEPS, step)
            for s in range(S):
                sp.wait_ge(stored[s], 16 * rounds)


def pna_edges(nc, A, D, W, Ed, plan):
    S, rounds = plan.ES, plan.EG // plan.ES
    mem = Mem(nc)
    rows = lambda n: [mem.sb(f"p_{n}{s}", [P, GROUP]) for s in range(S)]
    src, own, srcT, ownT, neg, sqr, rc = (rows(n) for n in ("src", "own", "srcT", "ownT", "neg", "sqr", "rc"))
    mx, mn, s1, s2, mean, var = (rows(n) for n in ("mx", "mn", "s1", "s2", "mean", "var"))
    y, x2 = (rows(n) for n in ("y", "x2"))
    m2, std, ya = sqr, var, neg
    bank = [[mem.ps(f"p_b{s}{k}") for k in range(4)] for s in range(S)]
    norm = Norm(mem, "pn", S, 1)
    gsrc = Gather(mem, "pg", S, Ed.src, D["x1"], src)
    look = [Lookup(mem, f"pk{s}", Ed.dst0, D["node_row"], TPG) for s in range(S)]
    (turned, copied, made, negated, squared, scanned, averaged, m2_made, var_made, rooted, mixed,
     loaded, stored) = (mem.sems("p_" + n, S) for n in (
        "turned", "copied", "made", "negated", "squared", "scanned", "averaged", "m2_made", "var_made", "rooted",
        "mixed", "loaded", "stored"))
    sums_made = mem.sems("p_sums_made", S)
    began = mem.sem("p_began")
    tin, tout = groups_of(D["x1"]), groups_of(D["x2"])
    GATHER, TURN = 0, 4
    (COPY, SOURCE, OWN, SCAN, MEAN, EXTREMES, SUBTRACT, CLAMP, ROOT, DEVIATION, SCALERS, ADD, ADD2, SQUARE, SUM,
     SCALE, STEPS) = range(TURN + 1, TURN + 18)
    LAG = (0, 10)

    with nc.Block() as block:
        @block.sync
        def _(sp):
            def step(k, s, i):
                if k == GATHER:
                    wait(sp, turned[s], 2 * i)
                    sp.dma_start(own[s][:], tin[i * S + s + plan.DG]).then_inc(loaded[s], 16)
                    wait(sp, averaged[s], 2 * i)
                    sp.dma_start(rc[s][:], D["rcount"][bass.ds(i * S + s, 1), :].to_broadcast([P, GROUP])).then_inc(loaded[s], 16)
                if k == SCALE:
                    wait(sp, norm.normed[s], i + 1)
                    sp.dma_start(tout[i * S + s + plan.DG], x2[s][:]).then_inc(stored[s], 16)

            in_turns(sp, rounds, LAG, STEPS, step)
            for s in range(S):
                sp.wait_ge(stored[s], 16 * rounds)

        @block.gpsimd
        def _(pool):
            def step(k, s, i):
                if k == GATHER:
                    wait(pool, turned[s], 2 * i)
                    gsrc.fetch(pool, i, s, i * S + s)
                if k == OWN:
                    look[s].begin(pool, i, (i * S + s) * TPG, 2)
                    for t in range(TPG):
                        look[s].fetch(pool, t)
                if k == SUM:
                    norm.root(pool, i, s, 0, W.minus_half)
                    look[s].take(pool, i, (i * S + s) * TPG, Ed.dst)

            in_turns(pool, rounds, LAG, STEPS, step)

        @block.tensor
        def _(pe):
            def products(s, n, cols, stop=False):
                for k in range(3):
                    mm = rows_matmul(pe, bank[s][1 + k], cols[s], W.post[:, 1 + 4 * k + n, :], stop=stop)
                return mm

            def step(k, s, i):
                if k == TURN:
                    gsrc.arrived(pe, i, s)
                    wait(pe, mixed[s], 4 * i)
                    transpose_tiles(pe, bank[s][0], src[s], W.ident).then_inc(turned[s], 1)
                    wait(pe, loaded[s], 32 * i + 32)
                    transpose_tiles(pe, bank[s][1], own[s], W.ident).then_inc(turned[s], 1)
                if k == SOURCE:
                    wait(pe, copied[s], 2 * i + 1)
                    pe.matmul(bank[s][0][:], W.pna_src[:], srcT[s][:], start=True, stop=True).then_inc(made[s], 1)
                if k == OWN:
                    wait(pe, copied[s], 2 * i + 2)
                    for b in range(3):
                        const_rows(pe, bank[s][1 + b], W, C_PNA + b)
                        rows_matmul(pe, bank[s][1 + b], ownT[s], W.own[:, b, :])
                if k == EXTREMES:
                    wait(pe, scanned[s], 4 * i + 4)
                    products(s, 0, mx)
                    products(s, 1, mn)
                if k == SUBTRACT:
                    wait(pe, averaged[s], 2 * i + 1)
                    products(s, 2, mean)
                if k == DEVIATION:
                    wait(pe, rooted[s], i + 1)
                    products(s, 3, std, stop=True).then_inc(sums_made[s], 1)

            in_turns(pe, rounds, LAG, STEPS, step)

        @block.scalar
        def _(act):
            def step(k, s, i):
                if k == COPY:
                    wait(act, turned[s], 2 * i + 1)
                    act.copy(srcT[s][:], bank[s][0][:]).then_inc(copied[s], 1)
                    wait(act, turned[s], 2 * i + 2)
                    act.copy(ownT[s][:], bank[s][1][:]).then_inc(copied[s], 1)
                if k == OWN:
                    wait(act, made[s], i + 1)
                    act.activation(sqr[s][:], bank[s][0][:], ACT.Square).then_inc(squared[s], 1)
                    act.activation(neg[s][:], bank[s][0][:], ACT.Copy, scale=-1.0).then_inc(negated[s], 1)
                if k == EXTREMES:
                    wait(act, averaged[s], 2 * i + 1)
                    act.activation(m2[s][:], mean[s][:], ACT.Square).then_inc(m2_made[s], 1)
                if k == ROOT:
                    wait(act, var_made[s], 2 * i + 2)
                    act.activation(std[s][:], var[s][:], ACT.Sqrt).then_inc(rooted[s], 1)
                if k == SQUARE:
                    wait(act, mixed[s], 4 * i + 4)
                    norm.square(act, s, tiles(y[s][:]))

            in_turns(act, rounds, LAG, STEPS, step)

        @block.vector
        def _(dve):
            norm.set_eps(dve, began)
            for k, rows_ in enumerate((mx, mn, s1, s2)):
                dve.memset(rows_[S - 1][:], 0.0).then_inc(began, 1)
            dve.wait_ge(began, S + 4)
            end = slice(GROUP - 1, GROUP)

            def step(k, s, i):
                g = i * S + s
                if k == SCAN:
                    wait(dve, made[s], i + 1)
                    wait(dve, squared[s], i + 1)
                    wait(dve, negated[s], i + 1)
                    wait(dve, scanned[s - 1], 4 * (i + 1 if s else i))
                    dve.tensor_tensor_scan(s1[s][:], pos(Ed.keep, g), bank[s][0][:], s1[s - 1][:, end], ALU.mult, ALU.add).then_inc(scanned[s], 1)
                    dve.tensor_tensor_scan(mx[s][:], pos(Ed.low, g), bank[s][0][:], mx[s - 1][:, end], ALU.add, ALU.max).then_inc(scanned[s], 1)
                    dve.tensor_tensor_scan(s2[s][:], pos(Ed.keep, g), sqr[s][:], s2[s - 1][:, end], ALU.mult, ALU.add).then_inc(scanned[s], 1)
                    dve.tensor_tensor_scan(mn[s][:], pos(Ed.low, g), neg[s][:], mn[s - 1][:, end], ALU.add, ALU.max).then_inc(scanned[s], 1)
                if k == MEAN:
                    wait(dve, loaded[s], 32 * i + 32)
                    wait(dve, scanned[s], 4 * i + 4)
                    dve.tensor_tensor(mean[s][:], s1[s][:], rc[s][:], ALU.mult).then_inc(averaged[s], 1)
                    dve.tensor_tensor(var[s][:], s2[s][:], rc[s][:], ALU.mult).then_inc(averaged[s], 1)
                if k == SUBTRACT:
                    wait(dve, averaged[s], 2 * i + 2)
                    wait(dve, m2_made[s], i + 1)
                    dve.tensor_tensor(var[s][:], var[s][:], m2[s][:], ALU.subtract).then_inc(var_made[s], 1)
                if k == CLAMP:
                    wait(dve, var_made[s], 2 * i + 1)
                    dve.tensor_scalar(var[s][:], var[s][:], 0.0, EPS, ALU.max, ALU.add).then_inc(var_made[s], 1)
                if k == SCALERS:
                    wait(dve, sums_made[s], i + 1)
                    dve.tensor_tensor(tiles(ya[s][:]), tiles(bank[s][2][:]), tok(Ed.amp, g), ALU.mult).then_inc(mixed[s], 1)
                    dve.tensor_tensor(tiles(y[s][:]), tiles(bank[s][3][:]), tok(Ed.att, g), ALU.mult).then_inc(mixed[s], 1)
                if k == ADD:
                    wait(dve, mixed[s], 4 * i + 2)
                    dve.tensor_tensor(ya[s][:], ya[s][:], bank[s][1][:], ALU.add).then_inc(mixed[s], 1)
                if k == ADD2:
                    wait(dve, mixed[s], 4 * i + 3)
                    dve.tensor_tensor(y[s][:], y[s][:], ya[s][:], ALU.add).then_inc(mixed[s], 1)
                if k == SUM:
                    norm.sums(dve, i, s, 0)
                if k == SCALE:
                    wait(dve, mixed[s], 4 * i + 4)
                    wait(dve, stored[s], 16 * i)
                    norm.scale(dve, i, s, 0, x2[s][:], y[s][:])

            in_turns(dve, rounds, LAG, STEPS, step)


def attention_edges(nc, A, D, W, Ed, plan):
    S, rounds = plan.ES, plan.EG // plan.ES
    mem = Mem(nc)
    rows = lambda n: [mem.sb(f"a_{n}{s}", [P, GROUP]) for s in range(S)]
    src, own, srcT, ownT, q, qk = (rows(n) for n in ("src", "own", "srcT", "ownT", "q", "qk"))
    fade, prob, pv, den, acc, x2b = (rows(n) for n in ("fade", "prob", "pv", "den", "acc", "x2b"))
    o, y, x3 = q, qk, pv
    m = [mem.sb(f"a_m{s}", [P, GROUP + 1]) for s in range(S)]
    typ = [mem.sb(f"a_typ{s}", [3 * TYPES, GROUP], I32) for s in range(S)]
    hot = [mem.sb(f"a_hot{s}", [3 * TYPES, GROUP], BF16) for s in range(S)]
    bank = [[mem.ps(f"a_b{s}{k}") for k in range(4)] for s in range(S)]
    norm = Norm(mem, "an", S, 2)
    last = Norm(Mem(nc), "al", S, 1, squares=False, stats=True)
    ff = FeedForward(mem, "af", S, W, norm, 0, last, 0, [b[2] for b in bank], [b[3] for b in bank],
                     n=prob, nT=srcT, h=ownT, y3=fade, x=x2b, out=x3)
    gsrc = Gather(mem, "as", S, Ed.src, D["x2"], src)
    gown = Gather(mem, "ao", S, Ed.dst, D["x2"], own)
    (turned, copied, q_made, q_moved, kv_made, matched, hot_made, logits, peaked, differed, exped, valued,
     scanned, divided, out_made, residual, loaded, stored) = (mem.sems("a_" + n, S) for n in (
        "turned", "copied", "q_made", "q_moved", "kv_made", "matched", "hot_made", "logits", "peaked", "differed",
        "exped", "valued", "scanned", "divided", "out_made", "residual", "loaded", "stored"))
    began = mem.sem("a_began")
    tout = groups_of(D["x3"])
    BQc, BKc, BVc = (W.cols[:, k:k + 1] for k in (BQ, BK, BV))
    GATHER, TURN = 0, 4
    (COPY, PROJECT, MOVE, MATCH, LOGITS, PEAK, DIFFER, FADE, EXP, ACCUMULATE, VALUES, RECIPROCAL, DIVIDE, PRODUCT, RESIDUAL,
     SQUARE, SUM, SCALE, FF) = range(TURN + 1, TURN + 20)
    STEPS = FF + ff.STEPS
    LAG = (0, 23)

    with nc.Block() as block:
        @block.sync
        def _(sp):
            def step(k, s, i):
                if k == GATHER:
                    wait(sp, hot_made[s], i)
                    sp.dma_start(typ[s][:], A["type_row"][bass.ds(i * S + s, 1), :].to_broadcast([3 * TYPES, GROUP])).then_inc(loaded[s], 16)
                if k == FF + ff.LAST:
                    wait(sp, last.normed[s], i + 1)
                    sp.dma_start(tout[i * S + s + plan.DG], x3[s][:]).then_inc(stored[s], 16)

            in_turns(sp, rounds, LAG, STEPS, step)
            for s in range(S):
                sp.wait_ge(stored[s], 16 * rounds)

        @block.gpsimd
        def _(pool):
            def step(k, s, i):
                if k == GATHER:
                    wait(pool, turned[s], 2 * i)
                    gsrc.fetch(pool, i, s, i * S + s)
                    wait(pool, residual[s], i)
                    gown.fetch(pool, i, s, i * S + s)
                if k == COPY:
                    gown.arrived(pool, i, s)
                    wait(pool, ff.joined[s], i)
                    pool.tensor_tensor(tiles(x2b[s][:]), tiles(own[s][:]), each(W.be2[:], TPG), ALU.add).then_inc(ff.added[s], 1)
                if k == SUM:
                    norm.root(pool, i, s, 0, W.minus_half)
                ff.pool(pool, k - FF, s, i)

            in_turns(pool, rounds, LAG, STEPS, step)

        @block.tensor
        def _(pe):
            def step(k, s, i):
                if k == TURN:
                    gsrc.arrived(pe, i, s)
                    wait(pe, norm.normed[s], 2 * i)
                    transpose_tiles(pe, bank[s][0], src[s], W.ident).then_inc(turned[s], 1)
                    gown.arrived(pe, i, s)
                    transpose_tiles(pe, bank[s][1], own[s], W.ident).then_inc(turned[s], 1)
                if k == PROJECT:
                    wait(pe, copied[s], 2 * i + 2)
                    pe.matmul(bank[s][2][:], W.wq[:], ownT[s][:], start=True, stop=True).then_inc(q_made[s], 1)
                    pe.matmul(bank[s][3][:], W.wk[:], srcT[s][:], start=True, stop=True)
                    pe.matmul(bank[s][0][:], W.wv[:], srcT[s][:], start=True, stop=True).then_inc(kv_made[s], 1)
                if k == LOGITS:
                    wait(pe, hot_made[s], i + 1)
                    pe.matmul(bank[s][1][:], W.head_bias[:], hot[s][:], start=True, stop=False)
                    wait(pe, matched[s], i + 1)
                    pe.matmul(bank[s][1][:], W.heads[:], qk[s][:], start=False, stop=True).then_inc(logits[s], 1)
                if k == PRODUCT:
                    const_rows(pe, bank[s][3], W, C_WO)
                    wait(pe, divided[s], 3 * i + 3)
                    rows_matmul(pe, bank[s][3], o[s], W.wo[:], stop=True).then_inc(out_made[s], 1)
                ff.pe(pe, k - FF, s, i)

            in_turns(pe, rounds, LAG, STEPS, step)

        @block.scalar
        def _(act):
            def step(k, s, i):
                if k == COPY:
                    wait(act, turned[s], 2 * i + 1)
                    act.copy(srcT[s][:], bank[s][0][:]).then_inc(copied[s], 1)
                    wait(act, turned[s], 2 * i + 2)
                    act.copy(ownT[s][:], bank[s][1][:]).then_inc(copied[s], 1)
                if k == MOVE:
                    wait(act, q_made[s], i + 1)
                    act.activation(q[s][:], bank[s][2][:], ACT.Identity, bias=BQc).then_inc(q_moved[s], 1)
                if k == EXP:
                    wait(act, differed[s], 3 * i + 2)
                    act.activation(prob[s][:], prob[s][:], ACT.Exp).then_inc(exped[s], 1)
                    wait(act, differed[s], 3 * i + 3)
                    act.activation(fade[s][:], fade[s][:], ACT.Exp).then_inc(exped[s], 1)
                if k == SQUARE:
                    wait(act, residual[s], i + 1)
                    norm.square(act, s, tiles(y[s][:]))
                ff.act(act, k - FF, s, i)

            in_turns(act, rounds, LAG, STEPS, step)

        @block.vector
        def _(dve):
            norm.set_eps(dve, began)
            dve.memset(m[S - 1][:], 0.0).then_inc(began, 1)
            dve.memset(den[S - 1][:], 0.0).then_inc(began, 1)
            dve.memset(acc[S - 1][:], 0.0).then_inc(began, 1)
            dve.wait_ge(began, S + 3)
            end = slice(GROUP - 1, GROUP)

            def step(k, s, i):
                g = i * S + s
                before = i + 1 if s else i
                if k == TURN:
                    wait(dve, loaded[s], 16 * i + 16)
                    dve.tensor_scalar(hot[s][:], typ[s][:], W.split[:, 0:1], None, ALU.is_equal).then_inc(hot_made[s], 1)
                if k == MATCH:
                    wait(dve, q_moved[s], i + 1)
                    wait(dve, kv_made[s], i + 1)
                    dve.scalar_tensor_tensor(qk[s][:], bank[s][3][:], BKc, q[s][:], ALU.add, ALU.mult).then_inc(matched[s], 1)
                if k == PEAK:
                    wait(dve, logits[s], i + 1)
                    wait(dve, peaked[s - 1], 2 * before)
                    dve.tensor_copy(m[s][:, 0:1], m[s - 1][:, GROUP:]).then_inc(peaked[s], 1)
                    dve.tensor_tensor_scan(m[s][:, 1:], pos(Ed.low, g), bank[s][1][:], m[s - 1][:, GROUP:], ALU.add, ALU.max).then_inc(peaked[s], 1)
                if k == DIFFER:
                    wait(dve, peaked[s], 2 * i + 2)
                    dve.tensor_tensor(fade[s][:], m[s][:, 0:GROUP], pos(Ed.low, g), ALU.add).then_inc(differed[s], 1)
                    dve.tensor_tensor(prob[s][:], bank[s][1][:], m[s][:, 1:], ALU.subtract).then_inc(differed[s], 1)
                if k == FADE:
                    wait(dve, differed[s], 3 * i + 1)
                    dve.tensor_tensor(fade[s][:], fade[s][:], m[s][:, 1:], ALU.subtract).then_inc(differed[s], 1)
                if k == ACCUMULATE:
                    wait(dve, exped[s], 2 * i + 1)
                    wait(dve, stored[s], 16 * i)
                    dve.scalar_tensor_tensor(pv[s][:], bank[s][0][:], BVc, prob[s][:], ALU.add, ALU.mult).then_inc(valued[s], 1)
                    wait(dve, exped[s], 2 * i + 2)
                    wait(dve, scanned[s - 1], 2 * before)
                    dve.tensor_tensor_scan(den[s][:], fade[s][:], prob[s][:], den[s - 1][:, end], ALU.mult, ALU.add).then_inc(scanned[s], 1)
                if k == VALUES:
                    wait(dve, valued[s], i + 1)
                    dve.tensor_tensor_scan(acc[s][:], fade[s][:], pv[s][:], acc[s - 1][:, end], ALU.mult, ALU.add).then_inc(scanned[s], 1)
                    wait(dve, scanned[s], 2 * i + 2)
                    dve.tensor_scalar(pv[s][:], den[s][:], 1e-16, None, ALU.add).then_inc(divided[s], 1)
                if k == RECIPROCAL:
                    wait(dve, divided[s], 3 * i + 1)
                    dve.reciprocal(o[s][:], pv[s][:]).then_inc(divided[s], 1)
                if k == DIVIDE:
                    wait(dve, divided[s], 3 * i + 2)
                    dve.tensor_tensor(o[s][:], acc[s][:], o[s][:], ALU.mult).then_inc(divided[s], 1)
                if k == RESIDUAL:
                    gown.arrived(dve, i, s)
                    wait(dve, out_made[s], i + 1)
                    dve.tensor_tensor(y[s][:], bank[s][3][:], own[s][:], ALU.add).then_inc(residual[s], 1)
                if k == SUM:
                    norm.sums(dve, i, s, 0)
                if k == SCALE:
                    wait(dve, residual[s], i + 1)
                    norm.scale(dve, i, s, 0, ff.n[s][:], y[s][:])
                ff.dve(dve, k - FF, s, i)

            in_turns(dve, rounds, LAG, STEPS, step)


def message_edges(nc, A, D, W, Ed, plan):
    S, rounds = plan.ES, plan.EG // plan.ES
    mem = Mem(nc)
    rows = lambda n: [mem.sb(f"m_{n}{s}", [P, GROUP]) for s in range(S)]
    src, own, srcT, ownT, mx, h, y, x4 = (rows(n) for n in ("src", "own", "srcT", "ownT", "mx", "h", "y", "x4"))
    wrow = [mem.sb(f"m_wrow{s}", [1, GROUP]) for s in range(S)]
    oslot = [mem.sb(f"m_oslot{s}", [P, TPG], I32) for s in range(S)]
    bank = [[mem.ps(f"m_b{s}{k}") for k in range(4)] for s in range(S)]
    norm = Norm(mem, "mn", S, 1)
    gsrc = Gather(mem, "mg", S, Ed.src, D["x3"], src)
    turned, copied, made, scanned, hidden, relued, out_made, residual, loaded, oslotted, stored = (
        mem.sems("m_" + n, S) for n in ("turned", "copied", "made", "scanned", "hidden", "relued", "out_made",
                                        "residual", "loaded", "oslotted", "stored"))
    began = mem.sem("m_began")
    tin = groups_of(D["x3"])
    GATHER, TURN = 0, 8
    COPY, SOURCE, OWN, HIDDEN, RELU, PRODUCT, RESIDUAL, SQUARE, SUM, SCALE, SCATTER, STEPS = range(TURN + 1, TURN + 13)
    LAG = (0, 10)

    with nc.Block() as block:
        @block.sync
        def _(sp):
            def step(k, s, i):
                if k == GATHER:
                    wait(sp, residual[s], i)
                    sp.dma_start(own[s][:], tin[i * S + s + plan.DG]).then_inc(loaded[s], 16)
                    wait(sp, made[s], i)
                    sp.dma_start(wrow[s][:], A["w_row"][bass.ds(i * S + s, 1), :]).then_inc(loaded[s], 16)

            in_turns(sp, rounds, LAG, STEPS, step)

        @block.gpsimd
        def _(pool):
            def step(k, s, i):
                if k == GATHER:
                    wait(pool, turned[s], 2 * i)
                    gsrc.fetch(pool, i, s, i * S + s)
                if k == SUM:
                    norm.root(pool, i, s, 0, W.minus_half)
                if k == SCATTER:
                    wait(pool, stored[s], i * 16 * TPG)
                    pool.tensor_copy(oslot[s][:], Ed.out[:, bass.ds((i * S + s) * TPG, TPG)]).then_inc(oslotted[s], 1)
                    wait(pool, oslotted[s], i + 1)
                    wait(pool, norm.normed[s], i + 1)
                    mem.settle(pool)
                    for t in range(TPG):
                        pool.indirect_dma_start(
                            out=D["out"], out_offset=bass.IndirectOffsetOnAxis(ap=oslot[s][:, t:t + 1], axis=0),
                            in_=x4[s][:, t * P:(t + 1) * P], in_offset=None, bounds_check=plan.N - 1, oob_is_err=False,
                        ).then_inc(stored[s], 16)

            in_turns(pool, rounds, LAG, STEPS, step)
            for s in range(S):
                pool.wait_ge(stored[s], rounds * 16 * TPG)

        @block.tensor
        def _(pe):
            def step(k, s, i):
                if k == TURN:
                    gsrc.arrived(pe, i, s)
                    wait(pe, residual[s], i)
                    transpose_tiles(pe, bank[s][0], src[s], W.ident).then_inc(turned[s], 1)
                    wait(pe, loaded[s], 32 * i + 32)
                    transpose_tiles(pe, bank[s][1], own[s], W.ident).then_inc(turned[s], 1)
                if k == SOURCE:
                    wait(pe, copied[s], 2 * i + 1)
                    pe.matmul(bank[s][0][:], W.msg_src[:], srcT[s][:], start=True, stop=False)
                    pe.matmul(bank[s][0][:], W.msg_w[:], wrow[s][:], start=False, stop=True).then_inc(made[s], 1)
                if k == OWN:
                    wait(pe, copied[s], 2 * i + 2)
                    pe.matmul(bank[s][2][:], W.w1a_edge[:], ownT[s][:], start=True, stop=False)
                    const_rows(pe, bank[s][3], W, C_MSG)
                if k == HIDDEN:
                    wait(pe, scanned[s], i + 1)
                    pe.matmul(bank[s][2][:], W.w1b[:], mx[s][:], start=False, stop=True).then_inc(hidden[s], 1)
                if k == PRODUCT:
                    wait(pe, relued[s], i + 1)
                    rows_matmul(pe, bank[s][3], h[s], W.w2_msg[:], stop=True).then_inc(out_made[s], 1)

            in_turns(pe, rounds, LAG, STEPS, step)

        @block.scalar
        def _(act):
            def step(k, s, i):
                if k == COPY:
                    wait(act, turned[s], 2 * i + 1)
                    act.copy(srcT[s][:], bank[s][0][:]).then_inc(copied[s], 1)
                    wait(act, turned[s], 2 * i + 2)
                    act.copy(ownT[s][:], bank[s][1][:]).then_inc(copied[s], 1)
                if k == RELU:
                    wait(act, hidden[s], i + 1)
                    act.activation(h[s][:], bank[s][2][:], ACT.Relu, bias=W.b1_msg[:, 0:1]).then_inc(relued[s], 1)
                if k == SQUARE:
                    wait(act, residual[s], i + 1)
                    norm.square(act, s, tiles(y[s][:]))

            in_turns(act, rounds, LAG, STEPS, step)

        @block.vector
        def _(dve):
            norm.set_eps(dve, began)
            dve.memset(mx[S - 1][:], 0.0).then_inc(began, 1)
            dve.wait_ge(began, S + 1)

            def step(k, s, i):
                if k == OWN:
                    wait(dve, made[s], i + 1)
                    wait(dve, scanned[s - 1], i + 1 if s else i)
                    dve.tensor_tensor_scan(mx[s][:], pos(Ed.low, i * S + s), bank[s][0][:], mx[s - 1][:, GROUP - 1:],
                                           ALU.add, ALU.max).then_inc(scanned[s], 1)
                if k == RESIDUAL:
                    wait(dve, loaded[s], 32 * i + 32)
                    wait(dve, out_made[s], i + 1)
                    dve.tensor_tensor(y[s][:], bank[s][3][:], own[s][:], ALU.add).then_inc(residual[s], 1)
                if k == SUM:
                    norm.sums(dve, i, s, 0)
                if k == SCALE:
                    wait(dve, residual[s], i + 1)
                    wait(dve, stored[s], i * 16 * TPG)
                    norm.scale(dve, i, s, 0, x4[s][:], y[s][:])

            in_turns(dve, rounds, LAG, STEPS, step)


def build(nc, A, out, nodes, edges):
    plan = Plan(nodes, edges)
    EG, R, EP = plan.EG, plan.R, plan.EP
    D = {"out": out}
    for k in (1, 2, 3):
        D[f"x{k}"] = nc.dram_tensor(f"table_x{k}", (R + EP, P), F32, kind="Internal").ap()
    for n, shape, dt in (
        ("node_row", (P * plan.C, 2), F32), ("keep", (EG, GROUP), BF16), ("low", (EG, GROUP), BF16),
        ("count", (EG, GROUP), F32), ("wsum", (EG, GROUP), F32), ("rcount", (EG, GROUP), F32),
        ("top_val1", (P * TOP, 1), F32), ("top_node", (P * TOP, 1), I32), ("top_val2", (16 * TOP, 1), F32),
        ("top_place", (16 * TOP, 1), I32), ("top_val3", (TOP, 1), F32), ("top_place3", (TOP, 1), I32),
    ):
        D[n] = nc.dram_tensor("scratch_" + n, shape, dt, kind="Internal").ap()
    W = Weights(nc)
    with nc.cleanup_on_exit():
        fold_weights(nc, A, W)
    Ed = EdgeData(nc, plan)
    with nc.cleanup_on_exit():
        scan_rows(nc, A, D, W, plan)
    with nc.cleanup_on_exit():
        mem = Mem(nc)
        score, weight = mem.sb("score", [P, max(plan.C, TOP)]), mem.sb("gru_weight", [P, P])
        Own = OwnRows(nc, plan)
        with nc.cleanup_on_exit():
            edge_tables(nc, A, D, W, Ed, Own, plan)
        with nc.cleanup_on_exit():
            scores(nc, A, D, W, Ed, Own, plan, score)
        with nc.cleanup_on_exit():
            top_nodes(nc, A, D, W, Ed, Own, plan, score, weight)
    with nc.cleanup_on_exit():
        dense_pass(nc, A, D, W, Ed, plan)
    Ed.add_masks(nc, plan)
    for layer in (gcn_edges, pna_edges, attention_edges, message_edges):
        with nc.cleanup_on_exit():
            layer(nc, A, D, W, Ed, plan)


def laid_out(inputs):
    import numpy as np

    a = {k: np.asarray(v) for k, v in inputs.items()}
    nodes, edges = a["x"].shape[0], a["src"].shape[0]
    plan = Plan(nodes, edges)

    def by_row(v, fill, shift=0):
        flat = np.full(plan.EP + 2, fill, v.dtype)
        flat[1:edges + 1] = v
        if shift < 0:
            flat[0] = -1
        return np.ascontiguousarray(flat[1 + shift:1 + shift + plan.EP].reshape(plan.EG, GROUP))

    def by_tile(v):
        return np.ascontiguousarray(v.reshape(plan.EG, P, TPG).transpose(1, 0, 2).reshape(P, plan.ET))

    col = lambda n: a[n].reshape(P, 1)
    row = lambda n: a[n].reshape(1, -1)
    T = np.ascontiguousarray
    out = {
        "x": a["x"],
        "dst_row": by_row(a["dst"], nodes), "prev_row": by_row(a["dst"], nodes, -1), "w_row": by_row(a["edge_weight"], 0),
        "type_row": by_row(a["edge_type_8"], 0),
        "dst_tok": by_tile(by_row(a["dst"], nodes)), "next_tok": by_tile(by_row(a["dst"], nodes, 1)),
        "dst0_tok": by_tile(by_row(a["dst"], 0)), "src_tok": by_tile(by_row(a["src"], 0)),
        "w_tok": by_tile(by_row(a["edge_weight"], 0)),
        "L0_p": row("L0_gnn_p"), "L0_w_ihT": T(a["L0_gnn_w_ih"].T), "L0_w_hhT": T(a["L0_gnn_w_hh"].T),
        "L0_b_ih": row("L0_gnn_b_ih"), "L0_b_hh": row("L0_gnn_b_hh"), "L0_W0": a["L0_gnn_W0"], "L0_W0T": T(a["L0_gnn_W0"].T),
        "L1_W_post": a["L1_gnn_W_post"], "L1_W_linT": T(a["L1_gnn_W_lin"].T),
        "L1_W_pre_dst": T(a["L1_gnn_W_pre"][:, :P]), "L1_W_pre_srcT": T(a["L1_gnn_W_pre"][:, P:].T),
        "L2_Wq": a["L2_gnn_Wq"], "L2_Wk": a["L2_gnn_Wk"], "L2_Wv": a["L2_gnn_Wv"], "L2_Wo": a["L2_gnn_Wo"],
        "L2_W1": a["L2_gnn_W1"], "L2_W2": a["L2_gnn_W2"], "L2_edge_bias": a["L2_gnn_edge_bias"],
        "L2_g2": row("L2_gnn_g2"), "L2_be2": row("L2_gnn_be2"), "L2_bo": row("L2_gnn_bo"),
        "L3_Ws": T(a["L3_gnn_Wm"][P:2 * P]), "L3_WdT": T(a["L3_gnn_Wm"][:P].T), "L3_ww": T(a["L3_gnn_Wm"][2 * P:]),
        "L3_W1": a["L3_gnn_W1"], "L3_W2": a["L3_gnn_W2"],
        "split": np.stack([np.arange(3 * TYPES) % TYPES] + [np.arange(3 * TYPES) // TYPES == k for k in range(3)], axis=1)
        .astype(np.float32),
        "columns": np.concatenate([col(n) for n in (
            "L2_gnn_g1", "L2_gnn_be1", "L2_gnn_b1", "L2_gnn_bq", "L2_gnn_bk", "L2_gnn_bv", "L3_gnn_b1", "L3_gnn_bm",
            "L1_gnn_b_post", "L1_gnn_b_pre")], axis=1),
        "rows": np.concatenate([row(n) for n in (
            "L2_gnn_be1", "L2_gnn_b2", "L3_gnn_b2", "L1_gnn_b_lin", "L2_gnn_bo")], axis=0),
    }
    return out, nodes, edges


def kernel(**inputs):
    import numpy as np
    import concourse.bacc as bacc
    from concourse.bass_utils import run_bass_kernel_spmd

    arrays, nodes, edges = laid_out(inputs)
    nc = bacc.Bacc("TRN2", target_bir_lowering=False, num_devices=1)
    A, fed = {}, {}
    for name, v in arrays.items():
        fed["in_" + name] = v
        A[name] = nc.dram_tensor("in_" + name, v.shape, mybir.dt.from_np(v.dtype), kind="ExternalInput").ap()
    out = nc.dram_tensor("out_rows", (nodes, P), F32, kind="ExternalOutput").ap()
    build(nc, A, out, nodes, edges)
    r = run_bass_kernel_spmd(nc, [fed], core_ids=[0])
    return r.results[0]["out_rows"]
```

```python
from contextlib import ExitStack

import concourse.bass as bass
from concourse import mybir

F32 = mybir.dt.float32
BF16 = mybir.dt.bfloat16
I32 = mybir.dt.int32
U32 = mybir.dt.uint32
ALU = mybir.AluOpType
ACT = mybir.ActivationFunctionType
AX = mybir.AxisListType.X

P = 128
TPG = 4
GROUP = P * TPG
TOP = 128
HEADS = 8
TYPES = 8
LOW = -3.0e38
EPS = 1e-5
ROOT = float(P) ** -0.5


def ceil_to(n, m):
    return (n + m - 1) // m * m


class Plan:

    def __init__(self, nodes, edges):
        self.N, self.E = nodes, edges
        self.DS, self.ES, self.AS = 4, 2, 3
        groups = (edges + GROUP - 1) // GROUP
        self.EG = ceil_to(groups, self.ES)
        self.A_ROUNDS = ceil_to(self.EG, self.AS) // self.AS
        self.AG = self.A_ROUNDS * self.AS
        self.EP = self.AG * GROUP
        self.ET = self.AG * TPG
        self.NF = nodes // GROUP
        self.DG = ceil_to((nodes + GROUP - 1) // GROUP, self.DS)
        self.R = self.DG * GROUP
        self.EARLY = self.EG // 6 * 2
        self.LOOKUPS = (self.ET + self.DG // self.DS - 1) // (self.DG // self.DS)
        self.LT = self.LOOKUPS * (self.DG // self.DS)
        self.C = (nodes + P - 1) // P
        self.LAST = nodes - (P - 1) * self.C
        assert 0 < self.LAST <= self.C and (nodes - self.NF * GROUP) % TPG == 0


def tiles(ap):
    return ap.rearrange("p (t f) -> p t f", t=TPG)


def over(ap, n):
    return ap.unsqueeze(2).to_broadcast([ap.shape[0], ap.shape[1], n])


def each(ap, n):
    return ap.unsqueeze(1).to_broadcast([ap.shape[0], n, ap.shape[1]])



def wait(eng, sem, count):
    if not (isinstance(count, int) and count == 0):
        eng.wait_ge(sem, count)


def each_round(eng, rounds, one_round):
    one_round(0)
    if rounds > 1:
        with eng.Fori(1, rounds) as i:
            one_round(i)


def in_turns(eng, rounds, lag, steps, step, tail=0):
    def one_round(i, begins=True, ends=True):
        for t in range(steps):
            for s, late in enumerate(lag):
                if t >= late:
                    if begins:
                        step(t - late, s, i)
                elif ends:
                    step(t - late + steps, s, i - 1)

    one_round(0, ends=False)
    if rounds > 1:
        one_round(1)
    if rounds - tail > 2:
        with eng.Fori(2, rounds - tail) as i:
            one_round(i)
    for i in range(max(2, rounds - tail), rounds):
        one_round(i)
    one_round(rounds, begins=False)


def another(i, rounds):
    return not isinstance(i, int) or i + 1 < rounds


class Mem:

    def __init__(self, nc):
        self.nc = nc
        self.gate = None

    def settle(self, eng):
        if self.gate is None:
            self.gate = self.sem(f"settled_{eng.engine.name}_{self.nc.next_id()}")
        eng.sem_inc(self.gate, 1)

    def sb(self, name, shape, dt=F32):
        return self.nc.alloc_sbuf_tensor(name, shape, dt)

    def ps(self, name):
        return self.nc.alloc_psum_tensor(name, [P, 512], F32)

    def sem(self, name):
        return self.nc.alloc_semaphore(name)

    def sems(self, name, n):
        return [self.sem(f"{name}{k}") for k in range(n)]


class Norm:

    def __init__(self, mem, name, S, per, squares=True, stats=False, by_scalar=False):
        self.per, self.mem = per, mem
        if squares:
            self.sq = [mem.sb(f"{name}_sq{s}", [P, TPG, P + 1]) for s in range(S)]
            self.squared = mem.sems(name + "_squared", S)
        if stats:
            self.st = [mem.sb(f"{name}_st{s}", [P, TPG, 6]) for s in range(S)]
            self.mv = [mem.sb(f"{name}_mv{s}", [P, TPG, 2]) for s in range(S)]
            self.stats_made = mem.sems(name + "_stats_made", S)
        self.var = [mem.sb(f"{name}_var{s}", [P, TPG]) for s in range(S)]
        self.rstd = [mem.sb(f"{name}_rstd{s}", [P, TPG]) for s in range(S)]
        self.summed = mem.sems(name + "_summed", S)
        self.rooted = mem.sems(name + "_rooted", S)
        if by_scalar:
            self.inverted = mem.sems(name + "_inverted", S)
            self.newton = [mem.sb(f"{name}_newton{s}", [P, TPG]) for s in range(S)]
        self.by_scalar = by_scalar
        self.normed = mem.sems(name + "_normed", S)

    def nth(self, i, j):
        return i * self.per + j + 1

    def set_eps(self, dve, began):
        for sq in self.sq:
            dve.memset(sq[:, :, P:P + 1], EPS).then_inc(began, 1)

    def square(self, act, i, s, j, y):
        wait(act, self.summed[s], i * self.per + j)
        act.activation(self.sq[s][:, :, 0:P], y, ACT.Square, scale=ROOT).then_inc(self.squared[s], 1)

    def sums(self, dve, i, s, j):
        wait(dve, self.squared[s], self.nth(i, j))
        dve.tensor_reduce(self.var[s][:], self.sq[s][:], AX, ALU.add).then_inc(self.summed[s], 1)

    def moments(self, dve, i, s, y):
        for t in range(TPG):
            dve.bn_stats(self.st[s][:, t, :], y[:, t * P:(t + 1) * P]).then_inc(self.stats_made[s], 1)
        wait(dve, self.stats_made[s], i * 2 * TPG + TPG)
        self.mem.settle(dve)
        for t in range(TPG):
            dve.bn_aggr(self.mv[s][:, t, :], self.st[s][:, t, :]).then_inc(self.stats_made[s], 1)
        wait(dve, self.stats_made[s], i * 2 * TPG + 2 * TPG)
        dve.tensor_scalar(self.var[s][:], self.mv[s][:, :, 1], EPS, None, ALU.add).then_inc(self.summed[s], 1)

    def root(self, pool, i, s, j, minus_half):
        wait(pool, self.summed[s], self.nth(i, j))
        pool.tensor_tensor(self.rstd[s][:], self.var[s][:], minus_half[:], ALU.pow).then_inc(self.rooted[s], 1)

    def root_by_scalar(self, act, i, s, j):
        wait(act, self.summed[s], self.nth(i, j))
        act.activation(self.rstd[s][:], self.var[s][:], ACT.Sqrt).then_inc(self.rooted[s], 1)

    def scale_by_scalar(self, act, i, s, j, out, y):
        wait(act, self.rooted[s], self.nth(i, j))
        for t in range(TPG):
            c = slice(t * P, (t + 1) * P)
            ins = act.activation(out[:, c], y[:, c], ACT.Copy, scale=self.rstd[s][:, t:t + 1])
        ins.then_inc(self.normed[s], 1)

    def wait_for_root(self, dve, i, s, j):
        wait(dve, self.rooted[s], self.nth(i, j))
        if self.by_scalar:
            v, r, t, done, before = self.var[s][:], self.rstd[s][:], self.newton[s][:], self.inverted[s], 4 * (self.nth(i, j) - 1)
            dve.reciprocal(r, r).then_inc(done, 1)
            wait(dve, done, before + 1)
            dve.tensor_tensor(t, r, r, ALU.mult).then_inc(done, 1)
            wait(dve, done, before + 2)
            dve.scalar_tensor_tensor(t, t, -0.5, v, ALU.mult, ALU.mult).then_inc(done, 1)
            wait(dve, done, before + 3)
            dve.scalar_tensor_tensor(r, t, 1.5, r, ALU.add, ALU.mult).then_inc(done, 1)
            wait(dve, done, before + 4)

    def scale(self, dve, i, s, j, out, y):
        self.wait_for_root(dve, i, s, j)
        dve.tensor_tensor(tiles(out), tiles(y), over(self.rstd[s][:], P), ALU.mult).then_inc(self.normed[s], 1)

    def scale_moments(self, dve, i, s, j, out, y):
        self.wait_for_root(dve, i, s, j)
        for t in range(TPG):
            c = slice(t * P, (t + 1) * P)
            ins = dve.tensor_scalar(out[:, c], y[:, c], self.mv[s][:, t, 0:1], self.rstd[s][:, t:t + 1],
                                    ALU.subtract, ALU.mult)
        ins.then_inc(self.normed[s], 1)


def transpose_tiles(pe, out, rows, ident):
    for t in range(TPG):
        mm = pe.transpose(out[:, t:GROUP:TPG], rows[:, t * P:(t + 1) * P], ident[:])
    return mm


def rows_matmul(pe, out, cols, w, start=False, stop=False):
    for t in range(TPG):
        mm = pe.matmul(out[:, t * P:(t + 1) * P], cols[:, t:GROUP:TPG], w,
                       start=start, stop=stop, skip_group_check=True)
    return mm


def const_rows(pe, out, W, c):
    pe.matmul(out[:], W.ones3[:], W.const[:, c, :, :], start=True, stop=False, skip_group_check=True)


def groups_of(ap):
    return ap.rearrange("(g p t) f -> g p (t f)", p=P, t=TPG)


class Weights:

    def __init__(self, nc):
        mem = Mem(nc)
        square = lambda name: mem.sb("w_" + name, [P, P])
        self.ident = square("ident")
        self.heads = square("heads")
        self.ones = square("ones")
        self.pna_src = square("pna_src")
        self.pna_dense = square("pna_dense")
        self.wq = square("wq")
        self.wk = square("wk")
        self.wv = square("wv")
        self.wo = square("wo")
        self.g1c = square("g1c")
        self.w1_ffn = square("w1_ffn")
        self.w2_ffn = square("w2_ffn")
        self.w1a = square("w1a")
        self.w1a_edge = square("w1a_edge")
        self.w1b = square("w1b")
        self.w2_msg = square("w2_msg")
        self.msg_src = square("msg_src")
        self.g2 = square("g2")
        self.be2 = square("be2")
        self.bo = square("bo")
        self.gru = square("gru")
        self.gru_dense = square("gru_dense")
        self.post = mem.sb("w_post", [P, 13, P])
        self.own = mem.sb("w_own", [P, 3, P])
        self.head_bias = mem.sb("w_head_bias", [3 * TYPES, P], BF16)
        self.split = mem.sb("w_split", [3 * TYPES, 4])
        self.msg_w = mem.sb("w_msg_w", [1, P])
        self.const = mem.sb("w_const", [3, C_ROWS, TPG, P], BF16)
        self.ones3 = mem.sb("w_ones3", [3, P], BF16)
        self.minus_half = mem.sb("w_minus_half", [P, TPG])
        self.cols = mem.sb("w_cols", [P, 16])
        self.b1_ffn = mem.sb("w_b1_ffn", [P, 1])
        self.b1_msg = mem.sb("w_b1_msg", [P, 1])


G1, BE1, B1_FFN, BQ, BK, BV, B1_MSG, BM, B_POST, B_PRE = range(10)
C_FFN, C_MSG, C_WO, C_PNA_DENSE, C_PNA = range(5)
C_ROWS = C_PNA + 3
R_BE1, R_B2_FFN, R_B2_MSG, R_B_LIN, R_BO, R_MADE = range(6)


def fold_weights(nc, A, W):
    mem = Mem(nc)
    raw_post = mem.sb("f_post", [P, 13 * P])
    raw = {n: mem.sb("f_" + n, [P, P]) for n in ("linT", "pre", "w1", "w2", "wo", "w1b", "w2m", "wdT")}
    bias8 = mem.sb("f_bias8", [3 * TYPES, HEADS])
    bias_wide = mem.sb("f_bias_wide", [3 * TYPES, P])
    crow = mem.sb("f_crow", [1, C_ROWS * P])
    crow3 = mem.sb("f_crow3", [3, C_ROWS * P])
    part3 = [mem.sb(f"f_part{k}", [3 * TYPES, C_ROWS * P], BF16) for k in range(4)]
    rows = mem.sb("f_rows", [1, 6, P])
    row = mem.sb("f_row", [1, P])
    sums = mem.sb("f_sums", [P, 1])
    csum = mem.sb("f_csum", [P, P])
    tmp = mem.sb("f_tmp", [P, P])
    bank = [mem.ps(f"f_bank{k}") for k in range(8)]
    loaded, made, step = mem.sem("f_loaded"), mem.sem("f_pool_made"), mem.sem("f_vector_step")
    linT_centred, block_made, block_copied = mem.sem("f_linT_centred"), mem.sem("f_block_made"), mem.sem("f_block_copied")
    csum_made, own_made = mem.sem("f_csum_made"), mem.sem("f_own_made")
    rows_done, thrice_made = mem.sem("f_rows_done"), mem.sem("f_thrice_made")
    std_made, last_made = mem.sem("f_std_weight"), mem.sem("f_last_products")
    loads = [
        (raw_post[:], A["L1_W_post"]), (raw["linT"][:], A["L1_W_linT"]), (raw["pre"][:], A["L1_W_pre_dst"]),
        (raw["w1"][:], A["L2_W1"]), (raw["w2"][:], A["L2_W2"]), (raw["wo"][:], A["L2_Wo"]),
        (raw["w1b"][:], A["L3_W1"][P:2 * P, :]), (raw["w2m"][:], A["L3_W2"]), (raw["wdT"][:], A["L3_WdT"]),
        (W.pna_src[:], A["L1_W_pre_srcT"]), (W.wq[:], A["L2_Wq"]),
        (W.wk[:], A["L2_Wk"]), (W.wv[:], A["L2_Wv"]), (W.msg_src[:], A["L3_Ws"]),
        (W.w1a[:], A["L3_W1"][0:P, :]), (W.w1b[:], A["L3_W1"][P:2 * P, :]), (W.msg_w[:], A["L3_ww"]),
        (W.g2[:], A["L2_g2"].to_broadcast([P, P])), (W.be2[:], A["L2_be2"].to_broadcast([P, P])),
        (W.bo[:], A["L2_bo"].to_broadcast([P, P])), (W.cols[:, 0:10], A["columns"]),
    ] + [(rows[0:1, k, :], A["rows"][k:k + 1, :]) for k in range(5)]
    loads += [(bias8[k * TYPES:(k + 1) * TYPES, :], A["L2_edge_bias"]) for k in range(3)] + [(W.split[:], A["split"])]
    cols = W.cols

    with nc.Block() as block:
        @block.sync
        def _(sp):
            for out, src in loads:
                sp.dma_start(out, src).then_inc(loaded, 16)

        @block.gpsimd
        def _(pool):
            heads = W.heads[:].rearrange("p (h d) -> p h d", h=HEADS)
            depth = P // HEADS
            pool.memset(W.ident[:], 1.0).then_inc(made, 1)
            pool.memset(W.heads[:], float(depth) ** -0.5).then_inc(made, 1)
            pool.memset(W.minus_half[:], -0.5).then_inc(made, 1)
            pool.memset(W.ones[:], 1.0).then_inc(made, 1)
            pool.memset(W.ones3[:], 1.0).then_inc(made, 1)
            pool.wait_ge(made, 5)
            pool.affine_select(out=W.ident[:], in_=W.ident[:], compare_op=ALU.is_equal, fill=0.0,
                               base=0, pattern=[[1, P]], channel_multiplier=-1).then_inc(made, 1)
            pool.affine_select(out=heads, in_=heads, compare_op=ALU.is_ge, fill=0.0, base=0,
                               pattern=[[-depth, HEADS], [0, depth]], channel_multiplier=1).then_inc(made, 1)
            pool.wait_ge(made, 7)
            pool.affine_select(out=heads, in_=heads, compare_op=ALU.is_ge, fill=0.0, base=depth - 1,
                               pattern=[[depth, HEADS], [0, depth]], channel_multiplier=-1).then_inc(made, 1)

        @block.vector
        def _(dve):
            steps = [0]

            def then(ins):
                ins.then_inc(step, 1)
                steps[0] += 1
                dve.wait_ge(step, steps[0])

            def centre(out, src):
                mean = sums[0:src.shape[0], :]
                then(dve.tensor_reduce(mean, src, AX, ALU.add))
                then(dve.tensor_scalar(mean, mean, -1.0 / P, None, ALU.mult))
                then(dve.tensor_scalar(out, src, mean, None, ALU.add))

            def constant(c, r):
                then(dve.tensor_copy(crow[:, c * P:(c + 1) * P], r))

            def split(out, x, member):
                n, m = x.shape
                high, middle, low, sum_ = (part3[k][0:n, 0:m] for k in range(4))
                then(dve.tensor_copy(high, x))
                then(dve.tensor_tensor(x, x, high, ALU.subtract))
                then(dve.tensor_copy(middle, x))
                then(dve.tensor_tensor(x, x, middle, ALU.subtract))
                then(dve.tensor_copy(low, x))
                then(dve.tensor_scalar(sum_, high, member[0], None, ALU.mult))
                then(dve.scalar_tensor_tensor(sum_, middle, member[1], sum_, ALU.mult, ALU.add))
                then(dve.scalar_tensor_tensor(sum_, low, member[2], sum_, ALU.mult, ALU.add))
                then(dve.tensor_copy(out, sum_.rearrange("p (c f) -> p c f", f=P).unsqueeze(2).to_broadcast([n, m // P, TPG, P])
                                     if m > P else sum_))

            dve.wait_ge(loaded, 16 * len(loads))
            dve.wait_ge(made, 8)
            centre(raw["linT"][:], raw["linT"][:])
            dve.tensor_copy(row[:], rows[0:1, R_BO, :]).then_inc(linT_centred, 1)
            dve.wait_ge(linT_centred, 1)
            centre(row[:], row[:])
            then(dve.tensor_tensor(row[:], row[:], W.be2[0:1, :], ALU.subtract))
            constant(C_WO, row[:])
            centre(W.w2_ffn[:], raw["w2"][:])
            centre(W.w2_msg[:], raw["w2m"][:])
            centre(W.wo[:], raw["wo"][:])
            centre(W.bo[:], W.bo[:])
            then(dve.tensor_scalar(W.g1c[:], W.ident[:], cols[:, G1:G1 + 1], None, ALU.mult))
            centre(W.g1c[:], W.g1c[:])
            then(dve.tensor_scalar(W.w1_ffn[:], raw["w1"][:], cols[:, G1:G1 + 1], None, ALU.mult))
            then(dve.tensor_tensor(row[:], rows[0:1, R_BE1, :], rows[0:1, R_B2_FFN, :], ALU.add))
            centre(row[:], row[:])
            constant(C_FFN, row[:])
            centre(row[:], rows[0:1, R_B2_MSG, :])
            constant(C_MSG, row[:])
            then(dve.tensor_copy(bias_wide[:].rearrange("p (h d) -> p h d", h=HEADS), over(bias8[:], P // HEADS)))
            split(W.head_bias[:], bias_wide[:], [W.split[:, k + 1:k + 2] for k in range(3)])

            for b in range(13):
                dve.wait_ge(block_made, b + 1)
                dve.tensor_copy(W.post[:, b, :], bank[b % 4][:, 0:P]).then_inc(block_copied, 1)
            dve.wait_ge(block_copied, 13)
            for k in range(3):
                mx, mn, mean = (W.post[:, 1 + 4 * k + n, :] for n in range(3))
                then(dve.tensor_tensor(csum[:], mx, mn, ALU.add))
                dve.tensor_tensor(csum[:], csum[:], mean, ALU.add).then_inc(csum_made, 1)
                then(dve.tensor_scalar(mn, mn, -1.0, None, ALU.mult))
                dve.wait_ge(own_made, k + 1)
                then(dve.tensor_copy(W.own[:, k, :], bank[4][:, 0:P]))
                then(dve.tensor_copy(row[:], bank[5][0:1, 0:P]))
                if k == 0:
                    centre(rows[0:1, R_B_LIN, :], rows[0:1, R_B_LIN, :])
                    then(dve.tensor_tensor(rows[0:1, R_B_LIN, :], rows[0:1, R_B_LIN, :], bank[5][0:1, P:2 * P], ALU.add))
                    then(dve.tensor_tensor(row[:], row[:], rows[0:1, R_B_LIN, :], ALU.add))
                constant(C_PNA + k, row[:])
            then(dve.tensor_scalar(tmp[:], W.ident[:], -1.0 / P, None, ALU.add))
            then(dve.tensor_tensor(W.pna_dense[:], W.post[:, 0, :], tmp[:], ALU.add))
            then(dve.tensor_tensor(W.own[:, 0, :], W.own[:, 0, :], W.pna_dense[:], ALU.add))
            ln2 = 0.6931471805599453
            then(dve.scalar_tensor_tensor(tmp[:], W.post[:, 8, :], ln2, W.post[:, 4, :], ALU.mult, ALU.add))
            then(dve.scalar_tensor_tensor(tmp[:], W.post[:, 12, :], 1.0 / ln2, tmp[:], ALU.mult, ALU.add))
            dve.tensor_scalar(tmp[:], tmp[:], EPS ** 0.5, None, ALU.mult).then_inc(std_made, 1)
            dve.wait_ge(last_made, 1)
            then(dve.tensor_tensor(row[:], rows[0:1, R_B_LIN, :], bank[6][0:1, 0:P], ALU.add))
            constant(C_PNA_DENSE, row[:])
            dve.tensor_tensor(W.b1_ffn[:], cols[:, B1_FFN:B1_FFN + 1], bank[7][:, 0:1], ALU.add)
            dve.tensor_tensor(W.b1_msg[:], cols[:, B1_MSG:B1_MSG + 1], bank[7][:, 1:2], ALU.add)
            dve.tensor_tensor(W.w1a_edge[:], W.w1a[:], bank[7][:, P:2 * P], ALU.add).then_inc(rows_done, 1)
            dve.wait_ge(thrice_made, 1)
            then(dve.tensor_copy(crow3[:, 0:GROUP], bank[0][0:3, :]))
            then(dve.tensor_copy(crow3[:, GROUP:], bank[1][0:3, 0:C_ROWS * P - GROUP]))
            split(W.const[:], crow3[:], [W.ident[0:3, k:k + 1] for k in range(3)])

        @block.tensor
        def _(pe):
            pe.wait_ge(loaded, 16 * len(loads))
            pe.wait_ge(made, 8)
            pe.wait_ge(linT_centred, 1)
            for b in range(13):
                if b >= 4:
                    pe.wait_ge(block_copied, b - 3)
                pe.matmul(bank[b % 4][:, 0:P], raw_post[:, b * P:(b + 1) * P], raw["linT"][:],
                          start=True, stop=True).then_inc(block_made, 1)
            pe.matmul(bank[5][0:1, P:2 * P], cols[:, B_POST:B_POST + 1], raw["linT"][:], start=True, stop=True)
            for k in range(3):
                pe.wait_ge(csum_made, k + 1)
                pe.matmul(bank[5][0:1, 0:P], cols[:, B_PRE:B_PRE + 1], csum[:], start=True, stop=True)
                pe.matmul(bank[4][:, 0:P], raw["pre"][:], csum[:], start=True, stop=True).then_inc(own_made, 1)
            pe.wait_ge(std_made, 1)
            pe.matmul(bank[6][0:1, 0:P], W.ones[:, 0:1], tmp[:], start=True, stop=True)
            pe.matmul(bank[7][:, 0:1], raw["w1"][:], cols[:, BE1:BE1 + 1], start=True, stop=True)
            pe.matmul(bank[7][:, 1:2], raw["w1b"][:], cols[:, BM:BM + 1], start=True, stop=True)
            pe.matmul(bank[7][:, P:2 * P], raw["wdT"][:], raw["w1b"][:], start=True, stop=True).then_inc(last_made, 1)
            pe.wait_ge(rows_done, 1)
            pe.matmul(bank[0][0:3, :], W.ones[0:1, 0:3], crow[:, 0:GROUP], start=True, stop=True)
            pe.matmul(bank[1][0:3, 0:C_ROWS * P - GROUP], W.ones[0:1, 0:3], crow[:, GROUP:], start=True, stop=True).then_inc(thrice_made, 1)


class EdgeData:

    def __init__(self, nc, plan):
        mem = Mem(nc)
        self.src0 = mem.sb("e_src0", [P, plan.LT], I32)
        self.src = mem.sb("e_src", [P, plan.LT], I32)
        self.coef = mem.sb("e_coef", [P, plan.LT])
        self.dst0 = mem.sb("e_dst0", [P, plan.ET], I32)
        self.dst = mem.sb("e_dst", [P, plan.ET], I32)
        self.out = mem.sb("e_out", [P, plan.ET], I32)
        self.dinv = mem.sb("e_dinv", [P, plan.ET])
        self.amp = mem.sb("e_amp", [P, plan.ET])
        self.att = mem.sb("e_att", [P, plan.ET])

    def add_low(self, nc, plan):
        self.low = Mem(nc).sb("e_low", [P, plan.EP], BF16)

    def add_keep(self, nc, plan):
        self.keep = Mem(nc).sb("e_keep", [P, plan.EP], BF16)


class OwnRows:

    def __init__(self, nc, plan):
        mem = Mem(nc)
        self.own = mem.sb("o_own", [P, plan.ET, 2])
        self.deg = mem.sb("o_deg", [P, plan.ET])
        self.half = mem.sb("o_half", [P, plan.ET])

    def root(self, mem, pool, Ed):
        rooted = mem.sem("o_rooted")
        pool.tensor_tensor(Ed.dinv[:], self.deg[:], self.half[:], ALU.pow).then_inc(rooted, 1)
        pool.wait_ge(rooted, 1)
        pool.tensor_copy(self.own[:, :, 1], Ed.dinv[:]).then_inc(rooted, 1)
        pool.wait_ge(rooted, 2)

    def scatter(self, mem, pool, D, Ed, plan, first, last):
        slot = [mem.sb(f"o_slot{u}_{first}", [P, TPG], I32) for u in range(2)]
        send = [mem.sb(f"o_send{u}_{first}", [P, TPG, 2]) for u in range(2)]
        slotted, moved = mem.sems(f"o_slotted_{first}_", 2), mem.sems(f"o_moved_{first}_", 2)

        def one_round(i):
            for u in range(2):
                at = bass.ds((i * 2 + u + first) * TPG, TPG)
                wait(pool, moved[u], i * 16 * TPG)
                pool.tensor_copy(slot[u][:], Ed.out[:, at]).then_inc(slotted[u], 1)
                pool.tensor_copy(send[u][:], self.own[:, at, :]).then_inc(slotted[u], 1)
            for u in range(2):
                wait(pool, slotted[u], i * 2 + 2)
                mem.settle(pool)
                for t in range(TPG):
                    pool.indirect_dma_start(
                        out=D["node_row"], out_offset=bass.IndirectOffsetOnAxis(ap=slot[u][:, t:t + 1], axis=0),
                        in_=send[u][:, t, :], in_offset=None, bounds_check=plan.N - 1, oob_is_err=False,
                    ).then_inc(moved[u], 16)

        rounds = (last - first) // 2
        if rounds:
            each_round(pool, rounds, one_round)
            for u in range(2):
                pool.wait_ge(moved[u], rounds * 16 * TPG)


class Lookup:

    def __init__(self, mem, name, node, table, n):
        self.mem, self.node, self.table, self.n = mem, node, table, n
        self.slot = mem.sb(name + "_slot", [P, n], I32)
        self.got = mem.sb(name + "_got", [P, n, 2])
        self.taken, self.fetched = mem.sem(name + "_taken"), mem.sem(name + "_fetched")

    def begin(self, pool, i, first, steps):
        pool.tensor_copy(self.slot[:], self.node[:, bass.ds(first, self.n)]).then_inc(self.taken, 1)
        wait(pool, self.taken, i * steps + 1)
        self.mem.settle(pool)

    def fetch(self, pool, t):
        pool.indirect_dma_start(out=self.got[:, t, :], out_offset=None, in_=self.table,
                                in_offset=bass.IndirectOffsetOnAxis(ap=self.slot[:, t:t + 1], axis=0)).then_inc(self.fetched, 16)

    def take(self, pool, i, first, row, factor=None):
        at = bass.ds(first, self.n)
        wait(pool, self.fetched, (i + 1) * 16 * self.n)
        pool.tensor_copy(row[:, at], self.got[:, :, 0]).then_inc(self.taken, 1)
        if factor is not None:
            pool.tensor_tensor(factor[:, at], factor[:, at], self.got[:, :, 1], ALU.mult).then_inc(self.taken, 1)


def scan_rows(nc, A, D, W, plan):
    EG = plan.AG
    mem = Mem(nc)
    dst, prev = mem.sb("r_dst", [EG, GROUP], I32), mem.sb("r_prev", [EG, GROUP], I32)
    wt = mem.sb("r_wt", [EG, GROUP])
    keep, low = mem.sb("r_keep", [EG, GROUP], BF16), mem.sb("r_low", [EG, GROUP], BF16)
    ones, zeros = mem.sb("r_ones", [EG, GROUP]), mem.sb("r_zeros", [EG, GROUP])
    whole = mem.sb("r_whole", [EG, GROUP])
    part = [mem.sb(f"r_part{k}", [EG, GROUP]) for k in range(2)]
    inv = mem.sb("r_inv", [EG, GROUP])
    line = mem.sb("r_line", [1, 3, EG])
    carry = mem.sb("r_carry", [1, 2, EG + 1])
    enter = mem.sb("r_enter", [EG, 2])
    turned, back = mem.ps("r_turned"), mem.ps("r_back")
    loaded, step, stored = mem.sem("r_loaded"), mem.sem("r_vector_step"), mem.sem("r_stored")
    ends, lined, carried, entered, full = (mem.sem("r_" + n) for n in ("ends", "lined", "carried", "entered", "full"))

    with nc.Block() as block:
        @block.sync
        def _(sp):
            sp.dma_start(dst[:], A["dst_row"]).then_inc(loaded, 16)
            sp.dma_start(prev[:], A["prev_row"]).then_inc(loaded, 16)
            sp.dma_start(wt[:], A["w_row"]).then_inc(loaded, 16)
            sp.wait_ge(full, 1)
            sp.dma_start(D["keep"], keep[:]).then_inc(stored, 16)
            sp.dma_start(D["low"], low[:]).then_inc(stored, 16)
            sp.dma_start(D["count"], part[0][:]).then_inc(stored, 16)
            sp.dma_start(D["wsum"], part[1][:]).then_inc(stored, 16)
            sp.dma_start(D["rcount"], inv[:]).then_inc(stored, 16)
            sp.wait_ge(stored, 80)

        @block.vector
        def _(dve):
            steps = [0]

            def then(ins):
                ins.then_inc(step, 1)
                steps[0] += 1
                dve.wait_ge(step, steps[0])

            then(dve.memset(ones[:], 1.0))
            then(dve.memset(zeros[:], 0.0))
            then(dve.memset(carry[:], 0.0))
            dve.wait_ge(loaded, 48)
            then(dve.tensor_tensor(keep[:], dst[:], prev[:], ALU.is_equal))
            then(dve.tensor_scalar(low[:], keep[:], -1.0, -LOW, ALU.add, ALU.mult))
            then(dve.tensor_tensor_scan(part[0][:], keep[:], ones[:], 0.0, ALU.mult, ALU.add))
            then(dve.tensor_tensor_scan(part[1][:], keep[:], wt[:], 0.0, ALU.mult, ALU.add))
            dve.tensor_tensor_scan(whole[:], keep[:], zeros[:], 1.0, ALU.mult, ALU.add).then_inc(ends, 1)
            dve.wait_ge(lined, 1)
            for k in range(3):
                then(dve.tensor_copy(line[:, k, :], turned[0:1, k * P:k * P + EG]))
            then(dve.tensor_tensor_scan(carry[:, 0, 1:], line[:, 2, :], line[:, 0, :], 0.0, ALU.mult, ALU.add))
            dve.tensor_tensor_scan(carry[:, 1, 1:], line[:, 2, :], line[:, 1, :], 0.0, ALU.mult, ALU.add).then_inc(carried, 1)
            dve.wait_ge(entered, 1)
            then(dve.tensor_copy(enter[:], back[0:EG, 0:2]))
            for k in range(2):
                then(dve.scalar_tensor_tensor(part[k][:], whole[:], enter[:, k:k + 1], part[k][:], ALU.mult, ALU.add))
            dve.reciprocal(inv[:], part[0][:]).then_inc(full, 1)

        @block.tensor
        def _(pe):
            pe.wait_ge(ends, 1)
            last = slice(GROUP - 1, GROUP)
            for k, rows in enumerate((part[0], part[1], whole)):
                mm = pe.transpose(turned[0:1, k * P:k * P + EG], rows[:, last], W.ident[0:EG, 0:EG])
            mm.then_inc(lined, 1)
            pe.wait_ge(carried, 1)
            for k in range(2):
                mm = pe.matmul(back[0:EG, k:k + 1], carry[0:1, k, 0:EG], W.ones[0:1, 0:1], start=True, stop=True)
            mm.then_inc(entered, 1)


def edge_tables(nc, A, D, W, Ed, Own, plan):
    C, ET, EG = plan.C, plan.ET, plan.AG
    mem = Mem(nc)
    nxt = mem.sb("t_next", [P, ET], I32)
    dsti = mem.sb("t_dst", [P, ET], I32)
    cnt, end = mem.sb("t_cnt", [P, ET]), mem.sb("t_end", [P, ET])
    pos = mem.sb("t_pos", [P, ET], I32)
    base_i = mem.sb("t_base_i", [P, C], I32)
    base = mem.sb("t_base", [P, C, 2])
    loaded, step, stored = mem.sem("t_loaded"), mem.sem("t_vector_step"), mem.sem("t_stored")
    made, logged, tables = mem.sem("t_pool_made"), mem.sem("t_logged"), mem.sem("t_tables")
    NONE = float(1 << 22)
    LOADS = 7

    with nc.Block() as block:
        @block.sync
        def _(sp):
            tok = lambda ap: ap.rearrange("g (p t) -> p g t", t=TPG)
            flat = lambda ap: ap.rearrange("p (g t) -> p g t", t=TPG)
            for out, src in ((dsti[:], "dst_tok"), (nxt[:], "next_tok"), (Ed.coef[:, 0:ET], "w_tok"), (Ed.src0[:, 0:ET], "src_tok"),
                             (Ed.dst0[:], "dst0_tok")):
                sp.dma_start(out, A[src]).then_inc(loaded, 16)
            sp.dma_start(flat(cnt[:]), tok(D["count"])).then_inc(loaded, 16)
            sp.dma_start(flat(Own.deg[:]), tok(D["wsum"])).then_inc(loaded, 16)
            sp.wait_ge(tables, 2)
            sp.dma_start(D["node_row"].rearrange("(p c) k -> p c k", p=P), base[:]).then_inc(stored, 16)
            sp.wait_ge(loaded, 16 * LOADS)
            sp.wait_ge(stored, 16)

        @block.vector
        def _(dve):
            steps = [0]

            def then(ins):
                ins.then_inc(step, 1)
                steps[0] += 1
                dve.wait_ge(step, steps[0])

            dve.wait_ge(made, 3)
            dve.tensor_copy(base[:, :, 0], base_i[:]).then_inc(tables, 1)
            dve.memset(base[:, :, 1], 1.0).then_inc(tables, 1)
            dve.tensor_copy(Own.own[:, :, 0], pos[:])
            dve.wait_ge(loaded, 16 * LOADS)
            then(dve.tensor_scalar(Own.deg[:], Own.deg[:], 1.0, None, ALU.add))
            then(dve.tensor_tensor(end[:], dsti[:], nxt[:], ALU.not_equal))
            then(dve.tensor_scalar(end[:], end[:], -NONE, NONE, ALU.mult, ALU.add))
            then(dve.tensor_tensor(end[:], end[:], dsti[:], ALU.add))
            then(dve.tensor_copy(Ed.out[:], end[:]))
            dve.wait_ge(logged, 1)
            then(dve.reciprocal(Ed.att[:], Ed.amp[:]))

        @block.scalar
        def _(act):
            act.wait_ge(loaded, 16 * LOADS)
            act.activation(Ed.amp[:], cnt[:], ACT.Ln, bias=1.0).then_inc(logged, 1)

        @block.gpsimd
        def _(pool):
            pool.iota(pos[:].rearrange("p (g t) -> p g t", t=TPG), [[GROUP, EG], [1, TPG]], base=plan.R,
                      channel_multiplier=TPG).then_inc(made, 1)
            pool.iota(base_i[:], [[1, C]], base=0, channel_multiplier=C).then_inc(made, 1)
            pool.memset(Own.half[:], -0.5).then_inc(made, 1)
            if plan.LT > ET:
                pool.memset(Ed.src0[:, ET:], 0)
                pool.memset(Ed.coef[:, ET:], 0.0)


def scores(nc, A, D, W, Ed, Own, plan, score):
    C, LAST = plan.C, plan.LAST
    mem = Mem(nc)
    wide = (C + 7) // 8
    chunks = [(c, min(c + wide, LAST), P) for c in range(0, LAST, wide)]
    chunks += [(c, min(c + wide, C), P - 1) for c in range(LAST, C, wide)]
    BUFS = 3
    buf = [mem.sb(f"s_x{k}", [P, wide * P]) for k in range(BUFS)]
    pb = mem.sb("s_p", [P, P])
    loaded, used = mem.sems("s_loaded", BUFS), mem.sem("s_used")
    p_loaded, weighted, cleared = mem.sem("s_p_loaded"), mem.sem("s_weighted"), mem.sem("s_cleared")

    def pieces(parts):
        return [(0, parts)] if parts % 16 == 0 else [(0, parts // 16 * 16), (parts // 16 * 16, parts)]

    with nc.Block() as block:
        @block.sync
        def _(sp):
            sp.dma_start(pb[:], A["L0_p"].to_broadcast([P, P])).then_inc(p_loaded, 16)
            for n, (a, b, parts) in enumerate(chunks):
                if n >= BUFS:
                    sp.wait_ge(used, n - BUFS + 1)
                for lo, hi in pieces(parts):
                    src = bass.AP(tensor=A["x"].tensor, offset=(lo * C + a) * P,
                                  ap=[[C * P, hi - lo], [1, (b - a) * P]])
                    sp.dma_start(buf[n % BUFS][lo:hi, 0:(b - a) * P], src).then_inc(loaded[n % BUFS], 16)

        @block.gpsimd
        def _(pool):
            Own.root(mem, pool, Ed)
            Own.scatter(mem, pool, D, Ed, plan, 0, plan.EARLY)

        @block.vector
        def _(dve):
            dve.memset(score[:], LOW).then_inc(cleared, 1)
            dve.wait_ge(p_loaded, 16)
            dve.wait_ge(cleared, 1)
            total = [0] * BUFS
            for n, (a, b, parts) in enumerate(chunks):
                total[n % BUFS] += 16 * len(pieces(parts))
                dve.wait_ge(loaded[n % BUFS], total[n % BUFS])
                rows = buf[n % BUFS][0:parts, 0:(b - a) * P].rearrange("p (c f) -> p c f", f=P)
                dve.tensor_tensor(rows, rows, each(pb[0:parts, :], b - a), ALU.mult).then_inc(weighted, 1)
                dve.wait_ge(weighted, n + 1)
                dve.tensor_reduce(score[0:parts, a:b], rows, AX, ALU.add).then_inc(used, 1)


def top_nodes(nc, A, D, W, Ed, Own, plan, score, weight):
    C, LEVELS = plan.C, 3
    mem = Mem(nc)
    ROWS = (32, 4, 1)
    v1, i1, n1 = mem.sb("k_v1", [P, TOP]), mem.sb("k_i1", [P, TOP], U32), mem.sb("k_n1", [P, TOP])
    n1i = mem.sb("k_n1i", [P, TOP], I32)
    basei, basef = mem.sb("k_basei", [P, 1 + LEVELS], I32), mem.sb("k_basef", [P, 1 + LEVELS])
    merged = [mem.sb(f"k_merged{r}", [r, before // r * TOP]) for r, before in zip(ROWS, (P,) + ROWS)]
    vm = [mem.sb(f"k_vm{r}", [r, TOP]) for r in ROWS]
    im = [mem.sb(f"k_im{r}", [r, TOP], U32) for r in ROWS]
    fm = [mem.sb(f"k_fm{r}", [r, TOP]) for r in ROWS]
    fmi = [mem.sb(f"k_fmi{r}", [r, TOP], I32) for r in ROWS]
    ids = mem.sb("k_ids", [P, 1 + LEVELS], I32)
    val = mem.sb("k_val", [P, 1])
    xt, pb = mem.sb("k_xt", [P, P]), mem.sb("k_pb", [P, P])
    pp, norm2, rnorm, th = mem.sb("k_pp", [P, P]), mem.sb("k_norm2", [P, 1]), mem.sb("k_rnorm", [P, 1]), mem.sb("k_th", [P, 1])
    w_ih, w_hh, w0t, w0 = mem.sb("k_w_ih", [P, 3 * P]), mem.sb("k_w_hh", [P, 3 * P]), mem.sb("k_w0t", [P, P]), mem.sb("k_w0", [P, P])
    b_ih, b_hh = mem.sb("k_b_ih", [1, 3 * P]), mem.sb("k_b_hh", [1, 3 * P])
    xtT = mem.sb("k_xtT", [P, P])
    rz, nn = mem.sb("k_rz", [P, 2 * P]), mem.sb("k_nn", [P, P])
    ssum = mem.sb("k_ssum", [P, 1])
    pt, prz, pin, phn = mem.ps("k_pt"), mem.ps("k_prz"), mem.ps("k_pin"), mem.ps("k_phn")
    step, loaded, made = mem.sem("k_step"), mem.sem("k_loaded"), mem.sem("k_made")
    best_found, best_stored, lists_loaded, val_loaded = (
        mem.sem("k_" + n) for n in ("best_found", "best_stored", "lists_loaded", "val_loaded"))
    found, rooted, tanhed = mem.sem("k_found"), mem.sem("k_rooted"), mem.sem("k_tanhed")
    normed, weighted, turned, copied, gates, opened, inner, newed = (
        mem.sem("k_" + n) for n in ("normed", "weighted", "turned", "copied", "gates", "opened", "inner", "newed"))
    row = lambda ap, p: ap.rearrange("(p c) k -> p (c k)", p=p)

    with nc.Block() as block:
        @block.sync
        def _(sp):
            for out, src in ((w_ih, A["L0_w_ihT"]), (w_hh, A["L0_w_hhT"]), (w0t, A["L0_W0T"]), (w0, A["L0_W0"]),
                             (b_ih, A["L0_b_ih"]), (b_hh, A["L0_b_hh"]), (pb, A["L0_p"].to_broadcast([P, P]))):
                sp.dma_start(out[:], src).then_inc(loaded, 16)
            sp.wait_ge(best_found, 1)
            sp.dma_start(row(D["top_val0"], P), v1[:]).then_inc(best_stored, 16)
            sp.dma_start(row(D["top_id0"], P), n1i[:]).then_inc(best_stored, 16)
            for n, r in enumerate(ROWS):
                sp.wait_ge(best_stored, 32 * (n + 1))
                sp.dma_start(merged[n][:], row(D[f"top_val{n}"], r)).then_inc(lists_loaded, 16)
                sp.wait_ge(best_found, n + 2)
                sp.dma_start(row(D[f"top_val{n + 1}"], r), vm[n][:]).then_inc(best_stored, 16)
                sp.dma_start(row(D[f"top_id{n + 1}"], r), fmi[n][:]).then_inc(best_stored, 16)
            sp.wait_ge(best_stored, 32 * (LEVELS + 1))
            sp.dma_start(val[:], D[f"top_val{LEVELS}"]).then_inc(val_loaded, 16)
            sp.dma_start(ids[:, 0:1], D[f"top_id{LEVELS}"]).then_inc(val_loaded, 16)
            sp.wait_ge(val_loaded, 32)

        @block.gpsimd
        def _(pool):
            pool.iota(basei[:], [[0, 1 + LEVELS]], base=0, channel_multiplier=C).then_inc(made, 1)
            pool.wait_ge(made, 1)
            for n, r in enumerate(ROWS):
                pool.iota(basei[0:r, n + 1:n + 2], [[0, 1]], base=0, channel_multiplier=merged[n].shape[1]).then_inc(made, 1)
            pool.wait_ge(normed, 1)
            pool.tensor_tensor(rnorm[:], norm2[:], W.minus_half[:, 0:1], ALU.pow).then_inc(rooted, 1)
            Own.scatter(mem, pool, D, Ed, plan, plan.EARLY, plan.EG)
            pool.wait_ge(val_loaded, 32)
            pool.wait_ge(best_stored, 32 * (LEVELS + 1))
            for k in range(LEVELS):
                pool.indirect_dma_start(out=ids[:, k + 1:k + 2], out_offset=None, in_=D[f"top_id{LEVELS - 1 - k}"],
                                        in_offset=bass.IndirectOffsetOnAxis(ap=ids[:, k:k + 1], axis=0)).then_inc(found, 16)
                pool.wait_ge(found, 16 * (k + 1))
            pool.indirect_dma_start(out=xt[:], out_offset=None, in_=A["x"],
                                    in_offset=bass.IndirectOffsetOnAxis(ap=ids[:, LEVELS:], axis=0)).then_inc(found, 16)
            pool.wait_ge(found, 16 * (LEVELS + 1))

        @block.scalar
        def _(act):
            act.wait_ge(rooted, 1)
            act.wait_ge(val_loaded, 32)
            act.activation(th[:], val[:], ACT.Tanh, scale=rnorm[:, 0:1]).then_inc(tanhed, 1)
            act.wait_ge(gates, 1)
            act.activation(rz[:], prz[:, 0:2 * P], ACT.Sigmoid).then_inc(opened, 1)
            act.wait_ge(inner, 1)
            act.activation(nn[:], nn[:], ACT.Tanh).then_inc(newed, 1)

        @block.tensor
        def _(pe):
            pe.wait_ge(loaded, 16 * 7)
            pe.matmul(prz[:, 0:2 * P], w0t[:], w_hh[:, 0:2 * P], start=True, stop=False)
            pe.matmul(prz[:, 0:2 * P], W.ones[0:1, :], b_hh[0:1, 0:2 * P], start=False, stop=False)
            pe.matmul(prz[:, 0:2 * P], W.ones[0:1, :], b_ih[0:1, 0:2 * P], start=False, stop=False)
            pe.matmul(phn[:, 0:P], w0t[:], w_hh[:, 2 * P:], start=True, stop=False)
            pe.matmul(phn[:, 0:P], W.ones[0:1, :], b_hh[0:1, 2 * P:], start=False, stop=True)
            pe.matmul(pin[:, 0:P], W.ones[0:1, :], b_ih[0:1, 2 * P:], start=True, stop=False)
            pe.wait_ge(weighted, 1)
            pe.transpose(pt[:, 0:P], xt[:], W.ident[:]).then_inc(turned, 1)
            pe.wait_ge(copied, 1)
            pe.matmul(prz[:, 0:2 * P], xtT[:], w_ih[:, 0:2 * P], start=False, stop=True)
            pe.matmul(pin[:, 0:P], xtT[:], w_ih[:, 2 * P:], start=False, stop=True).then_inc(gates, 1)

        @block.vector
        def _(dve):
            steps = [0]

            def then(ins):
                ins.then_inc(step, 1)
                steps[0] += 1
                dve.wait_ge(step, steps[0])

            def best(values, out, place):
                for r in range(TOP // 8):
                    c = slice(8 * r, 8 * r + 8)
                    then(dve.max(out[:, c], values[:]))
                    then(dve.max_index(place[:, c], out[:, c], values[:]))
                    then(dve.match_replace(values[:], out[:, c], values[:], LOW))

            dve.wait_ge(loaded, 16 * 7)
            then(dve.tensor_tensor(pp[:], pb[:], pb[:], ALU.mult))
            dve.tensor_reduce(norm2[:], pp[:], AX, ALU.add).then_inc(normed, 1)
            dve.wait_ge(made, 1 + LEVELS)
            then(dve.tensor_copy(basef[:], basei[:]))
            best(score, v1, i1)
            then(dve.tensor_copy(n1[:], i1[:]))
            then(dve.tensor_scalar(n1[:], n1[:], basef[:, 0:1], None, ALU.add))
            dve.tensor_copy(n1i[:], n1[:]).then_inc(best_found, 1)
            for n, r in enumerate(ROWS):
                dve.wait_ge(lists_loaded, 16 * (n + 1))
                best(merged[n], vm[n], im[n])
                then(dve.tensor_copy(fm[n][:], im[n][:]))
                then(dve.tensor_scalar(fm[n][:], fm[n][:], basef[0:r, n + 1:n + 2], None, ALU.add))
                dve.tensor_copy(fmi[n][:], fm[n][:]).then_inc(best_found, 1)
            dve.wait_ge(tanhed, 1)
            dve.wait_ge(found, 16 * (LEVELS + 1))
            dve.tensor_scalar(xt[:], xt[:], th[:, 0:1], None, ALU.mult).then_inc(weighted, 1)
            dve.wait_ge(turned, 1)
            dve.tensor_copy(xtT[:], pt[:, 0:P]).then_inc(copied, 1)
            dve.wait_ge(opened, 1)
            then(dve.tensor_tensor(nn[:], rz[:, 0:P], phn[:, 0:P], ALU.mult))
            dve.tensor_tensor(nn[:], nn[:], pin[:, 0:P], ALU.add).then_inc(inner, 1)
            dve.wait_ge(newed, 1)
            then(dve.tensor_tensor(weight[:], w0[:], nn[:], ALU.subtract))
            then(dve.tensor_tensor(weight[:], weight[:], rz[:, P:2 * P], ALU.mult))
            then(dve.tensor_tensor(weight[:], weight[:], nn[:], ALU.add))
            then(dve.tensor_reduce(ssum[:], weight[:], AX, ALU.add))
            then(dve.tensor_scalar(ssum[:], ssum[:], -1.0 / P, None, ALU.mult))
            then(dve.tensor_copy(W.gru[:], weight[:]))
            then(dve.tensor_scalar(weight[:], weight[:], ssum[:, 0:1], -1.0 / P, ALU.add, ALU.add))
            then(dve.tensor_tensor(W.gru_dense[:], weight[:], W.ident[:], ALU.add))


class FeedForward:

    TURN, COPY, HIDDEN, GELU, PRODUCT, SQUARE, SUM, SCALE, JOIN, MOMENTS, LAST, STEPS = range(12)

    def __init__(self, mem, name, S, W, norm, j, last, jl, bank_wide, bank_rows, n, nT, h, y3, x, out):
        self.n, self.nT, self.h, self.y3, self.x, self.out = n, nT, h, y3, x, out
        self.S, self.W, self.norm, self.j, self.last, self.jl = S, W, norm, j, last, jl
        self.bw, self.br = bank_wide, bank_rows
        self.turned, self.copied, self.hidden, self.gelued, self.rows_made, self.joined, self.added = (
            mem.sems(name + "_" + n, S)
            for n in ("turned", "copied", "hidden", "gelued", "rows_made", "joined", "added"))

    def pe(self, pe, k, s, i):
        W = self.W
        if k == self.TURN:
            wait(pe, self.norm.normed[s], self.norm.nth(i, self.j))
            transpose_tiles(pe, self.bw[s], self.n[s], W.ident).then_inc(self.turned[s], 1)
        if k == self.HIDDEN:
            wait(pe, self.copied[s], i + 1)
            pe.matmul(self.bw[s][:], W.w1_ffn[:], self.nT[s][:], start=True, stop=True).then_inc(self.hidden[s], 1)
            const_rows(pe, self.br[s], W, C_FFN)
            rows_matmul(pe, self.br[s], self.nT[s], W.g1c[:])
        if k == self.PRODUCT:
            wait(pe, self.gelued[s], i + 1)
            rows_matmul(pe, self.br[s], self.h[s], W.w2_ffn[:], stop=True).then_inc(self.rows_made[s], 1)

    def act(self, act, k, s, i):
        if k == self.COPY:
            wait(act, self.turned[s], i + 1)
            act.copy(self.nT[s][:], self.bw[s][:]).then_inc(self.copied[s], 1)
        if k == self.GELU:
            wait(act, self.hidden[s], i + 1)
            act.activation(self.h[s][:], self.bw[s][:], ACT.Gelu, bias=self.W.b1_ffn[:, 0:1]).then_inc(self.gelued[s], 1)
        if k == self.SQUARE:
            wait(act, self.rows_made[s], i + 1)
            self.norm.square(act, i, s, self.j + 1, tiles(self.br[s][:]))

    def dve(self, dve, k, s, i):
        if k == self.SUM:
            self.norm.sums(dve, i, s, self.j + 1)
        if k == self.SCALE:
            wait(dve, self.norm.rooted[s], self.norm.nth(i, self.j + 1))
            for t in range(TPG):
                c = slice(t * P, (t + 1) * P)
                ins = dve.scalar_tensor_tensor(self.n[s][:, c], self.br[s][:, c], self.norm.rstd[s][:, t:t + 1],
                                               self.W.g2[:], ALU.mult, ALU.mult)
            ins.then_inc(self.norm.normed[s], 1)
        if k == self.JOIN:
            wait(dve, self.added[s], i + 1)
            wait(dve, self.norm.normed[s], self.norm.nth(i, self.j + 1))
            dve.tensor_tensor(self.y3[s][:], self.n[s][:], self.x[s][:], ALU.add).then_inc(self.joined[s], 1)
        if k == self.MOMENTS:
            wait(dve, self.joined[s], i + 1)
            self.last.moments(dve, i, s, self.y3[s])
        if k == self.LAST:
            self.last.scale_moments(dve, i, s, self.jl, self.out[s], self.y3[s])

    def pool(self, pool, k, s, i):
        if k == self.SUM:
            self.norm.root(pool, i, s, self.j + 1, self.W.minus_half)
        if k == self.MOMENTS:
            self.last.root(pool, i, s, self.jl, self.W.minus_half)


def dense_pass(nc, A, D, W, Ed, plan):
    S, N, DG = plan.DS, plan.N, plan.DG
    mem = Mem(nc)
    sb4 = lambda n: [mem.sb(f"d_{n}{s}", [P, GROUP]) for s in range(S)]
    x, xT, x1, x2, y, x2b, x3, x4 = (sb4(n) for n in ("x", "xT", "x1", "x2", "y", "x2b", "x3", "x4"))
    bank_wide = [mem.ps(f"d_wide{s}") for s in range(S)]
    bank_rows = [mem.ps(f"d_rows{s}") for s in range(S)]
    norm = Norm(mem, "dn", S, 5)
    last = Norm(Mem(nc), "dl", S, 1, squares=False, stats=True)
    ff = FeedForward(mem, "df", S, W, norm, 2, last, 0, bank_wide, bank_rows,
                     sb4("n"), sb4("nT"), sb4("h"), sb4("y3"), x=x2b, out=x3)
    names = ("loaded", "turned", "copied", "rows_made", "residual", "hidden", "relued", "st1", "st2", "st3", "st4", "biased")
    sem = {n: mem.sems("d_" + n, S) for n in names}
    loaded, turned, copied, rows_made, residual, hidden, relued, st1, st2, st3, st4, biased = (sem[n] for n in names)
    began = mem.sem("d_began")
    rounds = DG // S
    LAYER0 = 0
    LAYER1 = LAYER0 + 6
    BIAS = LAYER1 + 6
    SUM2, SCALE2 = BIAS + 1, BIAS + 2
    FF = SCALE2 + 1
    TURN3 = FF + ff.STEPS
    COPY3, HIDDEN, RELU, PRODUCT, RESIDUAL, SQUARE4, SUM4, SCALE4, STEPS = range(TURN3 + 1, TURN3 + 10)
    LAG = (0, 6, 17, 23)
    look = Lookup(mem, "dk", Ed.src0, D["node_row"], plan.LOOKUPS)
    look_at = [1 + q * (STEPS - 3) // plan.LOOKUPS for q in range(plan.LOOKUPS)]

    def part(ap, g):
        parts = P
        if isinstance(g, int) and g >= plan.NF:
            parts = max(0, (N - g * GROUP) // TPG)
        return bass.AP(tensor=ap.tensor, offset=g * GROUP * P, ap=[[TPG * P, parts], [1, TPG * P]]), parts

    with nc.Block() as block:
        @block.sync
        def _(sp):
            t1, t2, t3 = (groups_of(D[f"x{k}"]) for k in (1, 2, 3))

            def load(s, g):
                src, parts = part(A["x"], g)
                if parts == 0:
                    src, parts = part(A["x"], 0)
                sp.dma_start(x[s][0:parts, :], src).then_inc(loaded[s], 16)

            def step(k, s, i):
                g = i * S + s
                if k == LAYER0 + 1 and another(i, rounds):
                    wait(sp, turned[s], i * 3 + 1)
                    load(s, g + S)
                if k == LAYER0 + 5:
                    wait(sp, norm.normed[s], norm.nth(i, 0))
                    sp.dma_start(t1[g], x1[s][:]).then_inc(st1[s], 16)
                if k == LAYER1 + 5:
                    wait(sp, norm.normed[s], norm.nth(i, 1))
                    sp.dma_start(t2[g], x2[s][:]).then_inc(st2[s], 16)
                if k == FF + ff.LAST:
                    wait(sp, last.normed[s], i + 1)
                    sp.dma_start(t3[g], x3[s][:]).then_inc(st3[s], 16)
                if k == SCALE4:
                    wait(sp, norm.normed[s], norm.nth(i, 4))
                    dst, parts = part(D["out"], g)
                    if parts:
                        sp.dma_start(dst, x4[s][0:parts, :]).then_inc(st4[s], 16)

            for s in range(S):
                load(s, s)
            in_turns(sp, rounds, LAG, STEPS, step, tail=2)
            for s in range(S):
                for st in (st1, st2, st3):
                    sp.wait_ge(st[s], 16 * rounds)
                sp.wait_ge(st4[s], 16 * (rounds - 1 if ((rounds - 1) * S + s) * GROUP >= N else rounds))

        @block.tensor
        def _(pe):
            def step(k, s, i):
                if k == LAYER0:
                    wait(pe, loaded[s], 16 * i + 16)
                    transpose_tiles(pe, bank_wide[s], x[s], W.ident).then_inc(turned[s], 1)
                if k == LAYER0 + 2:
                    wait(pe, copied[s], 3 * i + 1)
                    wait(pe, residual[s], i)
                    rows_matmul(pe, bank_rows[s], xT[s], W.gru_dense[:], start=True, stop=True).then_inc(rows_made[s], 1)
                if k == LAYER1:
                    wait(pe, norm.normed[s], norm.nth(i, 0))
                    transpose_tiles(pe, bank_wide[s], x1[s], W.ident).then_inc(turned[s], 1)
                if k == LAYER1 + 2:
                    wait(pe, copied[s], 3 * i + 2)
                    const_rows(pe, bank_rows[s], W, C_PNA_DENSE)
                    rows_matmul(pe, bank_rows[s], xT[s], W.pna_dense[:], stop=True).then_inc(rows_made[s], 1)
                ff.pe(pe, k - FF, s, i)
                if k == TURN3:
                    wait(pe, last.normed[s], i + 1)
                    transpose_tiles(pe, bank_wide[s], x3[s], W.ident).then_inc(turned[s], 1)
                if k == HIDDEN:
                    wait(pe, copied[s], 3 * i + 3)
                    pe.matmul(bank_wide[s][:], W.w1a[:], xT[s][:], start=True, stop=True).then_inc(hidden[s], 1)
                if k == PRODUCT:
                    const_rows(pe, bank_rows[s], W, C_MSG)
                    wait(pe, relued[s], i + 1)
                    rows_matmul(pe, bank_rows[s], ff.h[s], W.w2_msg[:], stop=True).then_inc(rows_made[s], 1)

            in_turns(pe, rounds, LAG, STEPS, step)

        @block.scalar
        def _(act):
            def step(k, s, i):
                for j, copy in enumerate((LAYER0 + 1, LAYER1 + 1, COPY3)):
                    if k == copy:
                        wait(act, turned[s], 3 * i + j + 1)
                        act.copy(xT[s][:], bank_wide[s][:]).then_inc(copied[s], 1)
                for j, square in enumerate((LAYER0 + 3, LAYER1 + 3)):
                    if k == square:
                        wait(act, rows_made[s], 3 * i + j + 1)
                        norm.square(act, i, s, j, tiles(bank_rows[s][:]))
                if k == LAYER0 + 5:
                    wait(act, st1[s], 16 * i)
                    norm.scale_by_scalar(act, i, s, 0, x1[s], bank_rows[s])
                if k == BIAS:
                    wait(act, biased[s], i + 1)
                    norm.square(act, i, s, 2, tiles(y[s][:]))
                ff.act(act, k - FF, s, i)
                if k == RELU:
                    wait(act, hidden[s], i + 1)
                    act.activation(ff.h[s][:], bank_wide[s][:], ACT.Relu, bias=W.cols[:, B1_MSG:B1_MSG + 1]).then_inc(relued[s], 1)
                if k == SQUARE4:
                    wait(act, residual[s], i + 1)
                    norm.square(act, i, s, 4, tiles(y[s][:]))
                if k == SCALE4:
                    wait(act, residual[s], i + 1)
                    wait(act, st4[s], 16 * i)
                    norm.scale_by_scalar(act, i, s, 4, x4[s], y[s])

            in_turns(act, rounds, LAG, STEPS, step)

        @block.gpsimd
        def _(pool):
            def step(k, s, i):
                if s == 0:
                    if k == 0:
                        look.begin(pool, i, i * plan.LOOKUPS, 3)
                    for t in range(plan.LOOKUPS):
                        if k == look_at[t]:
                            look.fetch(pool, t)
                    if k == STEPS - 1:
                        look.take(pool, i, i * plan.LOOKUPS, Ed.src, Ed.coef)
                for j, sum_ in enumerate((LAYER0 + 4, LAYER1 + 4, SUM2)):
                    if k == sum_:
                        norm.root(pool, i, s, j, W.minus_half)
                if k == BIAS:
                    wait(pool, norm.normed[s], norm.nth(i, 1))
                    pool.tensor_tensor(tiles(y[s][:]), tiles(x2[s][:]), each(W.bo[:], TPG), ALU.add).then_inc(biased[s], 1)
                if k == SCALE2:
                    pool.tensor_tensor(tiles(x2b[s][:]), tiles(x2[s][:]), each(W.be2[:], TPG), ALU.add).then_inc(ff.added[s], 1)
                ff.pool(pool, k - FF, s, i)
                if k == SUM4:
                    norm.root(pool, i, s, 4, W.minus_half)

            in_turns(pool, rounds, LAG, STEPS, step)

        @block.vector
        def _(dve):
            norm.set_eps(dve, began)
            dve.wait_ge(began, S)

            def step(k, s, i):
                for j, layer, out, stored in ((0, LAYER0, x1, st1), (1, LAYER1, x2, st2)):
                    if k == layer + 4:
                        norm.sums(dve, i, s, j)
                    if k == layer + 5 and j:
                        wait(dve, stored[s], 16 * i)
                        norm.scale(dve, i, s, j, out[s][:], bank_rows[s][:])
                if k == SUM2:
                    norm.sums(dve, i, s, 2)
                if k == SCALE2:
                    norm.scale(dve, i, s, 2, ff.n[s][:], y[s][:])
                if k == FF + ff.LAST:
                    wait(dve, st3[s], 16 * i)
                ff.dve(dve, k - FF, s, i)
                if k == RESIDUAL:
                    wait(dve, rows_made[s], 3 * i + 3)
                    dve.tensor_tensor(y[s][:], bank_rows[s][:], x3[s][:], ALU.add).then_inc(residual[s], 1)
                if k == SUM4:
                    norm.sums(dve, i, s, 4)

            in_turns(dve, rounds, LAG, STEPS, step)

class Gather:

    def __init__(self, mem, name, S, index, table, rows):
        self.index, self.table, self.rows, self.mem = index, table, rows, mem
        self.slot = [mem.sb(f"{name}_slot{s}", [P, TPG], I32) for s in range(S)]
        self.slotted = mem.sems(name + "_slotted", S)
        self.landed = mem.sems(name + "_landed", S)

    def begin(self, pool, i, s, g):
        pool.tensor_copy(self.slot[s][:], self.index[:, bass.ds(g * TPG, TPG)]).then_inc(self.slotted[s], 1)
        wait(pool, self.slotted[s], i + 1)
        self.mem.settle(pool)

    def tile(self, pool, s, t):
        pool.indirect_dma_start(
            out=self.rows[s][:, t * P:(t + 1) * P], out_offset=None, in_=self.table,
            in_offset=bass.IndirectOffsetOnAxis(ap=self.slot[s][:, t:t + 1], axis=0),
        ).then_inc(self.landed[s], 16)

    def fetch(self, pool, i, s, g):
        self.begin(pool, i, s, g)
        for t in range(TPG):
            self.tile(pool, s, t)

    def arrived(self, eng, i, s):
        wait(eng, self.landed[s], (i + 1) * 16 * TPG)


def tok(ap, g):
    return over(ap[:, bass.ds(g * TPG, TPG)], P)


def pos(ap, g):
    return ap[:, bass.ds(g * GROUP, GROUP)]


def gcn_edges(nc, A, D, W, Ed, plan):
    S, rounds = plan.ES, plan.EG // plan.ES
    mem = Mem(nc)
    rows = lambda n: [mem.sb(f"g_{n}{s}", [P, GROUP]) for s in range(S)]
    src, own, x0, scaled, ownd, run, u, y, x1 = (rows(n) for n in ("src", "own", "x0", "scaled", "ownd", "run", "u", "y", "x1"))
    bank_src, bank_own, bank_out = ([mem.ps(f"g_{n}{s}") for s in range(S)] for n in ("bsrc", "bown", "bout"))
    last = Norm(Mem(nc), "gl", S, 1, squares=False, stats=True, by_scalar=True)
    gsrc = Gather(mem, "gs", S, Ed.src0, A["x"], src)
    gown = Gather(mem, "go", S, Ed.dst0, A["x"], own)
    copied, weighted, turned, scanned, summed, made, mixed, masked, stored = (
        mem.sems("g_" + n, S) for n in ("copied", "weighted", "turned", "scanned", "summed", "made", "mixed", "masked", "stored"))
    began, padded = mem.sem("g_began"), mem.sem("g_padded")
    table = groups_of(D["x1"])
    WEIGH, TURN, SCAN, SUM, PRODUCT, OUTER, ADD, MOMENTS, SCALE, STEPS = range(10)
    AHEAD = TURN
    LAG = (0, 4)

    with nc.Block() as block:
        @block.gpsimd
        def _(pool):
            for s in range(S):
                gsrc.fetch(pool, 0, s, s)
                gown.fetch(pool, 0, s, s)

            def step(k, s, i):
                if another(i, rounds):
                    if k == AHEAD:
                        wait(pool, weighted[s], 2 * i + 2)
                        gsrc.begin(pool, i + 1, s, (i + 1) * S + s)
                    if k == AHEAD + TPG:
                        wait(pool, copied[s], i + 1)
                        gown.begin(pool, i + 1, s, (i + 1) * S + s)
                    for n, gather in enumerate((gsrc, gown)):
                        if 0 <= k - AHEAD - n * TPG < TPG:
                            gather.tile(pool, s, k - AHEAD - n * TPG)

            in_turns(pool, rounds, LAG, STEPS, step, tail=1)

        @block.scalar
        def _(act):
            def step(k, s, i):
                if k == WEIGH:
                    gown.arrived(act, i, s)
                    wait(act, mixed[s], 2 * i)
                    act.copy(x0[s][:], own[s][:]).then_inc(copied[s], 1)
                if k == MOMENTS:
                    last.root_by_scalar(act, i, s, 0)

            in_turns(act, rounds, LAG, STEPS, step)

        @block.vector
        def _(dve):
            dve.memset(run[S - 1][:], 0.0).then_inc(began, 1)
            dve.wait_ge(began, 1)

            def step(k, s, i):
                g = i * S + s
                if k == WEIGH:
                    gsrc.arrived(dve, i, s)
                    dve.tensor_tensor(tiles(scaled[s][:]), tiles(src[s][:]), tok(Ed.coef, g), ALU.mult).then_inc(weighted[s], 1)
                    gown.arrived(dve, i, s)
                    dve.tensor_tensor(tiles(ownd[s][:]), tiles(own[s][:]), tok(Ed.dinv, g), ALU.mult).then_inc(weighted[s], 1)
                if k == SCAN:
                    wait(dve, masked[s], 32 * i + 32)
                    wait(dve, turned[s], i + 1)
                    wait(dve, scanned[s - 1], i + 1 if s else i)
                    dve.tensor_tensor_scan(run[s][:], pos(Ed.keep, g), bank_src[s][:], run[s - 1][:, GROUP - 1:GROUP],
                                           ALU.mult, ALU.add).then_inc(scanned[s], 1)
                if k == SUM:
                    wait(dve, scanned[s], i + 1)
                    dve.tensor_tensor(u[s][:], run[s][:], bank_own[s][:], ALU.add).then_inc(summed[s], 1)
                if k == OUTER:
                    wait(dve, made[s], i + 1)
                    dve.tensor_tensor(tiles(y[s][:]), tiles(bank_out[s][:]), tok(Ed.dinv, g), ALU.mult).then_inc(mixed[s], 1)
                if k == ADD:
                    wait(dve, mixed[s], 2 * i + 1)
                    wait(dve, copied[s], i + 1)
                    dve.tensor_tensor(y[s][:], y[s][:], x0[s][:], ALU.add).then_inc(mixed[s], 1)
                if k == MOMENTS:
                    wait(dve, mixed[s], 2 * i + 2)
                    last.moments(dve, i, s, y[s])
                if k == SCALE:
                    wait(dve, stored[s], 16 * i)
                    last.scale_moments(dve, i, s, 0, x1[s], y[s])

            in_turns(dve, rounds, LAG, STEPS, step)

        @block.tensor
        def _(pe):
            def step(k, s, i):
                if k == TURN:
                    wait(pe, weighted[s], 2 * i + 2)
                    wait(pe, summed[s], i)
                    transpose_tiles(pe, bank_src[s], scaled[s], W.ident)
                    transpose_tiles(pe, bank_own[s], ownd[s], W.ident).then_inc(turned[s], 1)
                if k == PRODUCT:
                    wait(pe, summed[s], i + 1)
                    wait(pe, mixed[s], 2 * i)
                    rows_matmul(pe, bank_out[s], u[s], W.gru[:], start=True, stop=True).then_inc(made[s], 1)

            in_turns(pe, rounds, LAG, STEPS, step)

        @block.sync
        def _(sp):
            def step(k, s, i):
                g = i * S + s
                if k == WEIGH:
                    for mask, row in ((Ed.keep, D["keep"]), (Ed.low, D["low"])):
                        sp.dma_start(pos(mask, g), row[bass.ds(g, 1), :].to_broadcast([P, GROUP])).then_inc(masked[s], 16)
                if k == SCALE:
                    wait(sp, last.normed[s], i + 1)
                    sp.dma_start(table[g + plan.DG], x1[s][:]).then_inc(stored[s], 16)

            in_turns(sp, rounds, LAG, STEPS, step)
            if plan.AG > plan.EG:
                for g in range(plan.EG, plan.AG):
                    sp.dma_start(pos(Ed.low, g), D["low"][g:g + 1, :].to_broadcast([P, GROUP])).then_inc(padded, 16)
                sp.wait_ge(padded, 16 * (plan.AG - plan.EG))
            for s in range(S):
                sp.wait_ge(stored[s], 16 * rounds)


def pna_edges(nc, A, D, W, Ed, plan):
    S, rounds = plan.ES, plan.EG // plan.ES
    mem = Mem(nc)
    rows = lambda n: [mem.sb(f"p_{n}{s}", [P, GROUP]) for s in range(S)]
    src, own, srcT, ownT, neg, sqr, rc = (rows(n) for n in ("src", "own", "srcT", "ownT", "neg", "sqr", "rc"))
    mx, mn, s1, s2, mean, var = (rows(n) for n in ("mx", "mn", "s1", "s2", "mean", "var"))
    y, x2 = (rows(n) for n in ("y", "x2"))
    m2, std, ya = sqr, var, neg
    bank = [[mem.ps(f"p_b{s}{k}") for k in range(4)] for s in range(S)]
    norm = Norm(mem, "pn", S, 1)
    gsrc = Gather(mem, "pg", S, Ed.src, D["x1"], src)
    look = [Lookup(mem, f"pk{s}", Ed.dst0, D["node_row"], TPG) for s in range(S)]
    (turned, copied, made, negated, squared, scanned, averaged, m2_made, var_made, rooted, mixed,
     loaded, stored) = (mem.sems("p_" + n, S) for n in (
        "turned", "copied", "made", "negated", "squared", "scanned", "averaged", "m2_made", "var_made", "rooted",
        "mixed", "loaded", "stored"))
    sums_made, counted = mem.sems("p_sums_made", S), mem.sems("p_counted", S)
    began = mem.sem("p_began")
    tin, tout = groups_of(D["x1"]), groups_of(D["x2"])
    TURN = 0
    (COPY, SOURCE, OWN, SCAN, MEAN, EXTREMES, SUBTRACT, CLAMP, ROOT, DEVIATION, SCALERS, ADD, ADD2, SQUARE, SUM,
     SCALE, STEPS) = range(TURN + 1, TURN + 18)
    AHEAD, LOOK = (COPY, SOURCE, SCAN, EXTREMES), (OWN, MEAN, SUBTRACT, CLAMP)
    LAG = (0, 6)

    with nc.Block() as block:
        @block.sync
        def _(sp):
            def load_own(s, i):
                sp.dma_start(own[s][:], tin[i * S + s + plan.DG]).then_inc(loaded[s], 16)

            def load_counts(s, i):
                sp.dma_start(rc[s][:], D["rcount"][bass.ds(i * S + s, 1), :].to_broadcast([P, GROUP])).then_inc(counted[s], 16)

            for s in range(S):
                load_own(s, 0)
                load_counts(s, 0)

            def step(k, s, i):
                if k == COPY and another(i, rounds):
                    wait(sp, turned[s], 2 * i + 2)
                    load_own(s, i + 1)
                if k == SUBTRACT and another(i, rounds):
                    wait(sp, averaged[s], 2 * i + 2)
                    load_counts(s, i + 1)
                if k == SCALE:
                    wait(sp, norm.normed[s], i + 1)
                    sp.dma_start(tout[i * S + s + plan.DG], x2[s][:]).then_inc(stored[s], 16)

            in_turns(sp, rounds, LAG, STEPS, step, tail=1)
            for s in range(S):
                sp.wait_ge(stored[s], 16 * rounds)

        @block.gpsimd
        def _(pool):
            if plan.AG > plan.EG:
                pool.memset(Ed.dst[:, plan.EG * TPG:], 0)
            for s in range(S):
                gsrc.fetch(pool, 0, s, s)

            def step(k, s, i):
                if k in AHEAD and another(i, rounds):
                    if k == AHEAD[0]:
                        wait(pool, turned[s], 2 * i + 1)
                        gsrc.begin(pool, i + 1, s, (i + 1) * S + s)
                    gsrc.tile(pool, s, AHEAD.index(k))
                if k in LOOK:
                    if k == LOOK[0]:
                        look[s].begin(pool, i, (i * S + s) * TPG, 2)
                    look[s].fetch(pool, LOOK.index(k))
                if k == SUM:
                    norm.root(pool, i, s, 0, W.minus_half)
                    look[s].take(pool, i, (i * S + s) * TPG, Ed.dst)

            in_turns(pool, rounds, LAG, STEPS, step, tail=1)

        @block.tensor
        def _(pe):
            def products(s, n, cols, stop=False):
                for k in range(3):
                    mm = rows_matmul(pe, bank[s][1 + k], cols[s], W.post[:, 1 + 4 * k + n, :], stop=stop)
                return mm

            def step(k, s, i):
                if k == TURN:
                    gsrc.arrived(pe, i, s)
                    wait(pe, mixed[s], 4 * i)
                    transpose_tiles(pe, bank[s][0], src[s], W.ident).then_inc(turned[s], 1)
                    wait(pe, loaded[s], 16 * i + 16)
                    transpose_tiles(pe, bank[s][1], own[s], W.ident).then_inc(turned[s], 1)
                if k == SOURCE:
                    wait(pe, copied[s], 2 * i + 1)
                    pe.matmul(bank[s][0][:], W.pna_src[:], srcT[s][:], start=True, stop=True).then_inc(made[s], 1)
                if k == OWN:
                    wait(pe, copied[s], 2 * i + 2)
                    for b in range(3):
                        const_rows(pe, bank[s][1 + b], W, C_PNA + b)
                        rows_matmul(pe, bank[s][1 + b], ownT[s], W.own[:, b, :])
                if k == EXTREMES:
                    wait(pe, scanned[s], 4 * i + 4)
                    products(s, 0, mx)
                    products(s, 1, mn)
                if k == SUBTRACT:
                    wait(pe, averaged[s], 2 * i + 1)
                    products(s, 2, mean)
                if k == DEVIATION:
                    wait(pe, rooted[s], i + 1)
                    products(s, 3, std, stop=True).then_inc(sums_made[s], 1)

            in_turns(pe, rounds, LAG, STEPS, step)

        @block.scalar
        def _(act):
            def step(k, s, i):
                if k == COPY:
                    wait(act, turned[s], 2 * i + 1)
                    act.copy(srcT[s][:], bank[s][0][:]).then_inc(copied[s], 1)
                    wait(act, turned[s], 2 * i + 2)
                    act.copy(ownT[s][:], bank[s][1][:]).then_inc(copied[s], 1)
                if k == OWN:
                    wait(act, made[s], i + 1)
                    act.activation(sqr[s][:], bank[s][0][:], ACT.Square).then_inc(squared[s], 1)
                    act.activation(neg[s][:], bank[s][0][:], ACT.Copy, scale=-1.0).then_inc(negated[s], 1)
                if k == EXTREMES:
                    wait(act, averaged[s], 2 * i + 1)
                    act.activation(m2[s][:], mean[s][:], ACT.Square).then_inc(m2_made[s], 1)
                if k == ROOT:
                    wait(act, var_made[s], 2 * i + 2)
                    act.activation(std[s][:], var[s][:], ACT.Sqrt).then_inc(rooted[s], 1)
                if k == SQUARE:
                    wait(act, mixed[s], 4 * i + 4)
                    norm.square(act, i, s, 0, tiles(y[s][:]))

            in_turns(act, rounds, LAG, STEPS, step)

        @block.vector
        def _(dve):
            norm.set_eps(dve, began)
            for k, rows_ in enumerate((mx, mn, s1, s2)):
                dve.memset(rows_[S - 1][:], 0.0).then_inc(began, 1)
            dve.wait_ge(began, S + 4)
            end = slice(GROUP - 1, GROUP)

            def step(k, s, i):
                g = i * S + s
                if k == SCAN:
                    wait(dve, made[s], i + 1)
                    wait(dve, squared[s], i + 1)
                    wait(dve, negated[s], i + 1)
                    wait(dve, scanned[s - 1], 4 * (i + 1 if s else i))
                    dve.tensor_tensor_scan(s1[s][:], pos(Ed.keep, g), bank[s][0][:], s1[s - 1][:, end], ALU.mult, ALU.add).then_inc(scanned[s], 1)
                    dve.tensor_tensor_scan(mx[s][:], pos(Ed.low, g), bank[s][0][:], mx[s - 1][:, end], ALU.add, ALU.max).then_inc(scanned[s], 1)
                    dve.tensor_tensor_scan(s2[s][:], pos(Ed.keep, g), sqr[s][:], s2[s - 1][:, end], ALU.mult, ALU.add).then_inc(scanned[s], 1)
                    dve.tensor_tensor_scan(mn[s][:], pos(Ed.low, g), neg[s][:], mn[s - 1][:, end], ALU.add, ALU.max).then_inc(scanned[s], 1)
                if k == MEAN:
                    wait(dve, counted[s], 16 * i + 16)
                    wait(dve, scanned[s], 4 * i + 4)
                    dve.tensor_tensor(mean[s][:], s1[s][:], rc[s][:], ALU.mult).then_inc(averaged[s], 1)
                    dve.tensor_tensor(var[s][:], s2[s][:], rc[s][:], ALU.mult).then_inc(averaged[s], 1)
                if k == SUBTRACT:
                    wait(dve, averaged[s], 2 * i + 2)
                    wait(dve, m2_made[s], i + 1)
                    dve.tensor_tensor(var[s][:], var[s][:], m2[s][:], ALU.subtract).then_inc(var_made[s], 1)
                if k == CLAMP:
                    wait(dve, var_made[s], 2 * i + 1)
                    dve.tensor_scalar(var[s][:], var[s][:], 0.0, EPS, ALU.max, ALU.add).then_inc(var_made[s], 1)
                if k == SCALERS:
                    wait(dve, sums_made[s], i + 1)
                    dve.tensor_tensor(tiles(ya[s][:]), tiles(bank[s][2][:]), tok(Ed.amp, g), ALU.mult).then_inc(mixed[s], 1)
                    dve.tensor_tensor(tiles(y[s][:]), tiles(bank[s][3][:]), tok(Ed.att, g), ALU.mult).then_inc(mixed[s], 1)
                if k == ADD:
                    wait(dve, mixed[s], 4 * i + 2)
                    dve.tensor_tensor(ya[s][:], ya[s][:], bank[s][1][:], ALU.add).then_inc(mixed[s], 1)
                if k == ADD2:
                    wait(dve, mixed[s], 4 * i + 3)
                    dve.tensor_tensor(y[s][:], y[s][:], ya[s][:], ALU.add).then_inc(mixed[s], 1)
                if k == SUM:
                    norm.sums(dve, i, s, 0)
                if k == SCALE:
                    wait(dve, mixed[s], 4 * i + 4)
                    wait(dve, stored[s], 16 * i)
                    norm.scale(dve, i, s, 0, x2[s][:], y[s][:])

            in_turns(dve, rounds, LAG, STEPS, step)


def attention_edges(nc, A, D, W, Ed, plan):
    S, rounds = plan.AS, plan.A_ROUNDS
    mem = Mem(nc)
    rows = lambda n: [mem.sb(f"a_{n}{s}", [P, GROUP]) for s in range(S)]
    src, own, srcT, ownT, q, qk = (rows(n) for n in ("src", "own", "srcT", "ownT", "q", "qk"))
    fade, prob, pv, den, acc, x2b = (rows(n) for n in ("fade", "prob", "pv", "den", "acc", "x2b"))
    o, y, x3 = q, qk, pv
    m = [mem.sb(f"a_m{s}", [P, GROUP + 1]) for s in range(S)]
    typ = [mem.sb(f"a_typ{s}", [3 * TYPES, GROUP], I32) for s in range(S)]
    hot = [mem.sb(f"a_hot{s}", [3 * TYPES, GROUP], BF16) for s in range(S)]
    v = srcT
    wide, sums = [mem.ps(f"a_wide{s}") for s in range(S)], [mem.ps(f"a_sums{s}") for s in range(S)]
    norm = Norm(mem, "an", S, 2)
    last = Norm(Mem(nc), "al", S, 1, squares=False, stats=True)
    ff = FeedForward(mem, "af", S, W, norm, 0, last, 0, wide, sums,
                     n=prob, nT=srcT, h=ownT, y3=fade, x=x2b, out=x3)
    gsrc = Gather(mem, "as", S, Ed.src, D["x2"], src)
    gown = Gather(mem, "ao", S, Ed.dst, D["x2"], own)
    (turned, copied, q_made, q_moved, k_made, v_made, v_moved, matched, hot_made, logits, peaked, differed, exped, valued,
     scanned, divided, out_made, residual, loaded, stored) = (mem.sems("a_" + n, S) for n in (
        "turned", "copied", "q_made", "q_moved", "k_made", "v_made", "v_moved", "matched", "hot_made", "logits", "peaked", "differed",
        "exped", "valued", "scanned", "divided", "out_made", "residual", "loaded", "stored"))
    wide_inv, widened = qk, mem.sems("a_widened", S)
    den_turned, inverted, spread = mem.sems("a_den_turned", S), mem.sems("a_inverted", S), mem.sems("a_spread", S)
    inv = [mem.sb(f"a_inv{s}", [P, TPG * HEADS]) for s in range(S)]
    began = mem.sem("a_began")
    tout = groups_of(D["x3"])
    BQc, BKc, BVc = (W.cols[:, k:k + 1] for k in (BQ, BK, BV))
    (TURN, COPY, PROJECT, MOVE, MATCH, LOGITS, PEAK, DIFFER, FADE, EXP, ACCUMULATE, VALUES, INVERT, WIDEN, SPREAD,
     DIVIDE, PRODUCT, RESIDUAL, SQUARE, SUM, SCALE, FF) = range(22)
    STEPS = FF + ff.STEPS
    AHEAD_SRC, AHEAD_OWN = range(PROJECT, PROJECT + 3 * TPG, 3), range(SPREAD + 1, SPREAD + 1 + 3 * TPG, 3)
    LAG = (0, 8, 14)

    with nc.Block() as block:
        @block.sync
        def _(sp):
            def load(s, i):
                sp.dma_start(typ[s][:], A["type_row"][bass.ds(i * S + s, 1), :].to_broadcast([3 * TYPES, GROUP])).then_inc(loaded[s], 16)

            for s in range(S):
                load(s, 0)

            def step(k, s, i):
                if k == COPY and another(i, rounds):
                    wait(sp, hot_made[s], i + 1)
                    load(s, i + 1)
                if k == FF + ff.LAST:
                    wait(sp, last.normed[s], i + 1)
                    sp.dma_start(tout[i * S + s + plan.DG], x3[s][:]).then_inc(stored[s], 16)

            in_turns(sp, rounds, LAG, STEPS, step, tail=1)
            for s in range(S):
                sp.wait_ge(stored[s], 16 * rounds)

        @block.gpsimd
        def _(pool):
            for s in range(S):
                gsrc.fetch(pool, 0, s, s)
                gown.fetch(pool, 0, s, s)

            def step(k, s, i):
                for gather, ahead in ((gsrc, AHEAD_SRC), (gown, AHEAD_OWN)):
                    if k in ahead and another(i, rounds):
                        if k == ahead[0]:
                            wait(pool, turned[s], 2 * i + 2)
                            wait(pool, ff.added[s], i + 1)
                            gather.begin(pool, i + 1, s, (i + 1) * S + s)
                        gather.tile(pool, s, ahead.index(k))
                if k == COPY:
                    gown.arrived(pool, i, s)
                    wait(pool, ff.joined[s], i)
                    pool.tensor_tensor(tiles(x2b[s][:]), tiles(own[s][:]), each(W.be2[:], TPG), ALU.add).then_inc(ff.added[s], 1)
                if k == SUM:
                    norm.root(pool, i, s, 0, W.minus_half)
                ff.pool(pool, k - FF, s, i)

            in_turns(pool, rounds, LAG, STEPS, step, tail=1)

        @block.tensor
        def _(pe):
            def step(k, s, i):
                if k == TURN:
                    gsrc.arrived(pe, i, s)
                    wait(pe, norm.normed[s], 2 * i)
                    transpose_tiles(pe, wide[s], src[s], W.ident).then_inc(turned[s], 1)
                    gown.arrived(pe, i, s)
                    transpose_tiles(pe, sums[s], own[s], W.ident).then_inc(turned[s], 1)
                if k == PROJECT:
                    wait(pe, copied[s], 2 * i + 2)
                    pe.matmul(sums[s][:], W.wq[:], ownT[s][:], start=True, stop=True).then_inc(q_made[s], 1)
                    pe.matmul(wide[s][:], W.wk[:], srcT[s][:], start=True, stop=True).then_inc(k_made[s], 1)
                if k == MATCH:
                    wait(pe, q_moved[s], i + 1)
                    pe.matmul(sums[s][:], W.wv[:], srcT[s][:], start=True, stop=True).then_inc(v_made[s], 1)
                if k == LOGITS:
                    wait(pe, hot_made[s], i + 1)
                    wait(pe, matched[s], i + 1)
                    pe.matmul(wide[s][:], W.head_bias[:], hot[s][:], start=True, stop=False)
                    pe.matmul(wide[s][:], W.heads[:], qk[s][:], start=False, stop=True).then_inc(logits[s], 1)
                if k == VALUES:
                    wait(pe, scanned[s], 2 * i + 1)
                    for t in range(TPG):
                        mm = pe.matmul(wide[s][:, t * HEADS:(t + 1) * HEADS], den[s][:, t:GROUP:TPG], W.ident[:, 0:P:P // HEADS],
                                       start=True, stop=True)
                    mm.then_inc(den_turned[s], 1)
                if k == SPREAD:
                    wait(pe, widened[s], i + 1)
                    for t in range(TPG):
                        mm = pe.transpose(wide[s][:, t:GROUP:TPG], wide_inv[s][:, t * P:(t + 1) * P], W.ident[:])
                    mm.then_inc(spread[s], 1)
                if k == PRODUCT:
                    const_rows(pe, sums[s], W, C_WO)
                    wait(pe, divided[s], i + 1)
                    rows_matmul(pe, sums[s], o[s], W.wo[:], stop=True).then_inc(out_made[s], 1)
                ff.pe(pe, k - FF, s, i)

            in_turns(pe, rounds, LAG, STEPS, step)

        @block.scalar
        def _(act):
            def step(k, s, i):
                if k == COPY:
                    wait(act, turned[s], 2 * i + 1)
                    act.copy(srcT[s][:], wide[s][:]).then_inc(copied[s], 1)
                    wait(act, turned[s], 2 * i + 2)
                    act.copy(ownT[s][:], sums[s][:]).then_inc(copied[s], 1)
                if k == MOVE:
                    wait(act, q_made[s], i + 1)
                    act.activation(q[s][:], sums[s][:], ACT.Identity, bias=BQc).then_inc(q_moved[s], 1)
                if k == LOGITS:
                    wait(act, v_made[s], i + 1)
                    act.activation(v[s][:], sums[s][:], ACT.Identity, bias=BVc).then_inc(v_moved[s], 1)
                if k == EXP:
                    wait(act, differed[s], 3 * i + 2)
                    act.activation(prob[s][:], prob[s][:], ACT.Exp).then_inc(exped[s], 1)
                    wait(act, differed[s], 3 * i + 3)
                    act.activation(fade[s][:], fade[s][:], ACT.Exp).then_inc(exped[s], 1)
                if k == WIDEN:
                    wait(act, inverted[s], 2 * i + 2)
                    act.copy(wide_inv[s][:].rearrange("p (h d) -> p h d", d=P // HEADS), over(inv[s][:], P // HEADS)).then_inc(widened[s], 1)
                if k == SQUARE:
                    wait(act, residual[s], i + 1)
                    norm.square(act, i, s, 0, tiles(y[s][:]))
                ff.act(act, k - FF, s, i)

            in_turns(act, rounds, LAG, STEPS, step)

        @block.vector
        def _(dve):
            norm.set_eps(dve, began)
            dve.memset(m[S - 1][:], 0.0).then_inc(began, 1)
            dve.memset(den[S - 1][:], 0.0).then_inc(began, 1)
            dve.memset(acc[S - 1][:], 0.0).then_inc(began, 1)
            dve.wait_ge(began, S + 3)
            end = slice(GROUP - 1, GROUP)

            def step(k, s, i):
                g = i * S + s
                before = i + 1 if s else i
                if k == TURN:
                    wait(dve, loaded[s], 16 * i + 16)
                    dve.tensor_scalar(hot[s][:], typ[s][:], W.split[:, 0:1], None, ALU.is_equal).then_inc(hot_made[s], 1)
                if k == MATCH:
                    wait(dve, q_moved[s], i + 1)
                    wait(dve, k_made[s], i + 1)
                    dve.scalar_tensor_tensor(qk[s][:], wide[s][:], BKc, q[s][:], ALU.add, ALU.mult).then_inc(matched[s], 1)
                if k == PEAK:
                    wait(dve, logits[s], i + 1)
                    wait(dve, peaked[s - 1], 2 * before)
                    dve.tensor_copy(m[s][:, 0:1], m[s - 1][:, GROUP:]).then_inc(peaked[s], 1)
                    dve.tensor_tensor_scan(m[s][:, 1:], pos(Ed.low, g), wide[s][:], m[s - 1][:, GROUP:], ALU.add, ALU.max).then_inc(peaked[s], 1)
                if k == DIFFER:
                    wait(dve, peaked[s], 2 * i + 2)
                    dve.tensor_tensor(fade[s][:], m[s][:, 0:GROUP], pos(Ed.low, g), ALU.add).then_inc(differed[s], 1)
                    dve.tensor_tensor(prob[s][:], wide[s][:], m[s][:, 1:], ALU.subtract).then_inc(differed[s], 1)
                if k == FADE:
                    wait(dve, differed[s], 3 * i + 1)
                    dve.tensor_tensor(fade[s][:], fade[s][:], m[s][:, 1:], ALU.subtract).then_inc(differed[s], 1)
                if k == ACCUMULATE:
                    wait(dve, exped[s], 2 * i + 1)
                    wait(dve, stored[s], 16 * i)
                    wait(dve, v_moved[s], i + 1)
                    dve.tensor_tensor(pv[s][:], v[s][:], prob[s][:], ALU.mult).then_inc(valued[s], 1)
                    wait(dve, exped[s], 2 * i + 2)
                    wait(dve, scanned[s - 1], 2 * before)
                    dve.tensor_tensor_scan(den[s][:], fade[s][:], prob[s][:], den[s - 1][:, end], ALU.mult, ALU.add).then_inc(scanned[s], 1)
                if k == VALUES:
                    wait(dve, valued[s], i + 1)
                    dve.tensor_tensor_scan(acc[s][:], fade[s][:], pv[s][:], acc[s - 1][:, end], ALU.mult, ALU.add).then_inc(scanned[s], 1)
                if k == INVERT:
                    wait(dve, den_turned[s], i + 1)
                    dve.tensor_scalar(inv[s][:], wide[s][:, 0:TPG * HEADS], 1e-16, None, ALU.add).then_inc(inverted[s], 1)
                    wait(dve, inverted[s], 2 * i + 1)
                    dve.reciprocal(inv[s][:], inv[s][:]).then_inc(inverted[s], 1)
                if k == DIVIDE:
                    wait(dve, scanned[s], 2 * i + 2)
                    wait(dve, spread[s], i + 1)
                    dve.tensor_tensor(o[s][:], acc[s][:], wide[s][:], ALU.mult).then_inc(divided[s], 1)
                if k == RESIDUAL:
                    wait(dve, ff.added[s], i + 1)
                    wait(dve, out_made[s], i + 1)
                    dve.tensor_tensor(y[s][:], sums[s][:], x2b[s][:], ALU.add).then_inc(residual[s], 1)
                if k == SUM:
                    norm.sums(dve, i, s, 0)
                if k == SCALE:
                    wait(dve, residual[s], i + 1)
                    norm.scale(dve, i, s, 0, ff.n[s][:], y[s][:])
                ff.dve(dve, k - FF, s, i)

            in_turns(dve, rounds, LAG, STEPS, step)


def message_edges(nc, A, D, W, Ed, plan):
    S, rounds = plan.ES, plan.EG // plan.ES
    mem = Mem(nc)
    rows = lambda n: [mem.sb(f"m_{n}{s}", [P, GROUP]) for s in range(S)]
    src, own, srcT, ownT, mx, h, y, x4 = (rows(n) for n in ("src", "own", "srcT", "ownT", "mx", "h", "y", "x4"))
    wrow = [mem.sb(f"m_wrow{s}", [1, GROUP]) for s in range(S)]
    oslot = [mem.sb(f"m_oslot{s}", [P, TPG], I32) for s in range(S)]
    bank = [[mem.ps(f"m_b{s}{k}") for k in range(4)] for s in range(S)]
    norm = Norm(mem, "mn", S, 1, by_scalar=True)
    gsrc = Gather(mem, "mg", S, Ed.src, D["x3"], src)
    turned, copied, made, scanned, hidden, relued, out_made, residual, loaded, oslotted, stored = (
        mem.sems("m_" + n, S) for n in ("turned", "copied", "made", "scanned", "hidden", "relued", "out_made",
                                        "residual", "loaded", "oslotted", "stored"))
    began = mem.sem("m_began")
    tin = groups_of(D["x3"])
    TURN, COPY, SOURCE, OWN, HIDDEN, RELU, PRODUCT, RESIDUAL, SQUARE, SUM, SCALE, SCATTER = range(12)
    STEPS = SCATTER + TPG
    AHEAD = range(COPY, COPY + 2 * TPG, 2)
    LAG = (0, 7)

    with nc.Block() as block:
        @block.sync
        def _(sp):
            def load(s, i):
                sp.dma_start(own[s][:], tin[i * S + s + plan.DG]).then_inc(loaded[s], 16)
                sp.dma_start(wrow[s][:], A["w_row"][bass.ds(i * S + s, 1), :]).then_inc(loaded[s], 16)

            for s in range(S):
                load(s, 0)

            def step(k, s, i):
                if k == SQUARE and another(i, rounds):
                    wait(sp, residual[s], i + 1)
                    wait(sp, made[s], i + 1)
                    load(s, i + 1)

            in_turns(sp, rounds, LAG, STEPS, step, tail=1)

        @block.gpsimd
        def _(pool):
            for s in range(S):
                gsrc.fetch(pool, 0, s, s)

            def step(k, s, i):
                if k in AHEAD and another(i, rounds):
                    if k == AHEAD[0]:
                        wait(pool, turned[s], 2 * i + 1)
                        gsrc.begin(pool, i + 1, s, (i + 1) * S + s)
                    gsrc.tile(pool, s, AHEAD.index(k))
                if k == SCATTER:
                    wait(pool, stored[s], i * 16 * TPG)
                    pool.tensor_copy(oslot[s][:], Ed.out[:, bass.ds((i * S + s) * TPG, TPG)]).then_inc(oslotted[s], 1)
                    wait(pool, oslotted[s], i + 1)
                    wait(pool, norm.normed[s], i + 1)
                    mem.settle(pool)
                if k >= SCATTER:
                    t = k - SCATTER
                    pool.indirect_dma_start(
                        out=D["out"], out_offset=bass.IndirectOffsetOnAxis(ap=oslot[s][:, t:t + 1], axis=0),
                        in_=x4[s][:, t * P:(t + 1) * P], in_offset=None, bounds_check=plan.N - 1, oob_is_err=False,
                    ).then_inc(stored[s], 16)

            in_turns(pool, rounds, LAG, STEPS, step, tail=1)
            for s in range(S):
                pool.wait_ge(stored[s], rounds * 16 * TPG)

        @block.tensor
        def _(pe):
            def step(k, s, i):
                if k == TURN:
                    gsrc.arrived(pe, i, s)
                    wait(pe, residual[s], i)
                    transpose_tiles(pe, bank[s][0], src[s], W.ident).then_inc(turned[s], 1)
                    wait(pe, loaded[s], 32 * i + 32)
                    transpose_tiles(pe, bank[s][1], own[s], W.ident).then_inc(turned[s], 1)
                if k == SOURCE:
                    wait(pe, copied[s], 2 * i + 1)
                    pe.matmul(bank[s][0][:], W.msg_src[:], srcT[s][:], start=True, stop=False)
                    pe.matmul(bank[s][0][:], W.msg_w[:], wrow[s][:], start=False, stop=True).then_inc(made[s], 1)
                if k == OWN:
                    wait(pe, copied[s], 2 * i + 2)
                    pe.matmul(bank[s][2][:], W.w1a_edge[:], ownT[s][:], start=True, stop=False)
                    const_rows(pe, bank[s][3], W, C_MSG)
                if k == HIDDEN:
                    wait(pe, scanned[s], i + 1)
                    pe.matmul(bank[s][2][:], W.w1b[:], mx[s][:], start=False, stop=True).then_inc(hidden[s], 1)
                if k == PRODUCT:
                    wait(pe, relued[s], i + 1)
                    rows_matmul(pe, bank[s][3], h[s], W.w2_msg[:], stop=True).then_inc(out_made[s], 1)

            in_turns(pe, rounds, LAG, STEPS, step)

        @block.scalar
        def _(act):
            def step(k, s, i):
                if k == COPY:
                    wait(act, turned[s], 2 * i + 1)
                    act.copy(srcT[s][:], bank[s][0][:]).then_inc(copied[s], 1)
                    wait(act, turned[s], 2 * i + 2)
                    act.copy(ownT[s][:], bank[s][1][:]).then_inc(copied[s], 1)
                if k == RELU:
                    wait(act, hidden[s], i + 1)
                    act.activation(h[s][:], bank[s][2][:], ACT.Relu, bias=W.b1_msg[:, 0:1]).then_inc(relued[s], 1)
                if k == SQUARE:
                    wait(act, residual[s], i + 1)
                    norm.square(act, i, s, 0, tiles(y[s][:]))
                if k == SUM:
                    norm.root_by_scalar(act, i, s, 0)

            in_turns(act, rounds, LAG, STEPS, step)

        @block.vector
        def _(dve):
            norm.set_eps(dve, began)
            dve.memset(mx[S - 1][:], 0.0).then_inc(began, 1)
            dve.wait_ge(began, S + 1)

            def step(k, s, i):
                if k == OWN:
                    wait(dve, made[s], i + 1)
                    wait(dve, scanned[s - 1], i + 1 if s else i)
                    dve.tensor_tensor_scan(mx[s][:], pos(Ed.low, i * S + s), bank[s][0][:], mx[s - 1][:, GROUP - 1:],
                                           ALU.add, ALU.max).then_inc(scanned[s], 1)
                if k == RESIDUAL:
                    wait(dve, loaded[s], 32 * i + 32)
                    wait(dve, out_made[s], i + 1)
                    dve.tensor_tensor(y[s][:], bank[s][3][:], own[s][:], ALU.add).then_inc(residual[s], 1)
                if k == SUM:
                    norm.sums(dve, i, s, 0)
                if k == SCALE:
                    wait(dve, residual[s], i + 1)
                    wait(dve, stored[s], i * 16 * TPG)
                    norm.scale(dve, i, s, 0, x4[s][:], y[s][:])

            in_turns(dve, rounds, LAG, STEPS, step)


def build(nc, A, out, nodes, edges):
    plan = Plan(nodes, edges)
    EG, AG, R = plan.EG, plan.AG, plan.R
    D = {"out": out}
    for k in (1, 2, 3):
        behind = (plan.AG if k == 3 else EG) * GROUP
        D[f"x{k}"] = nc.dram_tensor(f"table_x{k}", (R + behind, P), F32, kind="Internal").ap()
    for n, shape, dt in (
        ("node_row", (P * plan.C, 2), F32), ("keep", (AG, GROUP), BF16), ("low", (AG, GROUP), BF16),
        ("count", (AG, GROUP), F32), ("wsum", (AG, GROUP), F32), ("rcount", (AG, GROUP), F32),
    ) + tuple((f"top_val{n}", (r * TOP, 1), F32) for n, r in enumerate((P, 32, 4, 1))) + tuple(
        (f"top_id{n}", (r * TOP, 1), I32) for n, r in enumerate((P, 32, 4, 1))
    ):
        D[n] = nc.dram_tensor("scratch_" + n, shape, dt, kind="Internal").ap()
    W = Weights(nc)
    with nc.cleanup_on_exit():
        fold_weights(nc, A, W)
    Ed = EdgeData(nc, plan)
    with nc.cleanup_on_exit():
        scan_rows(nc, A, D, W, plan)
    with nc.cleanup_on_exit():
        mem = Mem(nc)
        score, weight = mem.sb("score", [P, max(plan.C, TOP)]), mem.sb("gru_weight", [P, P])
        Own = OwnRows(nc, plan)
        with nc.cleanup_on_exit():
            edge_tables(nc, A, D, W, Ed, Own, plan)
        with nc.cleanup_on_exit():
            scores(nc, A, D, W, Ed, Own, plan, score)
        with nc.cleanup_on_exit():
            top_nodes(nc, A, D, W, Ed, Own, plan, score, weight)
    with nc.cleanup_on_exit():
        dense_pass(nc, A, D, W, Ed, plan)
    Ed.add_low(nc, plan)
    with nc.cleanup_on_exit():
        Ed.add_keep(nc, plan)
        for layer in (gcn_edges, pna_edges):
            with nc.cleanup_on_exit():
                layer(nc, A, D, W, Ed, plan)
    for layer in (attention_edges, message_edges):
        with nc.cleanup_on_exit():
            layer(nc, A, D, W, Ed, plan)


def laid_out(inputs):
    import numpy as np

    a = {k: np.asarray(v) for k, v in inputs.items()}
    nodes, edges = a["x"].shape[0], a["src"].shape[0]
    plan = Plan(nodes, edges)

    def by_row(v, fill, shift=0):
        flat = np.full(plan.EP + 2, fill, v.dtype)
        flat[1:edges + 1] = v
        if shift < 0:
            flat[0] = -1
        return np.ascontiguousarray(flat[1 + shift:1 + shift + plan.EP].reshape(plan.AG, GROUP))

    def by_tile(v):
        return np.ascontiguousarray(v.reshape(plan.AG, P, TPG).transpose(1, 0, 2).reshape(P, plan.ET))

    col = lambda n: a[n].reshape(P, 1)
    row = lambda n: a[n].reshape(1, -1)
    T = np.ascontiguousarray
    out = {
        "x": a["x"],
        "dst_row": by_row(a["dst"], nodes), "prev_row": by_row(a["dst"], nodes, -1), "w_row": by_row(a["edge_weight"], 0),
        "type_row": by_row(a["edge_type_8"], 0),
        "dst_tok": by_tile(by_row(a["dst"], nodes)), "next_tok": by_tile(by_row(a["dst"], nodes, 1)),
        "dst0_tok": by_tile(by_row(a["dst"], 0)), "src_tok": by_tile(by_row(a["src"], 0)),
        "w_tok": by_tile(by_row(a["edge_weight"], 0)),
        "L0_p": row("L0_gnn_p"), "L0_w_ihT": T(a["L0_gnn_w_ih"].T), "L0_w_hhT": T(a["L0_gnn_w_hh"].T),
        "L0_b_ih": row("L0_gnn_b_ih"), "L0_b_hh": row("L0_gnn_b_hh"), "L0_W0": a["L0_gnn_W0"], "L0_W0T": T(a["L0_gnn_W0"].T),
        "L1_W_post": a["L1_gnn_W_post"], "L1_W_linT": T(a["L1_gnn_W_lin"].T),
        "L1_W_pre_dst": T(a["L1_gnn_W_pre"][:, :P]), "L1_W_pre_srcT": T(a["L1_gnn_W_pre"][:, P:].T),
        "L2_Wq": a["L2_gnn_Wq"], "L2_Wk": a["L2_gnn_Wk"], "L2_Wv": a["L2_gnn_Wv"], "L2_Wo": a["L2_gnn_Wo"],
        "L2_W1": a["L2_gnn_W1"], "L2_W2": a["L2_gnn_W2"], "L2_edge_bias": a["L2_gnn_edge_bias"],
        "L2_g2": row("L2_gnn_g2"), "L2_be2": row("L2_gnn_be2"), "L2_bo": row("L2_gnn_bo"),
        "L3_Ws": T(a["L3_gnn_Wm"][P:2 * P]), "L3_WdT": T(a["L3_gnn_Wm"][:P].T), "L3_ww": T(a["L3_gnn_Wm"][2 * P:]),
        "L3_W1": a["L3_gnn_W1"], "L3_W2": a["L3_gnn_W2"],
        "split": np.stack([np.arange(3 * TYPES) % TYPES] + [np.arange(3 * TYPES) // TYPES == k for k in range(3)], axis=1)
        .astype(np.float32),
        "columns": np.concatenate([col(n) for n in (
            "L2_gnn_g1", "L2_gnn_be1", "L2_gnn_b1", "L2_gnn_bq", "L2_gnn_bk", "L2_gnn_bv", "L3_gnn_b1", "L3_gnn_bm",
            "L1_gnn_b_post", "L1_gnn_b_pre")], axis=1),
        "rows": np.concatenate([row(n) for n in (
            "L2_gnn_be1", "L2_gnn_b2", "L3_gnn_b2", "L1_gnn_b_lin", "L2_gnn_bo")], axis=0),
    }
    return out, nodes, edges


def kernel(**inputs):
    import numpy as np
    import concourse.bacc as bacc
    from concourse.bass_utils import run_bass_kernel_spmd

    arrays, nodes, edges = laid_out(inputs)
    nc = bacc.Bacc("TRN2", target_bir_lowering=False, num_devices=1)
    A, fed = {}, {}
    for name, v in arrays.items():
        fed["in_" + name] = v
        A[name] = nc.dram_tensor("in_" + name, v.shape, mybir.dt.from_np(v.dtype), kind="ExternalInput").ap()
    out = nc.dram_tensor("out_rows", (nodes, P), F32, kind="ExternalOutput").ap()
    build(nc, A, out, nodes, edges)
    r = run_bass_kernel_spmd(nc, [fed], core_ids=[0])
    return r.results[0]["out_rows"]
```
